# Optimizing a Trainium2 kernel written in Bass

```python
import numpy as np
import jax
import jax.numpy as jnp

def _softmax(x, axis=-1):
    return jax.nn.softmax(x, axis=axis)

def _gelu(x):
    return jax.nn.gelu(x, approximate=True)

def _silu(x):
    return jax.nn.silu(x)

def _sigmoid(x):
    return jax.nn.sigmoid(x)

def _layernorm(x, axis=-1, eps=1e-05):
    m = jnp.mean(x, axis=axis, keepdims=True)
    v = jnp.var(x, axis=axis, keepdims=True)
    return (x - m) / jnp.sqrt(v + eps)

def _scatter_add(tgt, idx, src, axis=0):
    return tgt.at[idx].add(src)

def _segment_sum(src, seg, n):
    return jax.ops.segment_sum(src, seg, n)
kernel_name = 'mk_xattn_ffn_d2_seqx_r2_54a787'

def setup_inputs(seed: int=0):
    np.random.seed(seed)
    _w = jnp.asarray

    def _rec_inputs():
        import jax
        import jax.numpy as jnp
        _rk = jax.random.key(seed)
        x = -0.0003929 + 0.9999 * jax.random.normal(jax.random.fold_in(_rk, 1), (2, 2048, 512), jnp.float32)
        _lenS = 2048 - jax.random.randint(jax.random.fold_in(_rk, 7), (2,), 0, max(1, 2048 // 4) + 1, jnp.int32)
        _lenS2 = 128 - jax.random.randint(jax.random.fold_in(_rk, 8), (2,), 0, max(1, 128 // 4) + 1, jnp.int32)
        _ctx_1024P = jax.random.normal(jax.random.fold_in(_rk, 11), (2, 16, 512), jnp.float32)
        _ctx_1024c = jax.random.dirichlet(jax.random.fold_in(_rk, 511), 0.3 * jnp.ones((16,), jnp.float32), (2, 128))
        _ctx_1024t = jnp.einsum('bsk,bkd->bsd', _ctx_1024c, _ctx_1024P)
        _ctx_1024t = _ctx_1024t * jax.lax.rsqrt(jnp.mean(jnp.square(_ctx_1024t)) + 1e-12) * 0.953939
        ctx_1024 = -0.000514642 + 1.00011 * (_ctx_1024t + 0.3 * jax.random.normal(jax.random.fold_in(_rk, 611), (2, 128, 512), jnp.float32))
        itok_BxS_0_511 = jax.random.randint(jax.random.fold_in(_rk, 12), (2, 2048), 0, 256, jnp.int32)
        return (x, ctx_1024, itok_BxS_0_511)
    x, ctx_1024, itok_BxS_0_511 = _rec_inputs()

    def _L0_xattn_setup():
        import jax, jax.numpy as jnp
        import numpy as np
        Q_DIM = 512
        KV_DIM = 512
        D_ATTN = 512
        N_HEADS = 16
        HDIM = D_ATTN // N_HEADS
        LOOKBACK = 3
        KW = LOOKBACK + 1
        SCALE = HDIM ** (-0.5)
        B, LQ, LKV = (4, 2048, 256)

        def _split_heads(x):
            b, l, _ = x.shape
            return x.reshape(b, l, N_HEADS, HDIM).transpose(0, 2, 1, 3)
        key = jax.random.key(seed)
        ks = jax.random.split(key, 6)
        q = jax.random.normal(ks[0], (B, LQ, Q_DIM), dtype=jnp.float32)
        kv_src = jax.random.normal(ks[1], (B, LKV, KV_DIM), dtype=jnp.float32)
        seg_id = jnp.sort(jax.random.randint(ks[2], (B, LQ), 0, LKV), axis=-1)
        Wq = jax.random.normal(ks[3], (D_ATTN, Q_DIM), dtype=jnp.float32) * Q_DIM ** (-0.5)
        Wkv = jax.random.normal(ks[4], (2 * D_ATTN, KV_DIM), dtype=jnp.float32) * KV_DIM ** (-0.5)
        Wo = jax.random.normal(ks[5], (Q_DIM, D_ATTN), dtype=jnp.float32) * D_ATTN ** (-0.5)
        return {'q': q, 'kv_src': kv_src, 'seg_id': seg_id, 'Wq': Wq, 'Wkv': Wkv, 'Wo': Wo}
    _L0_xattn_all = _L0_xattn_setup()
    _L0_xattn_in = {k: v for k, v in _L0_xattn_all.items() if k in ('Wq', 'Wkv', 'Wo')}
    del _L0_xattn_all

    def _L0_ffn_setup():
        import jax, jax.numpy as jnp
        import numpy as np
        INT8_MAX = 127.0

        def _absmax_scale(x, axes):
            amax = jnp.max(jnp.abs(x), axis=axes, keepdims=True)
            return jnp.maximum(amax, 1e-12) / INT8_MAX
        key = jax.random.key(seed)
        k1, k2 = jax.random.split(key)
        lhs = jax.random.normal(k1, (4, 4096, 512), dtype=jnp.float32)
        rhs = jax.random.normal(k2, (512, 512), dtype=jnp.float32)
        return {'lhs': lhs, 'rhs': rhs}
    _L0_ffn_all = _L0_ffn_setup()
    _L0_ffn_in = {k: v for k, v in _L0_ffn_all.items() if k in ('rhs',)}
    del _L0_ffn_all

    def _L1_xattn_setup():
        import jax, jax.numpy as jnp
        import numpy as np
        EMBED_DIM = 512
        NUM_HEADS = 16
        HEAD_DIM = EMBED_DIM // NUM_HEADS
        B, T, S = (2, 1024, 1024)
        key = jax.random.key(seed)
        ks = jax.random.split(key, 5)
        scale_w = 1.0 / np.sqrt(EMBED_DIM)
        return {'q': jax.random.normal(ks[0], (B, T, EMBED_DIM), dtype=jnp.float32), 'k': jax.random.normal(ks[1], (B, S, EMBED_DIM), dtype=jnp.float32), 'v': jax.random.normal(ks[2], (B, S, EMBED_DIM), dtype=jnp.float32), 'in_proj_weight': jax.random.normal(ks[3], (3 * EMBED_DIM, EMBED_DIM), dtype=jnp.float32) * scale_w, 'in_proj_bias': jnp.zeros((3 * EMBED_DIM,), dtype=jnp.float32), 'out_w': jax.random.normal(ks[4], (EMBED_DIM, EMBED_DIM), dtype=jnp.float32) * scale_w, 'out_b': jnp.zeros((EMBED_DIM,), dtype=jnp.float32)}
    _L1_xattn_all = _L1_xattn_setup()
    _L1_xattn_in = {k: v for k, v in _L1_xattn_all.items() if k in ('in_proj_weight', 'in_proj_bias', 'out_w', 'out_b')}
    del _L1_xattn_all

    def _L1_ffn_setup():
        import jax, jax.numpy as jnp
        import numpy as np
        D_MODEL = 512
        EXPERT_DIM = 2048
        N_EXPERTS = 8
        CAP_FACTOR = 0.5
        key = jax.random.key(seed)
        ks = jax.random.split(key, 7)
        inp = {'input': jax.random.normal(ks[0], (4, 2048, D_MODEL), dtype=jnp.float32), 'w_switch': jax.random.normal(ks[1], (D_MODEL, N_EXPERTS), dtype=jnp.float32) * 0.02, 'b_switch': jnp.zeros((N_EXPERTS,), jnp.float32), 'w1': jax.random.normal(ks[2], (N_EXPERTS, D_MODEL, EXPERT_DIM), dtype=jnp.float32) * 0.02, 'b1': jnp.zeros((N_EXPERTS, EXPERT_DIM), jnp.float32), 'w2': jax.random.normal(ks[3], (N_EXPERTS, EXPERT_DIM, D_MODEL), dtype=jnp.float32) * 0.02, 'b2': jnp.zeros((N_EXPERTS, D_MODEL), jnp.float32)}
        return inp
    _L1_ffn_all = _L1_ffn_setup()
    _L1_ffn_in = {k: v for k, v in _L1_ffn_all.items() if k in ('w_switch', 'b_switch', 'w1', 'b1', 'w2', 'b2')}
    del _L1_ffn_all
    return {'x': x, 'ctx_1024': ctx_1024, 'itok_BxS_0_511': itok_BxS_0_511, 'L0_xattn_Wq': _L0_xattn_in['Wq'], 'L0_xattn_Wkv': _L0_xattn_in['Wkv'], 'L0_xattn_Wo': _L0_xattn_in['Wo'], 'L0_ffn_rhs': _L0_ffn_in['rhs'], 'L1_xattn_in_proj_weight': _L1_xattn_in['in_proj_weight'], 'L1_xattn_in_proj_bias': _L1_xattn_in['in_proj_bias'], 'L1_xattn_out_w': _L1_xattn_in['out_w'], 'L1_xattn_out_b': _L1_xattn_in['out_b'], 'L1_ffn_w_switch': _L1_ffn_in['w_switch'], 'L1_ffn_b_switch': _L1_ffn_in['b_switch'], 'L1_ffn_w1': _L1_ffn_in['w1'], 'L1_ffn_b1': _L1_ffn_in['b1'], 'L1_ffn_w2': _L1_ffn_in['w2'], 'L1_ffn_b2': _L1_ffn_in['b2']}

def reference(x, ctx_1024, itok_BxS_0_511, L0_xattn_Wq, L0_xattn_Wkv, L0_xattn_Wo, L0_ffn_rhs, L1_xattn_in_proj_weight, L1_xattn_in_proj_bias, L1_xattn_out_w, L1_xattn_out_b, L1_ffn_w_switch, L1_ffn_b_switch, L1_ffn_w1, L1_ffn_b1, L1_ffn_w2, L1_ffn_b2):
    import jax
    import jax.numpy as jnp

    def _L0_xattn_ref(q, kv_src, seg_id, Wq, Wkv, Wo):
        import jax, jax.numpy as jnp
        import numpy as np
        Q_DIM = 512
        KV_DIM = 512
        D_ATTN = 512
        N_HEADS = 16
        HDIM = D_ATTN // N_HEADS
        LOOKBACK = 3
        KW = LOOKBACK + 1
        SCALE = HDIM ** (-0.5)
        B, LQ, LKV = (4, 2048, 256)

        def _split_heads(x):
            b, l, _ = x.shape
            return x.reshape(b, l, N_HEADS, HDIM).transpose(0, 2, 1, 3)
        b, lq, _ = q.shape
        lkv = kv_src.shape[1]
        qh = _split_heads(q @ Wq.T)
        kv = kv_src @ Wkv.T
        k, v = jnp.split(kv, 2, axis=-1)
        kh = _split_heads(k)
        vh = _split_heads(v)
        offsets = jnp.arange(KW)
        gather = seg_id[:, :, None] - offsets
        neg_mask = gather < 0
        gc = jnp.clip(gather, 0, lkv - 1)
        b_idx = jnp.arange(b)[:, None, None]
        k_sel = kh[b_idx, :, gc].transpose(0, 3, 1, 2, 4)
        v_sel = vh[b_idx, :, gc].transpose(0, 3, 1, 2, 4)
        scores = jnp.einsum('bhqd,bhqkd->bhqk', qh, k_sel) * SCALE
        neg_inf = jnp.finfo(scores.dtype).min
        scores = jnp.where(neg_mask[:, None, :, :], neg_inf, scores)
        probs = jax.nn.softmax(scores, axis=-1)
        out = jnp.einsum('bhqk,bhqkd->bhqd', probs, v_sel)
        out = out.transpose(0, 2, 1, 3).reshape(b, lq, D_ATTN)
        return out @ Wo.T

    def _L0_ffn_ref(lhs, rhs):
        import jax, jax.numpy as jnp
        import numpy as np
        INT8_MAX = 127.0

        def _absmax_scale(x, axes):
            amax = jnp.max(jnp.abs(x), axis=axes, keepdims=True)
            return jnp.maximum(amax, 1e-12) / INT8_MAX
        lhs_scale = _absmax_scale(lhs, (2,))
        rhs_scale = _absmax_scale(rhs, (0,))
        q_lhs = jnp.clip(jnp.round(lhs / lhs_scale), -INT8_MAX, INT8_MAX).astype(jnp.int8)
        q_rhs = jnp.clip(jnp.round(rhs / rhs_scale), -INT8_MAX, INT8_MAX).astype(jnp.int8)
        acc = jax.lax.dot_general(q_lhs, q_rhs, (((2,), (0,)), ((), ())), preferred_element_type=jnp.int32)
        return acc.astype(jnp.float32) * lhs_scale * rhs_scale

    def _L1_xattn_ref(q, k, v, in_proj_weight, in_proj_bias, out_w, out_b):
        import jax, jax.numpy as jnp
        import numpy as np
        EMBED_DIM = 512
        NUM_HEADS = 16
        HEAD_DIM = EMBED_DIM // NUM_HEADS
        B, T, S = (2, 1024, 1024)
        H, D = (NUM_HEADS, HEAD_DIM)
        w_q, w_k, w_v = jnp.split(in_proj_weight, 3, axis=0)
        b_q, b_k, b_v = jnp.split(in_proj_bias, 3, axis=0)
        qp = q @ w_q.T + b_q
        kp = k @ w_k.T + b_k
        vp = v @ w_v.T + b_v
        bsz, t, _ = qp.shape
        s = kp.shape[1]
        qh = qp.reshape(bsz, t, H, D).transpose(0, 2, 1, 3)
        kh = kp.reshape(bsz, s, H, D).transpose(0, 2, 1, 3)
        vh = vp.reshape(bsz, s, H, D).transpose(0, 2, 1, 3)
        scale = D ** (-0.5)
        attn = jnp.einsum('bhtd,bhsd->bhts', qh, kh) * scale
        attn = jax.nn.softmax(attn, axis=-1)
        ctx = jnp.einsum('bhts,bhsd->bhtd', attn, vh)
        ctx = ctx.transpose(0, 2, 1, 3).reshape(bsz, t, H * D)
        out = ctx @ out_w.T + out_b
        return out

    def _L1_ffn_ref(input, w_switch, b_switch, w1, b1, w2, b2):
        import jax, jax.numpy as jnp
        import numpy as np
        D_MODEL = 512
        EXPERT_DIM = 2048
        N_EXPERTS = 8
        CAP_FACTOR = 0.5
        B, S, D = input.shape
        T = B * S
        E = b_switch.shape[0]
        capacity = int(CAP_FACTOR * T / E)
        x = input.reshape(T, D)
        logits = x @ w_switch + b_switch
        probs = jax.nn.softmax(logits, axis=-1)
        pmax = probs.max(axis=-1)
        routes = probs.argmax(axis=-1)
        oh = (routes[:, None] == jnp.arange(E)[None, :]).astype(jnp.int32)
        pos = (jnp.cumsum(oh, axis=0) * oh).sum(-1) - 1
        keep = pos < capacity
        slot = jnp.where(keep, routes * capacity + pos, E * capacity)
        buf = jnp.zeros((E * capacity + 1, D), x.dtype).at[slot].set(x)
        buf_e = buf[:E * capacity].reshape(E, capacity, D)
        h = jax.nn.relu(jnp.einsum('ecd,edh->ech', buf_e, w1) + b1[:, None, :])
        y = jnp.einsum('ech,ehd->ecd', h, w2) + b2[:, None, :]
        y_flat = jnp.concatenate([y.reshape(E * capacity, D), jnp.zeros((1, D), x.dtype)], axis=0)
        out = jnp.where(keep[:, None], y_flat[slot], x)
        scale = pmax / jax.lax.stop_gradient(pmax)
        out = out * scale[:, None]
        return out.reshape(B, S, D)
    x = x + _L0_xattn_ref(_layernorm(x, axis=-1), ctx_1024, itok_BxS_0_511, L0_xattn_Wq, L0_xattn_Wkv, L0_xattn_Wo)
    x = x + _L0_ffn_ref(_layernorm(x, axis=-1), L0_ffn_rhs)
    x = x + _L1_xattn_ref(_layernorm(x, axis=-1), ctx_1024, ctx_1024, L1_xattn_in_proj_weight, L1_xattn_in_proj_bias, L1_xattn_out_w, L1_xattn_out_b)
    x = x + _L1_ffn_ref(_layernorm(x, axis=-1), L1_ffn_w_switch, L1_ffn_b_switch, L1_ffn_w1, L1_ffn_b1, L1_ffn_w2, L1_ffn_b2)
    return x

_drawn_inputs = setup_inputs


def setup_inputs(seed=0):
    import zlib

    import numpy as np

    out = dict(_drawn_inputs(seed))
    spreads = {'L1_xattn_in_proj_bias': (0.0, 0.8),
     'L1_xattn_out_b': (0.0, 0.8),
     'L1_ffn_b_switch': (0.0, 0.468),
     'L1_ffn_b1': (0.0, 0.8),
     'L1_ffn_b2': (0.0, 2.0)}
    factors = {'L1_ffn_w_switch': 3.096, 'L1_ffn_w1': 7.821, 'L1_ffn_w2': 6.335}
    for name, (base, spread) in spreads.items():
        noise = np.random.default_rng([zlib.crc32(name.encode()), seed]).standard_normal(out[name].shape)
        drawn = base * np.exp(spread * noise) if base else spread * noise
        out[name] = jnp.asarray(drawn.astype(out[name].dtype))
    for name, factor in factors.items():
        out[name] = (out[name] * factor).astype(out[name].dtype)
    return out
```

```python
import numpy as np
import concourse.bass as bass
from concourse import mybir
from contextlib import ExitStack

P = 128
B, S, D = 2, 2048, 512
T = B * S
KEYS = 128
H, HD = 16, 32
KC = D // P
HPC = H // KC
SUP = 512
NSUB = SUP // P
NSUP = T // SUP
NSUP_B = NSUP // B
NT = T // P
E, F = 8, 2048
CAP = T // 2 // E
RT = CAP // P
NU, UF = 4, F // 4
UC = UF // P
LOOKBACK = 3
ROW = D + 4
EPS = 1e-5
SCALE = HD ** -0.5
HIDE = -1e30
MAGIC = 1.5 * 2.0 ** 23
NOWHERE = 1 << 20


def log_counts():
    parts = []
    for c in range(1, LOOKBACK + 2):
        v = np.float64(np.log(c) / SCALE)
        e = 2.0 ** (11 - np.floor(np.log2(v))) if v else 1.0
        hi = np.round(v * e) / e
        lo = v - hi
        e = 2.0 ** (11 - np.floor(np.log2(abs(lo)))) if lo else 1.0
        parts.append((float(hi), float(np.round(lo * e) / e)))
    return parts


def build(nc, x, ctxT, segT, seg, wq0, wkv0, wo0, rhs, wqkv1, bq1, bk1, bv1, wo1, bo1,
          wsw, bsw, w1, b1, w2, b2, out):
    fp32, bf16, f32r = mybir.dt.float32, mybir.dt.bfloat16, mybir.dt.float32r
    i32, u32 = mybir.dt.int32, mybir.dt.uint32
    ALU, ACT, AX = mybir.AluOpType, mybir.ActivationFunctionType, mybir.AxisListType

    x2_dram = nc.dram_tensor("x2_scratch", [T, D], fp32, kind="Internal").ap()
    slots_dram = nc.dram_tensor("slots_scratch", [E * CAP, ROW], fp32, kind="Internal").ap()
    x_tiles = x.rearrange("(n p) d -> n p d", p=P)
    x2_tiles = x2_dram.rearrange("(n p) d -> n p d", p=P)
    out_tiles = out.rearrange("(n p) d -> n p d", p=P)
    slot_tiles = slots_dram.rearrange("(n p) d -> n p d", p=P)

    ctx = ExitStack()
    with ctx:
        attn = ExitStack()
        ctx.enter_context(attn)

        def keep(name, shape, dt):
            return ctx.enter_context(nc.sbuf_tensor(name, shape, dt))

        def sb(name, shape, dt):
            return attn.enter_context(nc.sbuf_tensor(name, shape, dt))

        def sem(name):
            return ctx.enter_context(nc.semaphore(name))

        ident = keep("ident", [P, P], fp32)
        eps_half = keep("eps_half", [P, 8], fp32)
        moments = keep("moments", [P, NSUB, 6], fp32)
        mean_var = keep("mean_var", [P, NSUB, 2], fp32)
        var_eps = keep("var_eps", [P, NSUB], fp32)
        rstd = keep("rstd", [P, NSUB], fp32)
        b1_sb = keep("b1_sb", [P, E * NU * UC], fp32)

        identb = sb("identb", [P, P], bf16)
        wq_hi, wq_lo = sb("wq_hi", [P, KC, D], f32r), sb("wq_lo", [P, KC, D], f32r)
        wo_hi, wo_lo = sb("wo_hi", [P, KC, D], f32r), sb("wo_lo", [P, KC, D], f32r)
        kd_hi, kd_lo = sb("kd_hi", [P, B, KC, HPC * KEYS], f32r), sb("kd_lo", [P, B, KC, HPC * KEYS], f32r)
        kT1 = sb("kT1", [P, 2, 2, B * KEYS], fp32)
        v_sb = sb("v_sb", [KEYS, 2, B, D], fp32)
        select = sb("select", [H + 2, H, KEYS], f32r)
        ones = sb("ones", [P, HD], fp32)
        w_stage = sb("w_stage", [P, KC, D], fp32)
        xa = sb("xa", [P, NSUB, D], fp32)
        xb = sb("xb", [P, 2, D], fp32)
        xT_hi, xT_lo = sb("xT_hi", [P, KC, SUP], f32r), sb("xT_lo", [P, KC, SUP], f32r)
        qT_hi, qT_lo = sb("qT_hi", [P, KC, SUP], f32r), sb("qT_lo", [P, KC, SUP], f32r)
        probs = sb("probs", [KEYS, 2 * HPC, SUP], fp32)
        inv_sum = sb("inv_sum", [P, SUP], fp32)
        ctx_f = sb("ctx_f", [P, SUP], fp32)
        cT_hi, cT_lo = sb("cT_hi", [P, KC, SUP], f32r), sb("cT_lo", [P, KC, SUP], f32r)
        neg_max = sb("neg_max", [P, NSUB, H + 2], fp32)
        nmT = sb("nmT", [H + 2, SUP], f32r)
        hideT = sb("hideT", [KEYS, SUP], bf16)
        seg_row = sb("seg_row", [KEYS, SUP], i32)
        seg_f = sb("seg_f", [KEYS, SUP], fp32)
        seg_col = sb("seg_col", [P, NT], i32)
        seg_cf = sb("seg_cf", [P, NT], fp32)
        seg_t = sb("seg_t", [P, NT], fp32)
        logc = sb("logc", [P, NT, 2], fp32)
        key_num = sb("key_num", [P, 1], fp32)
        xs = sb("xs", [P, NSUB, ROW], fp32)
        xn = sb("xn", [P, NSUB, D], fp32)
        t_moments = sb("t_moments", [P, NSUB, 6], fp32)
        t_mean_var = sb("t_mean_var", [P, NSUB, 2], fp32)
        t_var_eps = sb("t_var_eps", [P, NSUB], fp32)
        t_rstd = sb("t_rstd", [P, NSUB], fp32)
        zb = sb("zb", [P, D], bf16)
        zT = sb("zT", [P, KC, P], bf16)
        rq = sb("rq", [P, KC, D], bf16)
        rscale = sb("rscale", [P, D], fp32)
        amax = sb("amax", [P, NSUB], fp32)
        lscale = sb("lscale", [P, NSUB], fp32)
        linv = sb("linv", [P, NSUB], fp32)
        minus_magic = sb("minus_magic", [P, 1], fp32)
        bq_sb, bk_sb = sb("bq_sb", [P, KC], fp32), sb("bk_sb", [P, KC], fp32)
        bo_sb = rscale
        wsw_sb = sb("wsw_sb", [P, KC, E], fp32)
        bsw_sb = sb("bsw_sb", [E, 1], fp32)
        xrT = rq[:, 0:2, :].rearrange("p a b -> p (a b)").bitcast(fp32).rearrange("p (k t) -> p k t", k=KC)
        logT = rq[0:E, 2:4, :].rearrange("p a b -> p (a b)").bitcast(fp32)
        logits = sb("logits", [P, NSUB, E], fp32)
        top8 = sb("top8", [P, NSUB, 8], fp32)
        top_at = sb("top_at", [P, NSUB, 8], u32)
        route = sb("route", [P, NSUB], fp32)
        expl = sb("expl", [P, NSUB, E], fp32)
        psum_e = sb("psum_e", [P, NSUB], fp32)
        pmax = sb("pmax", [P, NSUB], fp32)
        scale_t = sb("scale_t", [P, NSUB], fp32)
        lane8 = sb("lane8", [P, E], fp32)
        onehot = sb("onehot", [P, NSUB, E], bf16)
        upto = sb("upto", [P, P], bf16)
        onesb = sb("onesb", [P, P], bf16)
        carry = sb("carry", [P, E], fp32)
        place = sb("place", [P, NSUB, E], fp32)
        pos = sb("pos", [P, NSUB], fp32)
        full = sb("full", [P, NSUB], fp32)
        slot_f = sb("slot_f", [P, NSUB], fp32)
        slot = sb("slot", [P, NSUB], u32)
        token_num = sb("token_num", [P, NT], i32)
        wk_stage, wv_stage = probs[:, 0:4, :], probs[:, 4:8, :]
        select_f = xn[0:H + 2, :, :].rearrange("p j (h k) -> p (j h) k", k=KEYS)
        kT0 = xs[:, 1:3, 0:D].rearrange("p a (c n) -> p a c n", c=2)
        ctxT_sb = xa[:, 0:2, :].rearrange("p a (c n) -> p (a c) n", c=2)

        kT = (kT0, kT1)

        attn.close()
        moe = ExitStack()
        ctx.enter_context(moe)

        def mb(name, shape, dt):
            return moe.enter_context(nc.sbuf_tensor(name, shape, dt))

        NR = NU
        w1_raw = mb("w1_raw", [P, NR, KC, UF], fp32)
        w2_raw = mb("w2_raw", [P, NR, UC, D], fp32)
        w1_hi, w1_lo = mb("w1_hi", [P, 2, KC, UF], f32r), mb("w1_lo", [P, 2, KC, UF], f32r)
        w2_hi, w2_lo = mb("w2_hi", [P, 2, UC, D], f32r), mb("w2_lo", [P, 2, UC, D], f32r)
        tok = mb("tok", [P, RT, ROW], fp32)
        tokn = mb("tokn", [P, RT, D], fp32)
        tT_hi, tT_lo = mb("tT_hi", [P, KC, CAP], f32r), mb("tT_lo", [P, KC, CAP], f32r)
        hid = mb("hid", [P, UC, CAP], fp32)
        h_hi, h_lo = mb("h_hi", [P, UC, CAP], f32r), mb("h_lo", [P, UC, CAP], f32r)
        b2_sb = mb("b2_sb", [P, D], fp32)
        y_sb = mb("y_sb", [P, RT, D], fp32)
        e_moments = mb("e_moments", [P, RT, 6], fp32)
        e_mean_var = mb("e_mean_var", [P, RT, 2], fp32)
        e_var_eps = mb("e_var_eps", [P, RT], fp32)
        e_rstd = mb("e_rstd", [P, RT], fp32)
        tok_id = mb("tok_id", [P, RT], u32)

        banks = [ctx.enter_context(nc.psum_tensor(f"bank{i}", [P, 512], fp32)) for i in range(8)]
        row_bank, col_bank = banks[0:2], banks[2:4]
        ctx_bank, sum_bank = banks[4], banks[5]
        g_bank = banks[6:8]
        hb_bank, y_bank, tt_bank = banks[0:2], banks[2:4], banks[4:6]

        ld_w = {n: sem("ld_" + n) for n in
                ("ctx", "wk0", "wv0", "wk1", "wv1", "wq0", "wo0", "wq1", "wo1", "rhs", "small", "bv", "bo")}
        consts_ready, pool_step, dve_step = sem("consts_ready"), sem("pool_step"), sem("dve_step")
        act_step = sem("act_step")
        k_done, k_evac, v_done, v_evac = sem("k_done"), sem("k_evac"), sem("v_done"), sem("v_evac")
        kd_hi_done, kd_done = sem("kd_hi_done"), sem("kd_done")
        wq_hi_done, wq_done, wo_hi_done, wo_done = (sem("wq_hi_done"), sem("wq_done"),
                                                    sem("wo_hi_done"), sem("wo_done"))
        met = sem("met")
        dve_consts, empty_row, hide_wide = sem("dve_consts"), sem("empty_row"), sem("hide_wide")
        rhs_amax, rhs_all, rhs_done = sem("rhs_amax"), sem("rhs_all"), sem("rhs_done")
        xa_load = [sem(f"xa_load{j}") for j in range(NSUB)]
        xb_load = [sem(f"xb_load{j}") for j in range(2)]
        xb_biased = sem("xb_biased")
        seg_load, hide_step, hide_done = sem("seg_load"), sem("hide_step"), sem("hide_done")
        stats, aggr, rstd_step, rstd_done, xn_done = (sem("stats"), sem("aggr"), sem("rstd_step"),
                                                      sem("rstd_done"), sem("xn_done"))
        xT_done, xT_hi_done, xT_lo_done = sem("xT_done"), sem("xT_hi_done"), sem("xT_lo_done")
        q_done, q_hi_done, q_lo_done = sem("q_done"), sem("q_hi_done"), sem("q_lo_done")
        rows_done, max_done, logc_put = sem("rows_done"), sem("max_done"), sem("logc_put")
        nmT_done, nmT_evac = sem("nmT_done"), sem("nmT_evac")
        cols_done, exp_done, pv_done = sem("cols_done"), sem("exp_done"), sem("pv_done")
        inv_done, norm_done, c_hi_done, c_lo_done = (sem("inv_done"), sem("norm_done"),
                                                     sem("c_hi_done"), sem("c_lo_done"))
        o_done, res_done = sem("o_done"), sem("res_done")
        t_stats, t_aggr, t_rstd_step, t_rstd_done = (sem("t_stats"), sem("t_aggr"), sem("t_rstd_step"),
                                                     sem("t_rstd_done"))
        txn_done = sem("txn_done")
        f_step, f_round, f_z, f_zT, f_zT_evac, f_acc, f_deq, x2_done = (
            sem("f_step"), sem("f_round"), sem("f_z"), sem("f_zT"), sem("f_zT_evac"),
            sem("f_acc"), sem("f_deq"), sem("x2_done"))
        x2_store = [sem(f"x2_store{j}") for j in range(NSUB)]
        r_T, r_T_evac, r_log, r_log_evac, r_lt, r_lt_evac = (
            sem("r_T"), sem("r_T_evac"), sem("r_log"), sem("r_log_evac"), sem("r_lt"), sem("r_lt_evac"))
        r_step, r_negtop, r_exp, r_hot, r_cum, r_slot, r_plain = (
            sem("r_step"), sem("r_negtop"), sem("r_exp"), sem("r_hot"), sem("r_cum"), sem("r_slot"), sem("r_plain"))
        plain_store, slot_init, slot_store = sem("plain_store"), sem("slot_init"), sem("slot_store")
        w_load = [[sem(f"w{n}_load{r}") for r in range(NR)] for n in (1, 2)]
        w_hi_done, w_lo_done = sem("w_hi_done"), sem("w_lo_done")
        tok_load, b2_load = sem("tok_load"), sem("b2_load")
        e_stats, e_aggr, e_rstd_step, e_rstd_done, e_xn = (sem("e_stats"), sem("e_aggr"), sem("e_rstd_step"),
                                                      sem("e_rstd"), sem("e_xn"))
        e_T, e_T_hi, e_T_lo = sem("e_T"), sem("e_T_hi"), sem("e_T_lo")
        e_h, e_relu, e_hhi, e_hlo = sem("e_h"), sem("e_relu"), sem("e_hhi"), sem("e_hlo")
        e_y, e_yb, e_yout, e_id, y_store = sem("e_y"), sem("e_yb"), sem("e_yout"), sem("e_id"), sem("y_store")

        SMALL = [(seg_col[:, :], segT), (bq_sb[:, :], bq1), (bk_sb[:, :], bk1),
                 (wsw_sb[:, :, :], wsw.rearrange("(k p) n -> p k n", p=P)), (bsw_sb[:, :], bsw), (b1_sb[:, :], b1)]
        ROUTE_STEPS = 22

        def bodies(engine, L, emit, loads=False):
            emit(L, -1, True, False, False, 0, 0)
            emit(L, 0, True, True, False, 0, 0)
            with engine.Fori(1, NSUP_B - 1) as i:
                emit(L, i, True, True, True, 0, 0)
            emit(L, NSUP_B - 1, True, True, True, 0, 1)
            with engine.Fori(NSUP_B, NSUP - 1 - loads) as i:
                emit(L, i, True, True, True, 1, 1)
            if loads:
                emit(L, NSUP - 2, True, True, True, 1, 1)
            emit(L, NSUP - 1, False, True, True, 1, 1)
            emit(L, NSUP, False, False, True, 1, 1)

        def last(L, i):
            return isinstance(i, int) and i == NSUP - 1

        def mm3(out, a_hi, a_lo, b_hi, b_lo, start, stop):
            nc.tensor.matmul(out, a_hi, b_hi, start=start, stop=False)
            nc.tensor.matmul(out, a_hi, b_lo, start=False, stop=False)
            return nc.tensor.matmul(out, a_lo, b_hi, start=False, stop=stop)

        def wait(e, s, v):
            if not isinstance(v, int) or v > 0:
                e.wait_ge(s, v)

        def wait_apart(e, s, v):
            wait(e, s, v)
            e.sem_inc(met, 1)

        def cols128(n):
            return slice(n * P, (n + 1) * P)

        block = ctx.enter_context(nc.Block())


        @block.sync
        def _(sp):
            def load(dst, src, s):
                sp.dma_start(dst, src).then_inc(s, 16)

            def chunked(w):
                return w.rearrange("(k p) n -> p k n", p=P)

            load(ctxT_sb, chunked(ctxT), ld_w["ctx"])
            load(wk_stage, chunked(wkv0[:, 0:D]), ld_w["wk0"])
            load(w_stage[:, :, :], chunked(wq0), ld_w["wq0"])
            load(wv_stage, chunked(wkv0[:, D:2 * D]), ld_w["wv0"])
            for dst, src in SMALL:
                load(dst, src, ld_w["small"])
            load(ctx_f[:, :], bv1.to_broadcast([P, D]), ld_w["bv"])
            sp.wait_ge(k_done, KC)
            load(wk_stage, chunked(wqkv1[:, D:2 * D]), ld_w["wk1"])
            sp.wait_ge(v_done, B)
            load(wv_stage, chunked(wqkv1[:, 2 * D:3 * D]), ld_w["wv1"])
            sp.wait_ge(wq_done, 1)
            load(w_stage[:, :, :], chunked(wo0), ld_w["wo0"])
            sp.wait_ge(wo_done, 1)
            load(w_stage[:, :, :], chunked(rhs), ld_w["rhs"])
            sp.wait_ge(empty_row, 2)
            for n in range(E * RT):
                load(slot_tiles[n, :, :], xs[:, 0, :], slot_init)
            sp.wait_ge(v_done, 2 * B)
            sp.wait_ge(k_done, 2 * KC)

            for L in range(2):
                src = (x_tiles, x2_tiles)[L]
                if L == 0:
                    sp.wait_ge(rhs_done, 1)
                    load(w_stage[:, :, :], chunked(wqkv1[:, 0:D]), ld_w["wq1"])
                else:
                    sp.wait_ge(wq_done, 2)
                    load(w_stage[:, :, :], chunked(wo1), ld_w["wo1"])
                    sp.wait_ge(f_deq, NT)
                    load(bo_sb[:, :], bo1.to_broadcast([P, D]), ld_w["bo"])

                def load_xa(L, i, j):
                    wait(sp, xT_done, NSUB * (NSUP * L + i - 1) + j + 1)
                    if L == 1:
                        sp.wait_ge(x2_store[j], 16 * (i + 1))
                    load(xa[:, j, :], src[NSUB * i + j, :, :], xa_load[j])

                def load_xb(L, i, j):
                    wait(sp, res_done, NSUB * (NSUP * L + i) + j - 1)
                    load(xb[:, j % 2, :], src[NSUB * i + j, :, :], xb_load[j % 2])

                def body(L, i, front, middle, tail, batch, front_batch):
                    if front and L == 0:
                        wait(sp, hide_step, 2 * i + 1)
                        load(seg_row[:, :], seg[:, bass.ds((i + 1) * SUP, SUP)].to_broadcast([KEYS, SUP]), seg_load)
                    if not middle and not tail:
                        for j in range(NSUB):
                            load_xa(L, 0, j)
                    if not isinstance(i, int) or i < NSUP - 2:
                        for j in range(NSUB):
                            load_xa(L, i + 2, j)
                    if middle:
                        load_xb(L, i, 0)
                        load_xb(L, i, 1)
                    if tail:
                        for j in range(NSUB):
                            n = NSUB * (i - 1) + j
                            if L == 0:
                                sp.wait_ge(x2_done, n + 1)
                                load(x2_tiles[n, :, :], xs[:, j, 0:D], x2_store[j])
                            else:
                                sp.wait_ge(r_plain, n + 1)
                                load(out_tiles[n, :, :], xn[:, j, :], plain_store)
                    if middle:
                        load_xb(L, i, 2)
                        load_xb(L, i, 3)
                bodies(sp, L, body, loads=True)

            sp.wait_ge(slot_store, 16 * NT)
            sp.wait_ge(plain_store, 16 * NT)
            w1_u = w1.rearrange("e (k p) (u f) -> e u p k f", p=P, u=NU)
            w2_u = w2.rearrange("e (u c p) d -> e u p c d", p=P, u=NU)

            def expert_loads(e):
                wait(sp, e_yout, RT * e)
                for r in range(RT):
                    load(tok[:, r, :], slot_tiles[RT * e + r, :, :], tok_load)
                load(b2_sb[:, :], b2[bass.ds(e, 1), :].to_broadcast([P, D]), b2_load)

            def unit_loads(e, u):
                wait(sp, w_lo_done, 2 * (NU * (e - 1) + u + 1))
                load(w1_raw[:, u, :, :], w1_u[e, u, :, :, :], w_load[0][u])
                load(w2_raw[:, u, :, :], w2_u[e, u, :, :, :], w_load[1][u])

            def expert(e):
                for u in range(NU):
                    unit_loads(e, u)
                    if u == 0:
                        expert_loads(e)
            expert(0)
            with sp.Fori(1, E) as e:
                expert(e)

        @block.gpsimd
        def _(pool):
            g = nc.gpsimd
            steps = [0]

            def step(ins):
                steps[0] += 1
                ins.then_inc(pool_step, 1)
                pool.wait_ge(pool_step, steps[0])

            step(g.memset(ident[:, :], 0.0))
            g.affine_select(out=ident[:, :], in_=ident[:, :], compare_op=ALU.not_equal, fill=1.0,
                            base=0, pattern=[[-1, P]], channel_multiplier=1).then_inc(consts_ready, 1)
            g.memset(kd_hi[:, :, :, :].bitcast(fp32), 0.0).then_inc(consts_ready, 1)
            g.memset(eps_half[:, :], -0.5)
            g.memset(ones[:, :], 1.0)
            g.memset(minus_magic[:, :], -MAGIC)
            g.memset(carry[:, :], 0.0)
            g.memset(onesb[:, :], 1.0)
            step(g.memset(upto[:, :], 1.0))
            g.affine_select(out=upto[:, :], in_=upto[:, :], compare_op=ALU.is_ge, fill=0.0,
                            base=0, pattern=[[1, P]], channel_multiplier=-1)
            g.iota(key_num[:, :], pattern=[[0, 1]], base=0, channel_multiplier=1,
                   allow_small_or_imprecise_dtypes=True)
            g.iota(lane8[:, :], pattern=[[1, E]], base=0, channel_multiplier=0,
                   allow_small_or_imprecise_dtypes=True)
            g.iota(token_num[:, :], pattern=[[P, NT]], base=0, channel_multiplier=1).then_inc(consts_ready, 1)
            g.memset(xs[:, 1:NSUB, D:ROW], 0.0)
            step(g.memset(xs[:, 0, :], 0.0))
            g.iota(xs[:, 0, D:D + 1].bitcast(i32), pattern=[[0, 1]], base=NOWHERE,
                   channel_multiplier=0).then_inc(empty_row, 2)
            step(g.memset(select_f[:, :, :], 1.0))
            step(g.affine_select(out=select_f[:, :, :], in_=select_f[:, :, :], compare_op=ALU.is_equal, fill=0.0,
                                 base=0, pattern=[[-1, H], [0, KEYS]], channel_multiplier=1))
            far = KEYS
            g.affine_select(out=select_f[:, :, :], in_=select_f[:, :, :], compare_op=ALU.is_gt, fill=1.0,
                            base=far * (KEYS - 1) + H, pattern=[[0, H], [-far, KEYS]],
                            channel_multiplier=-1).then_inc(consts_ready, 1)
            pool.wait_ge(rhs_amax, 1)
            g.partition_all_reduce(rscale[:, :], xn[:, 0, :], P, bass.bass_isa.ReduceOp.absmax).then_inc(rhs_all, 1)

            def inverse_root(ve, mv, r, ready, count, mid, mid_count, done):
                wait_apart(pool, ready, count)
                g.tensor_scalar(ve[:, :], mv[:, :, 1], EPS, 0.0, ALU.add, ALU.add).then_inc(mid, 1)
                pool.wait_ge(mid, mid_count)
                n = ve.shape[1]
                g.tensor_tensor(r[:, :], ve[:, :], eps_half[:, 0:n], ALU.pow).then_inc(done, 1)

            for L in range(2):
                def bias_xb(L, i, j):
                    n = NSUP * L + i
                    pool.wait_ge(xb_load[j % 2], 16 * (2 * n + j // 2 + 1))
                    g.tensor_tensor(xb[:, j % 2, :], xb[:, j % 2, :], bo_sb[:, :], ALU.add).then_inc(xb_biased, 1)

                def body(L, i, front, middle, tail, batch, front_batch):
                    nf, nb = NSUP * L + i + 1, NSUP * L + i - 1
                    if front:
                        inverse_root(var_eps, mean_var, rstd, aggr, NSUB * (nf + 1), rstd_step, nf + 1, rstd_done)
                    if tail:
                        inverse_root(t_var_eps, t_mean_var, t_rstd, t_aggr, NSUB * (nb + 1), t_rstd_step, nb + 1,
                                     t_rstd_done)
                    if L == 1 and middle:
                        bias_xb(L, i, 0)
                        bias_xb(L, i, 1)
                    if L == 1 and tail:
                        wait_apart(pool, r_slot, i)
                        for j in range(NSUB):
                            pool.indirect_dma_start(
                                slots_dram, bass.IndirectOffsetOnAxis(ap=slot[:, j:j + 1], axis=0),
                                xs[:, j, :], None, bounds_check=E * CAP - 1, oob_is_err=False).then_inc(slot_store, 16)
                    if L == 1 and middle:
                        bias_xb(L, i, 2)
                        bias_xb(L, i, 3)
                if L == 1:
                    pool.wait_ge(slot_init, 16 * E * RT)
                    pool.wait_ge(ld_w["bo"], 16)
                bodies(pool, L, body)

            def expert(e):
                inverse_root(e_var_eps, e_mean_var, e_rstd, e_aggr, RT * (e + 1), e_rstd_step, e + 1, e_rstd_done)
                for r in range(RT):
                    wait_apart(pool, e_yout, RT * e + r + 1)
                    pool.indirect_dma_start(
                        out, bass.IndirectOffsetOnAxis(ap=tok_id[:, r:r + 1], axis=0),
                        y_sb[:, r, :], None, bounds_check=T - 1, oob_is_err=False).then_inc(y_store, 16)
            pool.wait_ge(plain_store, 16 * NT)
            with pool.Fori(0, E) as e:
                expert(e)
            pool.wait_ge(y_store, 16 * E * RT)

        @block.scalar
        def _(act):
            a = nc.scalar

            def k_copy(L):
                for m in range(KC):
                    act.wait_ge(k_done, KC * L + m + 1)
                    bank = g_bank[m % 2][:, 0:B * KEYS]
                    if L == 0:
                        a.activation(kT[L][:, m // 2, m % 2, :], bank, ACT.Copy).then_inc(k_evac, 1)
                    else:
                        a.activation(kT[L][:, m // 2, m % 2, :], bank, ACT.Identity, bias=bk_sb[:, m:m + 1]).then_inc(k_evac, 1)

            def k_high(L, b):
                act.wait_ge(k_evac, KC * (L + 1))
                if L == 0:
                    act.wait_ge(consts_ready, 2)
                else:
                    act.wait_ge(cols_done, H * (NSUP_B * (b + 1)))
                    act.wait_ge(rows_done, H * (NSUP_B * (b + 1)))
                for g in range(HPC):
                    rows = slice(HD * g, HD * (g + 1))
                    a.activation(kd_hi[rows, b, :, cols128(g)].rearrange("p (a c) n -> p a c n", c=2),
                                 kT[L][rows, :, :, b * KEYS:(b + 1) * KEYS],
                                 ACT.Copy).then_inc(kd_hi_done, 1)

            act.wait_ge(ld_w["small"], 16 * len(SMALL))
            k_copy(0)
            k_high(0, 0)
            act.wait_ge(ld_w["wq0"], 16)
            a.activation(wq_hi[:, :, :], w_stage[:, :, :], ACT.Copy).then_inc(wq_hi_done, 1)
            k_high(0, 1)
            act.wait_ge(ld_w["wo0"], 16)
            a.activation(wo_hi[:, :, :], w_stage[:, :, :], ACT.Copy).then_inc(wo_hi_done, 1)
            k_copy(1)

            def body(L, i, front, middle, tail, batch, front_batch):
                n, nf, nb = NSUP * L + i, NSUP * L + i + 1, NSUP * L + i - 1

                def exps(m, g):
                    u = HPC * m + g
                    act.wait_ge(cols_done, H * n + u + 1)
                    wait(act, pv_done, KC * n + m - 1)
                    a.activation(probs[:, u % (2 * HPC), :], col_bank[u % 2][:, :], ACT.Exp,
                                 scale=SCALE).then_inc(exp_done, 1)

                def x_high(j):
                    act.wait_ge(xT_done, NSUB * nf + j + 1)
                    wait(act, q_done, KC * nf)
                    a.activation(xT_hi[:, :, cols128(j)], g_bank[0][:, :].rearrange("p (k t) -> p k t", k=KC),
                                 ACT.Copy).then_inc(xT_hi_done, 1)

                def c_high(m):
                    act.wait_ge(norm_done, KC * n + m + 1)
                    wait(act, o_done, NSUB * n)
                    a.activation(cT_hi[:, m, :], ctx_f[:, :], ACT.Copy).then_inc(c_hi_done, 1)

                def int8(j):
                    t = NSUB * nb + j
                    act.wait_ge(f_round, t + 1)
                    a.activation(zb[:, :], xn[:, j, :], ACT.Identity, bias=minus_magic[:, 0:1]).then_inc(f_z, 1)
                    act.wait_ge(f_zT, t + 1)
                    a.activation(zT[:, :, :], g_bank[1][:, 0:D // 2].bitcast(bf16).rearrange("p (k t) -> p k t", k=KC),
                                 ACT.Copy).then_inc(f_zT_evac, 1)

                def routing(j):
                    t = NSUB * (i - 1) + j
                    act.wait_ge(r_T, t + 1)
                    a.activation(xrT[:, :, :], g_bank[1][:, :].rearrange("p (k t) -> p k t", k=KC),
                                 ACT.Copy).then_inc(r_T_evac, 1)
                    act.wait_ge(r_log, t + 1)
                    a.activation(logT[:, cols128(j)], g_bank[1][0:E, 0:P], ACT.Identity,
                                 bias=bsw_sb[:, 0:1]).then_inc(r_log_evac, 1)

                if L == 0 and last(L, i):
                    act.wait_ge(ld_w["wq1"], 16)
                    act.wait_ge(q_done, KC * NSUP)
                    a.activation(wq_hi[:, :, :], w_stage[:, :, :], ACT.Copy).then_inc(wq_hi_done, 1)
                    k_high(1, 0)
                if L == 1 and not middle and not tail:
                    k_high(1, 1)
                for m in range(KC):
                    if middle:
                        for g in range(HPC):
                            exps(m, g)
                    if front:
                        x_high(m)
                    if middle and m:
                        c_high(m - 1)
                    if tail:
                        (int8, routing)[L](m)
                if middle:
                    c_high(KC - 1)
                if tail and L == 1:
                    act.wait_ge(r_negtop, i)
                    a.activation(expl[:, :, :], expl[:, :, :], ACT.Exp).then_inc(r_exp, 1)
                if front:
                    for m in range(KC):
                        act.wait_ge(q_done, KC * nf + m + 1)
                        if L == 0:
                            a.activation(qT_hi[:, m, :], g_bank[m % 2][:, :], ACT.Copy).then_inc(q_hi_done, 1)
                        else:
                            a.activation(qT_hi[:, m, :], g_bank[m % 2][:, :], ACT.Identity,
                                         bias=bq_sb[:, m:m + 1]).then_inc(q_hi_done, 1)
                    rows = H + 2 if L == 0 else H
                    act.wait_ge(nmT_done, nf + 1)
                    a.activation(nmT[0:rows, :], g_bank[0][0:rows, :], ACT.Copy).then_inc(nmT_evac, 1)

            bodies(act, 0, body)
            act.wait_ge(ld_w["wo1"], 16)
            act.wait_ge(o_done, NSUB * NSUP)
            a.activation(wo_hi[:, :, :], w_stage[:, :, :], ACT.Copy).then_inc(wo_hi_done, 1)
            bodies(act, 1, body)

            def split_high(e, u):
                c = NU * e + u
                act.wait_ge(w_load[0][u], 16 * (e + 1))
                wait(act, e_h, UC * (c - 1))
                a.activation(w1_hi[:, u % 2, :, :], w1_raw[:, u, :, :], ACT.Copy).then_inc(w_hi_done, 1)
                act.wait_ge(w_load[1][u], 16 * (e + 1))
                wait(act, e_y, c - 1)
                a.activation(w2_hi[:, u % 2, :, :], w2_raw[:, u, :, :], ACT.Copy).then_inc(w_hi_done, 1)

            def hidden(e, u):
                c = NU * e + u
                for f in range(UC):
                    act.wait_ge(e_h, UC * c + f + 1)
                    if f == 0:
                        wait(act, e_hlo, c)
                    a.activation(hid[:, f, :], hb_bank[f % 2][:, 0:CAP], ACT.Relu,
                                 bias=b1_sb[:, bass.ds(c * UC + f, 1)]).then_inc(e_relu, 1)
                act.wait_ge(e_relu, UC * (c + 1))
                wait(act, e_y, c)
                a.activation(h_hi[:, :, :], hid[:, :, :], ACT.Copy).then_inc(e_hhi, 1)

            def rows_high(e):
                for r in range(RT):
                    act.wait_ge(e_T, RT * e + r + 1)
                    a.activation(tT_hi[:, :, cols128(r)], tt_bank[r][:, :].rearrange("p (k t) -> p k t", k=KC),
                                 ACT.Copy).then_inc(e_T_hi, 1)

            act.wait_ge(plain_store, 16 * NT)
            act.wait_ge(slot_store, 16 * NT)
            split_high(0, 0)
            rows_high(0)

            def expert(e, more):
                for u in range(NU):
                    if u < NU - 1:
                        split_high(e, u + 1)
                    elif more:
                        split_high(e + 1, 0)
                    hidden(e, u)
                if more:
                    rows_high(e + 1)
            expert(0, True)
            with act.Fori(1, E - 1) as e:
                expert(e, True)
            expert(E - 1, False)

        @block.vector
        def _(dve):
            v = nc.vector
            steps = [0]

            def step(ins):
                steps[0] += 1
                ins.then_inc(dve_step, 1)
                dve.wait_ge(dve_step, steps[0])

            def v_copy(L):
                for b in range(B):
                    dve.wait_ge(v_done, B * L + b + 1)
                    if L == 0:
                        v.tensor_copy(v_sb[:, L, b, :], row_bank[b][:, :]).then_inc(v_evac, 1)
                    else:
                        v.tensor_tensor(v_sb[:, L, b, :], row_bank[b][:, :], ctx_f[:, :], ALU.add).then_inc(v_evac, 1)

            def k_low(L, b):
                for g in range(HPC):
                    rows = slice(HD * g, HD * (g + 1))
                    dve.wait_ge(kd_hi_done, HPC * (B * L + b) + g + 1)
                    v.tensor_tensor(kd_lo[rows, b, :, cols128(g)].rearrange("p (a c) n -> p a c n", c=2),
                                    kT[L][rows, :, :, b * KEYS:(b + 1) * KEYS],
                                    kd_hi[rows, b, :, cols128(g)].bitcast(fp32).rearrange("p (a c) n -> p a c n", c=2),
                                    ALU.subtract).then_inc(kd_done, 1)

            v.memset(kd_lo[:, :, :, :].bitcast(fp32), 0.0).then_inc(dve_step, 1)
            steps[0] += 1
            dve.wait_ge(consts_ready, 4)
            v.tensor_copy(identb[:, :], ident[:, :]).then_inc(dve_consts, 1)
            v.tensor_copy(select[:, :, :], select_f[:, :, :]).then_inc(dve_consts, 1)
            dve.wait_ge(dve_step, steps[0])
            k_low(0, 0)
            dve.wait_ge(wq_hi_done, 1)
            v.tensor_tensor(wq_lo[:, :, :], w_stage[:, :, :], wq_hi[:, :, :].bitcast(fp32),
                            ALU.subtract).then_inc(wq_done, 1)
            v_copy(0)
            k_low(0, 1)
            dve.wait_ge(ld_w["small"], 16 * len(SMALL))
            step(v.tensor_copy(seg_cf[:, :], seg_col[:, :]))
            step(v.memset(logc[:, :, :], 0.0))
            counts = log_counts()
            for c in range(2, LOOKBACK + 2):
                for part in range(2):
                    gain = counts[c - 1][part] - counts[c - 2][part]
                    step(v.tensor_scalar(seg_t[:, :], seg_cf[:, :], float(KEYS - 2 + c) - 0.5, gain,
                                         ALU.is_gt, ALU.mult))
                    step(v.tensor_tensor(logc[:, :, part], logc[:, :, part], seg_t[:, :], ALU.add))
            dve.wait_ge(ld_w["bv"], 16)
            v_copy(1)
            dve.wait_ge(wo_hi_done, 1)
            v.tensor_tensor(wo_lo[:, :, :], w_stage[:, :, :], wo_hi[:, :, :].bitcast(fp32),
                            ALU.subtract).then_inc(wo_done, 1)
            dve.wait_ge(ld_w["rhs"], 16)
            v.tensor_reduce(xn[:, 0, :], w_stage[:, :, :].rearrange("p k n -> p n k"), AX.X, ALU.max,
                            apply_absolute_value=True).then_inc(rhs_amax, 1)
            dve.wait_ge(rhs_all, 1)
            step(v.tensor_scalar(rscale[:, :], rscale[:, :], 1e-12, float(np.float32(1) / np.float32(127)),
                                 ALU.max, ALU.mult))
            step(v.reciprocal(xn[:, 1, :], rscale[:, :]))
            for k in range(KC):
                step(v.tensor_tensor(xn[:, 0, :], w_stage[:, k, :], xn[:, 1, :], ALU.mult))
                step(v.tensor_scalar(xn[:, 0, :], xn[:, 0, :], 127.0, -127.0, ALU.min, ALU.max))
                step(v.tensor_scalar(rq[:, k, :], xn[:, 0, :], MAGIC, MAGIC, ALU.add, ALU.subtract))
            v.tensor_copy(seg_t[:, 0:1], seg_cf[:, 0:1]).then_inc(rhs_done, 1)

            def layer_norm_stats(xt, n_rows, mom, mv, s1, s2, n, loads):
                for j in range(n_rows):
                    loads(j)
                    v.bn_stats(mom[:, j, :], xt(j)).then_inc(s1, 1)
                for j in range(n_rows):
                    wait_apart(dve, s1, n_rows * n + j + 1)
                    v.bn_aggr(mv[:, j, :], mom[:, j, :]).then_inc(s2, 1)

            def body(L, i, front, middle, tail, batch, front_batch):
                n, nf, nb = NSUP * L + i, NSUP * L + i + 1, NSUP * L + i - 1
                if L == 0 and last(L, i):
                    dve.wait_ge(wq_hi_done, 2)
                    v.tensor_tensor(wq_lo[:, :, :], w_stage[:, :, :], wq_hi[:, :, :].bitcast(fp32),
                                    ALU.subtract).then_inc(wq_done, 1)
                    k_low(1, 0)
                if L == 1 and not middle and not tail:
                    k_low(1, 1)
                if front:
                    layer_norm_stats(lambda j: xa[:, j, :], NSUB, moments, mean_var, stats, aggr, nf,
                                     lambda j: dve.wait_ge(xa_load[j], 16 * (nf + 1)))
                if tail:
                    layer_norm_stats(lambda j: xs[:, j, 0:D], NSUB, t_moments, t_mean_var, t_stats, t_aggr, nb,
                                     lambda j: dve.wait_ge(res_done, NSUB * nb + j + 1))
                if front and L == 0:
                    dve.wait_ge(seg_load, 16 * (i + 2))
                    v.tensor_scalar(seg_f[:, :], seg_row[:, :], 0.0, float(KEYS - 1 + LOOKBACK),
                                    ALU.max, ALU.min).then_inc(hide_step, 1)
                    dve.wait_ge(hide_step, 2 * (i + 1) + 1)
                    v.tensor_scalar(seg_f[:, :], seg_f[:, :], key_num[:, 0:1], LOOKBACK / 2,
                                    ALU.subtract, ALU.subtract).then_inc(hide_step, 1)
                if front:
                    dve.wait_ge(rstd_done, nf + 1)
                    for j in range(NSUB):
                        v.tensor_scalar(xa[:, j, :], xa[:, j, :], mean_var[:, j, 0:1], rstd[:, j:j + 1],
                                        ALU.subtract, ALU.mult).then_inc(xn_done, 1)

                def x_low(j):
                    dve.wait_ge(xT_hi_done, NSUB * nf + j + 1)
                    v.tensor_tensor(xT_lo[:, :, cols128(j)], g_bank[0][:, :].rearrange("p (k t) -> p k t", k=KC),
                                    xT_hi[:, :, cols128(j)].bitcast(fp32), ALU.subtract).then_inc(xT_lo_done, 1)

                def norm(m):
                    dve.wait_ge(pv_done, KC * n + m + 1)
                    v.reciprocal(inv_sum[:, :], sum_bank[:, :]).then_inc(inv_done, 1)
                    dve.wait_ge(inv_done, KC * n + m + 1)
                    v.tensor_tensor(ctx_f[:, :], ctx_bank[:, :], inv_sum[:, :], ALU.mult).then_inc(norm_done, 1)

                def c_low(m):
                    dve.wait_ge(c_hi_done, KC * n + m + 1)
                    v.tensor_tensor(cT_lo[:, m, :], ctx_f[:, :], cT_hi[:, m, :].bitcast(fp32),
                                    ALU.subtract).then_inc(c_lo_done, 1)

                def tail_norm(j):
                    if j == 0:
                        dve.wait_ge(t_rstd_done, nb + 1)
                    v.tensor_scalar(xn[:, j, :], xs[:, j, 0:D], t_mean_var[:, j, 0:1], t_rstd[:, j:j + 1],
                                    ALU.subtract, ALU.mult).then_inc(txn_done, 1)

                def quantise(j):
                    c = 4 * (NSUB * nb + j)
                    dve.wait_ge(txn_done, NSUB * nb + j + 1)
                    v.tensor_reduce(amax[:, j:j + 1], xn[:, j, :], AX.X, ALU.max,
                                    apply_absolute_value=True).then_inc(f_step, 1)
                    dve.wait_ge(f_step, c + 1)
                    v.tensor_scalar(lscale[:, j:j + 1], amax[:, j:j + 1], 1e-12,
                                    float(np.float32(1) / np.float32(127)), ALU.max, ALU.mult).then_inc(f_step, 1)
                    dve.wait_ge(f_step, c + 2)
                    v.reciprocal(linv[:, j:j + 1], lscale[:, j:j + 1]).then_inc(f_step, 1)
                    dve.wait_ge(f_step, c + 3)
                    v.tensor_scalar(xn[:, j, :], xn[:, j, :], linv[:, j:j + 1], -127.0,
                                    ALU.mult, ALU.max).then_inc(f_step, 1)
                    dve.wait_ge(f_step, c + 4)
                    v.tensor_scalar(xn[:, j, :], xn[:, j, :], 127.0, MAGIC, ALU.min, ALU.add).then_inc(f_round, 1)

                def dequantise(j):
                    dve.wait_ge(f_acc, NSUB * nb + j + 1)
                    v.scalar_tensor_tensor(xn[:, j, :], g_bank[1][:, :], lscale[:, j:j + 1], rscale[:, :],
                                           ALU.mult, ALU.mult).then_inc(f_deq, 1)
                    dve.wait_ge(f_deq, NSUB * nb + j + 1)
                    v.tensor_tensor(xs[:, j, 0:D], xs[:, j, 0:D], xn[:, j, :], ALU.add).then_inc(x2_done, 1)

                if tail:
                    tail_norm(0)
                    if L == 0:
                        quantise(0)
                for m in range(KC):
                    if front:
                        x_low(m)
                    if middle and m:
                        norm(m - 1)
                    if tail and L == 0 and m:
                        dequantise(m - 1)
                    if tail and m < NSUB - 1:
                        tail_norm(m + 1)
                        if L == 0:
                            quantise(m + 1)
                    if middle and m:
                        c_low(m - 1)
                if middle:
                    norm(KC - 1)
                if tail and L == 0:
                    dequantise(NSUB - 1)
                if middle:
                    c_low(KC - 1)

                count = [0]

                def link(ins):
                    count[0] += 1
                    ins.then_inc(r_step, 1)
                    dve.wait_ge(r_step, ROUTE_STEPS * (i - 1) + count[0])

                def mark(ins):
                    count[0] += 1
                    ins.then_inc(r_step, 1)

                if tail and L == 1:
                    dve.wait_ge(r_lt, i)
                    v.tensor_copy(logits[:, :, :], g_bank[1][:, 0:NSUB * E].rearrange("p (j e) -> p j e", e=E))\
                        .then_inc(r_lt_evac, 1)
                    wait_apart(dve, r_lt_evac, i)
                    for j in range(NSUB):
                        mark(v.max(top8[:, j, :], logits[:, j, :]))
                    dve.wait_ge(r_step, ROUTE_STEPS * (i - 1) + count[0])
                    v.tensor_tensor(expl[:, :, :], logits[:, :, :],
                                    top8[:, :, 0:1].to_broadcast([P, NSUB, E]), ALU.subtract).then_inc(r_negtop, 1)
                    for j in range(NSUB):
                        mark(v.max_index(top_at[:, j, :], top8[:, j, :], logits[:, j, :]))
                    dve.wait_ge(r_step, ROUTE_STEPS * (i - 1) + count[0])
                    link(v.tensor_copy(route[:, :], top_at[:, :, 0]))
                    v.tensor_tensor(onehot[:, :, :], lane8[:, :].unsqueeze(1).to_broadcast([P, NSUB, E]),
                                    route[:, :].unsqueeze(2).to_broadcast([P, NSUB, E]), ALU.is_equal)\
                        .then_inc(r_hot, 1)
                    dve.wait_ge(r_exp, i)
                    link(v.tensor_reduce(psum_e[:, :], expl[:, :, :], AX.X, ALU.add))
                    link(v.reciprocal(pmax[:, :], psum_e[:, :]))
                    link(v.reciprocal(psum_e[:, :], pmax[:, :]))
                    link(v.tensor_tensor(scale_t[:, :], pmax[:, :], psum_e[:, :], ALU.mult))
                    dve.wait_ge(r_cum, i)
                    link(v.tensor_tensor(place[:, :, :], sum_bank[:, 0:NSUB * E].rearrange("p (j e) -> p j e", e=E),
                                         carry[:, :].unsqueeze(1).to_broadcast([P, NSUB, E]), ALU.add))
                    link(v.tensor_tensor(carry[:, :], sum_bank[:, NSUB * E:(NSUB + 1) * E], carry[:, :], ALU.add))
                    link(v.tensor_tensor(place[:, :, :], place[:, :, :], onehot[:, :, :], ALU.mult))
                    link(v.tensor_reduce(pos[:, :], place[:, :, :], AX.X, ALU.add))
                    mark(v.tensor_scalar(full[:, :], pos[:, :], CAP + 0.5, float(NOWHERE), ALU.is_gt, ALU.mult))
                    link(v.scalar_tensor_tensor(slot_f[:, :], route[:, :], float(CAP), pos[:, :], ALU.mult, ALU.add))
                    link(v.tensor_tensor(slot_f[:, :], slot_f[:, :], full[:, :], ALU.add))
                    mark(v.tensor_copy(xs[:, :, D + 1], scale_t[:, :]))
                    mark(v.tensor_copy(xs[:, :, D].bitcast(i32), token_num[:, bass.ds((i - 1) * NSUB, NSUB)]))
                    v.tensor_scalar(slot[:, :], slot_f[:, :], -1.0, 0.0, ALU.add, ALU.add).then_inc(r_slot, 1)
                    for j in range(NSUB):
                        v.scalar_tensor_tensor(xn[:, j, :], xn[:, j, :], scale_t[:, j:j + 1], xs[:, j, 0:D],
                                               ALU.mult, ALU.add).then_inc(r_plain, 1)
                    assert count[0] == ROUTE_STEPS

                if front:
                    if L == 0:
                        dve.wait_ge(hide_step, 2 * (i + 2))
                        v.tensor_tensor(seg_f[:, :], seg_f[:, :], seg_f[:, :], ALU.mult).then_inc(hide_wide, 1)
                        dve.wait_ge(hide_wide, i + 2)
                        wait(dve, cols_done, H * (i + 1))
                        v.tensor_scalar(hideT[:, :], seg_f[:, :], (LOOKBACK / 2 + 0.1) ** 2, HIDE,
                                        ALU.is_gt, ALU.mult).then_inc(hide_done, 1)
                        wait(dve, nmT_done, i + 1)
                        v.tensor_copy(neg_max[:, :, H:H + 2], logc[:, bass.ds((i + 1) * NSUB, NSUB), :])\
                            .then_inc(logc_put, 1)

                def q_low(m):
                    dve.wait_ge(q_hi_done, KC * nf + m + 1)
                    if L == 0:
                        v.tensor_tensor(qT_lo[:, m, :], g_bank[m % 2][:, :], qT_hi[:, m, :].bitcast(fp32),
                                        ALU.subtract).then_inc(q_lo_done, 1)
                    else:
                        v.scalar_tensor_tensor(qT_lo[:, m, :], g_bank[m % 2][:, :], bq_sb[:, m:m + 1],
                                               qT_hi[:, m, :].bitcast(fp32), ALU.add, ALU.subtract)\
                            .then_inc(q_lo_done, 1)

                def row_max(m):
                    for j in range(NSUB):
                        u = NSUB * m + j
                        dve.wait_ge(rows_done, H * nf + u + 1)
                        v.tensor_reduce(neg_max[:, j, HPC * m:HPC * (m + 1)],
                                        row_bank[u % 2][:, :].rearrange("p (g k) -> p g k", g=HPC), AX.X, ALU.max,
                                        negate=True).then_inc(max_done, 1)

                def residual(j):
                    t = NSUB * n + j
                    dve.wait_ge(o_done, t + 1)
                    if L == 0:
                        dve.wait_ge(xb_load[j % 2], 16 * (2 * n + j // 2 + 1))
                        wait(dve, x2_store[j], 16 * i)
                    else:
                        dve.wait_ge(xb_biased, NSUB * i + j + 1)
                        wait(dve, slot_store, 16 * NSUB * i)
                        wait(dve, r_plain, NSUB * (i - 1) + j + 1)
                    v.tensor_tensor(xs[:, j, 0:D], g_bank[j % 2][:, :], xb[:, j % 2, :], ALU.add).then_inc(res_done, 1)

                if middle and isinstance(i, int) and i == 0:
                    if L == 0:
                        dve.wait_ge(slot_init, 16 * E * RT)
                    else:
                        for j in range(NSUB):
                            dve.wait_ge(x2_store[j], 16 * NSUP)
                if front:
                    q_low(0)
                    q_low(1)
                    row_max(0)
                    q_low(2)
                    row_max(1)
                    q_low(3)
                    row_max(2)
                if middle:
                    residual(0)
                    residual(1)
                if front:
                    row_max(3)
                if middle:
                    residual(2)
                    residual(3)
                if tail and L == 1:
                    dve.wait_ge(plain_store, 16 * NSUB * i)

            bodies(dve, 0, body)
            dve.wait_ge(wo_hi_done, 2)
            v.tensor_tensor(wo_lo[:, :, :], w_stage[:, :, :], wo_hi[:, :, :].bitcast(fp32),
                            ALU.subtract).then_inc(wo_done, 1)
            bodies(dve, 1, body)

            def split_low(e, u):
                c = NU * e + u
                dve.wait_ge(w_hi_done, 2 * c + 1)
                v.tensor_tensor(w1_lo[:, u % 2, :, :], w1_raw[:, u, :, :], w1_hi[:, u % 2, :, :].bitcast(fp32),
                                ALU.subtract).then_inc(w_lo_done, 1)
                dve.wait_ge(w_hi_done, 2 * c + 2)
                v.tensor_tensor(w2_lo[:, u % 2, :, :], w2_raw[:, u, :, :], w2_hi[:, u % 2, :, :].bitcast(fp32),
                                ALU.subtract).then_inc(w_lo_done, 1)

            def rows_norm(e):
                layer_norm_stats(lambda r: tok[:, r, 0:D], RT, e_moments, e_mean_var, e_stats, e_aggr, e,
                                 lambda r: dve.wait_ge(tok_load, 16 * RT * (e + 1)))
                dve.wait_ge(e_rstd_done, e + 1)
                wait(dve, e_T, RT * e)
                for r in range(RT):
                    v.tensor_scalar(tokn[:, r, :], tok[:, r, 0:D], e_mean_var[:, r, 0:1], e_rstd[:, r:r + 1],
                                    ALU.subtract, ALU.mult).then_inc(e_xn, 1)

            def rows_low(e):
                for r in range(RT):
                    dve.wait_ge(e_T_hi, RT * e + r + 1)
                    v.tensor_tensor(tT_lo[:, :, cols128(r)], tt_bank[r][:, :].rearrange("p (k t) -> p k t", k=KC),
                                    tT_hi[:, :, cols128(r)].bitcast(fp32), ALU.subtract).then_inc(e_T_lo, 1)

            def hidden_low(e, u):
                c = NU * e + u
                dve.wait_ge(e_hhi, c + 1)
                wait(dve, e_y, c)
                v.tensor_tensor(h_lo[:, :, :], hid[:, :, :], h_hi[:, :, :].bitcast(fp32),
                                ALU.subtract).then_inc(e_hlo, 1)

            def results(e):
                dve.wait_ge(e_y, NU * (e + 1))
                dve.wait_ge(b2_load, 16 * (e + 1))
                wait(dve, y_store, 16 * RT * e)
                for r in range(RT):
                    v.tensor_tensor(y_sb[:, r, :], y_bank[r][:, :], b2_sb[:, :], ALU.add).then_inc(e_yb, 1)
                v.tensor_copy(tok_id[:, :], tok[:, :, D].bitcast(i32)).then_inc(e_id, 1)
                for r in range(RT):
                    dve.wait_ge(e_yb, RT * e + r + 1)
                    v.scalar_tensor_tensor(y_sb[:, r, :], y_sb[:, r, :], tok[:, r, D + 1:D + 2], tok[:, r, 0:D],
                                           ALU.mult, ALU.add).then_inc(e_yout, 1)

            dve.wait_ge(plain_store, 16 * NT)
            dve.wait_ge(slot_store, 16 * NT)
            split_low(0, 0)
            rows_norm(0)
            rows_low(0)

            def expert(e, more):
                for u in range(NU):
                    if u < NU - 1:
                        split_low(e, u + 1)
                    elif more:
                        split_low(e + 1, 0)
                    hidden_low(e, u)
                results(e)
                if more:
                    rows_norm(e + 1)
                    rows_low(e + 1)
            expert(0, True)
            with dve.Fori(1, E - 1) as e:
                expert(e, True)
            expert(E - 1, False)

        @block.tensor
        def _(pe):
            t = nc.tensor

            def k_and_v(L):
                if L == 0:
                    pe.wait_ge(ld_w["ctx"], 16)
                pe.wait_ge(ld_w[f"wk{L}"], 16)
                for m in range(KC):
                    wait(pe, k_evac, KC * L + m - 1)
                    for k in range(KC):
                        mm = t.matmul(g_bank[m % 2][:, 0:B * KEYS], wk_stage[:, k, cols128(m)], ctxT_sb[:, k, :],
                                      start=(k == 0), stop=(k == KC - 1))
                    mm.then_inc(k_done, 1)
                pe.wait_ge(ld_w[f"wv{L}"], 16)
                for b in range(B):
                    wait(pe, v_evac, B * L + b - 1)
                    for k in range(KC):
                        mm = t.matmul(row_bank[b][:, :], ctxT_sb[:, k, b * KEYS:(b + 1) * KEYS], wv_stage[:, k, :],
                                      start=(k == 0), stop=(k == KC - 1))
                    mm.then_inc(v_done, 1)

            k_and_v(0)
            k_and_v(1)
            pe.wait_ge(consts_ready, 4)
            pe.wait_ge(dve_consts, 2)
            pe.wait_ge(v_evac, 2 * B)
            pe.wait_ge(k_evac, 2 * KC)

            def body(L, i, front, middle, tail, batch, front_batch):
                n, nf, nb = NSUP * L + i, NSUP * L + i + 1, NSUP * L + i - 1

                def scores_cols(m, g):
                    u, h = HPC * m + g, HPC * m + g
                    bank = col_bank[u % 2][:, :]
                    if u == 0:
                        pe.wait_ge(nmT_evac, n + 1)
                        pe.wait_ge(q_lo_done, KC * (n + 1))
                        pe.wait_ge(kd_done, HPC * (B * L + batch + 1))
                    wait(pe, exp_done, H * n + u - 1)
                    k_hi, k_lo = kd_hi[:, batch, m, cols128(g)], kd_lo[:, batch, m, cols128(g)]
                    mm3(bank, k_hi, k_lo, qT_hi[:, m, :], qT_lo[:, m, :], True, False)
                    if L == 0:
                        t.matmul(bank, select[:, h, :], nmT[:, :], start=False, stop=False)
                        mm = t.matmul(bank, identb[:, :], hideT[:, :], start=False, stop=True)
                    else:
                        mm = t.matmul(bank, select[0:H, h, :], nmT[0:H, :], start=False, stop=True)
                    mm.then_inc(cols_done, 1)

                def weighted(m):
                    pe.wait_ge(exp_done, H * n + HPC * (m + 1))
                    wait(pe, norm_done, KC * n + m)
                    for g in range(HPC):
                        u, h = HPC * m + g, HPC * m + g
                        rows = slice(HD * g, HD * (g + 1))
                        t.matmul(ctx_bank[rows, :], v_sb[:, L, batch, HD * h:HD * (h + 1)],
                                 probs[:, u % (2 * HPC), :], start=True, stop=True, tile_position=(0, HD * g))
                    for g in range(HPC):
                        u = HPC * m + g
                        rows = slice(HD * g, HD * (g + 1))
                        mm = t.matmul(sum_bank[rows, :], ones[:, :], probs[:, u % (2 * HPC), :],
                                      start=True, stop=True, tile_position=(0, HD * g))
                    mm.then_inc(pv_done, 1)

                def x_transpose(j):
                    pe.wait_ge(xn_done, NSUB * nf + j + 1)
                    if j == 0:
                        wait(pe, nmT_evac, nf)
                        if L == 1 and isinstance(i, int) and i == -1:
                            pe.wait_ge(res_done, NSUB * NSUP)
                    else:
                        pe.wait_ge(xT_lo_done, NSUB * nf + j)
                    for k in range(KC):
                        mm = t.transpose(g_bank[0][:, cols128(k)], xa[:, j, cols128(k)], ident[:, :])
                    mm.then_inc(xT_done, 1)

                def bank1_free():
                    if tail and L == 0:
                        pe.wait_ge(f_deq, NSUB * (nb + 1))
                    elif tail:
                        pe.wait_ge(r_lt_evac, i)
                    elif L == 1 and not middle:
                        pe.wait_ge(f_deq, NSUB * NSUP)

                def project_q(m):
                    if m == 0:
                        pe.wait_ge(wq_done, L + 1)
                        pe.wait_ge(xT_lo_done, NSUB * (nf + 1))
                    elif m == 1:
                        bank1_free()
                    else:
                        pe.wait_ge(q_lo_done, KC * nf + m - 1)
                    for k in range(KC):
                        mm = mm3(g_bank[m % 2][:, :], wq_hi[:, k, cols128(m)], wq_lo[:, k, cols128(m)],
                                 xT_hi[:, k, :], xT_lo[:, k, :], k == 0, k == KC - 1)
                    mm.then_inc(q_done, 1)

                def scores_rows(m):
                    if m == 0:
                        pe.wait_ge(kd_done, HPC * (B * L + front_batch + 1))
                        if L == 0:
                            pe.wait_ge(hide_done, i + 2)
                    pe.wait_ge(q_hi_done, KC * nf + m + 1)
                    for j in range(NSUB):
                        u = NSUB * m + j
                        bank = row_bank[u % 2][:, :]
                        wait(pe, max_done, H * nf + u - 1)
                        mm = t.matmul(bank, qT_hi[:, m, cols128(j)], kd_hi[:, front_batch, m, :],
                                      start=True, stop=(L == 1))
                        if L == 0:
                            mm = t.matmul(bank.rearrange("p (g k) -> p g k", g=HPC), hideT[:, cols128(j)],
                                          identb[:, :].unsqueeze(1).to_broadcast([P, HPC, KEYS]),
                                          start=False, stop=True)
                        mm.then_inc(rows_done, 1)

                def max_transpose():
                    rows = H + 2 if L == 0 else H
                    pe.wait_ge(max_done, H * (nf + 1))
                    if L == 0:
                        pe.wait_ge(logc_put, i + 2)
                    if middle:
                        wait_apart(pe, res_done, NSUB * n + 3)
                    else:
                        wait_apart(pe, q_lo_done, KC * nf + 3)
                    for j in range(NSUB):
                        mm = t.transpose(g_bank[0][0:rows, cols128(j)], neg_max[:, j, 0:rows], ident[:, :])
                    mm.then_inc(nmT_done, 1)

                def project_out(j):
                    if j == 0:
                        pe.wait_ge(wo_done, L + 1)
                        pe.wait_ge(c_lo_done, KC * (n + 1))
                        if front:
                            pe.wait_ge(q_lo_done, KC * nf + 3)
                    elif j == 1:
                        if front:
                            pe.wait_ge(q_lo_done, KC * nf + 4)
                        else:
                            bank1_free()
                    else:
                        pe.wait_ge(res_done, NSUB * n + j - 1)
                    for k in range(KC):
                        mm = mm3(g_bank[j % 2][:, :], cT_hi[:, k, cols128(j)], cT_lo[:, k, cols128(j)],
                                 wo_hi[:, k, :], wo_lo[:, k, :], k == 0, k == KC - 1)
                    mm.then_inc(o_done, 1)

                def int8_transpose(j):
                    pe.wait_ge(f_z, NSUB * nb + j + 1)
                    if j:
                        pe.wait_ge(f_deq, NSUB * nb + j)
                    bank = g_bank[1][:, 0:D // 2].bitcast(bf16)
                    for k in range(KC):
                        mm = t.transpose(bank[:, cols128(k)], zb[:, cols128(k)], identb[:, :])
                    mm.then_inc(f_zT, 1)

                def int8_product(j):
                    pe.wait_ge(f_zT_evac, NSUB * nb + j + 1)
                    for k in range(KC):
                        mm = t.matmul(g_bank[1][:, :], zT[:, k, :], rq[:, k, :], start=(k == 0), stop=(k == KC - 1))
                    mm.then_inc(f_acc, 1)

                def route_transpose(j):
                    u = NSUB * (i - 1) + j
                    pe.wait_ge(txn_done, NSUB * nb + j + 1)
                    if j:
                        pe.wait_ge(r_log_evac, u)
                    for k in range(KC):
                        mm = t.transpose(g_bank[1][:, cols128(k)], xn[:, j, cols128(k)], ident[:, :])
                    mm.then_inc(r_T, 1)

                def route_logits(j):
                    pe.wait_ge(r_T_evac, NSUB * (i - 1) + j + 1)
                    for k in range(KC):
                        mm = t.matmul(g_bank[1][0:E, 0:P], wsw_sb[:, k, :], xrT[:, k, :],
                                      start=(k == 0), stop=(k == KC - 1))
                    mm.then_inc(r_log, 1)

                def logits_transpose():
                    wait_apart(pe, r_log_evac, NSUB * i)
                    for j in range(NSUB):
                        mm = t.transpose(g_bank[1][:, E * j:E * (j + 1)], logT[:, cols128(j)], ident[0:E, 0:E])
                    mm.then_inc(r_lt, 1)

                def route_counts():
                    pe.wait_ge(r_hot, i)
                    wait(pe, norm_done, KC * (n + 1) if middle else KC * 2 * NSUP)
                    for j in range(NSUB + 1):
                        for k in range(min(j, NSUB - 1) + 1):
                            full_tile = k < j
                            mm = t.matmul(sum_bank[:, E * j:E * (j + 1)], (onesb if full_tile else upto)[:, :],
                                          onehot[:, k, :], start=(k == 0), stop=(k == min(j, NSUB - 1)))
                    mm.then_inc(r_cum, 1)

                for m in range(KC):
                    if middle:
                        scores_cols(m, 0)
                        scores_cols(m, 1)
                    if tail and m:
                        (int8_product, route_logits)[L](m - 1)
                    if middle:
                        scores_cols(m, 2)
                        scores_cols(m, 3)
                    if front:
                        x_transpose(m)
                    if middle and m:
                        weighted(m - 1)
                    if tail:
                        (int8_transpose, route_transpose)[L](m)
                if middle:
                    weighted(KC - 1)
                if tail:
                    (int8_product, route_logits)[L](NSUB - 1)
                if front:
                    project_q(0)
                if tail and L == 1:
                    logits_transpose()
                if front:
                    project_q(1)
                if tail and L == 1:
                    route_counts()
                if front:
                    scores_rows(0)
                    project_q(2)
                    scores_rows(1)
                    project_q(3)
                    scores_rows(2)
                if middle:
                    project_out(0)
                    project_out(1)
                if front:
                    scores_rows(3)
                if middle:
                    project_out(2)
                    project_out(3)
                if front:
                    max_transpose()

            bodies(pe, 0, body)
            bodies(pe, 1, body)

            def rows_transpose(e):
                for r in range(RT):
                    pe.wait_ge(e_xn, RT * e + r + 1)
                    wait(pe, e_T_lo, RT * (e - 1) + r + 1)
                    for k in range(KC):
                        mm = t.transpose(tt_bank[r][:, cols128(k)], tokn[:, r, cols128(k)], ident[:, :])
                    mm.then_inc(e_T, 1)

            def hidden(e, u):
                c = NU * e + u
                pe.wait_ge(w_lo_done, 2 * c + 1)
                if u == 0:
                    pe.wait_ge(e_T_lo, RT * (e + 1))
                for f in range(UC):
                    wait(pe, e_relu, UC * c + f - 1)
                    for k in range(KC):
                        mm = mm3(hb_bank[f % 2][:, 0:CAP], w1_hi[:, u % 2, k, cols128(f)], w1_lo[:, u % 2, k, cols128(f)],
                                 tT_hi[:, k, :], tT_lo[:, k, :], k == 0, k == KC - 1)
                    mm.then_inc(e_h, 1)

            def second(e, u):
                c = NU * e + u
                pe.wait_ge(w_lo_done, 2 * c + 2)
                pe.wait_ge(e_hlo, c + 1)
                if u == 0:
                    wait(pe, e_yb, RT * e)
                for r in range(RT):
                    for f in range(UC):
                        mm = mm3(y_bank[r][:, :], h_hi[:, f, cols128(r)], h_lo[:, f, cols128(r)],
                                 w2_hi[:, u % 2, f, :], w2_lo[:, u % 2, f, :],
                                 u == 0 and f == 0, u == NU - 1 and f == UC - 1)
                mm.then_inc(e_y, 1)

            def expert(e):
                for u in range(NU):
                    hidden(e, u)
                    second(e, u)

            rows_transpose(0)
            expert(0)
            with pe.Fori(1, E) as e:
                rows_transpose(e)
                expert(e)


def kernel(x, ctx_1024, itok_BxS_0_511, L0_xattn_Wq, L0_xattn_Wkv, L0_xattn_Wo, L0_ffn_rhs,
           L1_xattn_in_proj_weight, L1_xattn_in_proj_bias, L1_xattn_out_w, L1_xattn_out_b,
           L1_ffn_w_switch, L1_ffn_b_switch, L1_ffn_w1, L1_ffn_b1, L1_ffn_w2, L1_ffn_b2):
    import concourse.bacc as bacc
    from concourse.bass_utils import run_bass_kernel_spmd

    def lay(a):
        return np.ascontiguousarray(np.asarray(a))

    def chunks(v):
        return lay(np.asarray(v).reshape(-1, P).T)

    bias = np.asarray(L1_xattn_in_proj_bias)
    seg = np.asarray(itok_BxS_0_511).reshape(T)
    arrays = {
        "x": lay(np.asarray(x).reshape(T, D)),
        "ctxT": lay(np.asarray(ctx_1024).reshape(B * KEYS, D).T),
        "segT": chunks(seg), "seg": lay(seg.reshape(1, T)),
        "wq0": lay(np.asarray(L0_xattn_Wq).T), "wkv0": lay(np.asarray(L0_xattn_Wkv).T),
        "wo0": lay(np.asarray(L0_xattn_Wo).T), "rhs": lay(L0_ffn_rhs),
        "wqkv1": lay(np.asarray(L1_xattn_in_proj_weight).T),
        "bq1": chunks(bias[0:D]), "bk1": chunks(bias[D:2 * D]), "bv1": lay(bias[2 * D:].reshape(1, D)),
        "wo1": lay(np.asarray(L1_xattn_out_w).T), "bo1": lay(np.asarray(L1_xattn_out_b).reshape(1, D)),
        "wsw": lay(L1_ffn_w_switch), "bsw": lay(np.asarray(L1_ffn_b_switch).reshape(E, 1)),
        "w1": lay(L1_ffn_w1), "b1": chunks(np.asarray(L1_ffn_b1).reshape(-1)),
        "w2": lay(L1_ffn_w2), "b2": lay(L1_ffn_b2),
    }
    nc = bacc.Bacc("TRN2", target_bir_lowering=False, num_devices=1)
    args = {n: nc.dram_tensor("in_" + n, a.shape, mybir.dt.from_np(a.dtype), kind="ExternalInput").ap()
            for n, a in arrays.items()}
    out = nc.dram_tensor("out", [T, D], mybir.dt.float32, kind="ExternalOutput").ap()
    build(nc, out=out, **args)
    r = run_bass_kernel_spmd(nc, [{"in_" + n: a for n, a in arrays.items()}], core_ids=[0])
    return r.results[0]["out"].reshape(B, S, D)
```

```python
import numpy as np
import concourse.bass as bass
from concourse import mybir
from contextlib import ExitStack

P = 128
B, S, D = 2, 2048, 512
T = B * S
KEYS = 128
H, HD = 16, 32
KC = D // P
HPC = H // KC
SUP = 512
NSUB = SUP // P
NSUP = T // SUP
NSUP_B = NSUP // B
NT = T // P
E, F = 8, 2048
CAP = T // 2 // E
RT = CAP // P
NU, UF = 4, F // 4
UC = UF // P
LOOKBACK = 3
ROW = D + 4
EPS = 1e-5
SCALE = HD ** -0.5
HIDE = -1e30
MAGIC = 1.5 * 2.0 ** 23
NOWHERE = 1 << 20

UNITS = KC * NSUB
ROWS_BUF = 4
LAG = 3
XT_AT = (3, 4, 5, 6)
Q_AT = (8, 10, 13, UNITS)
PV_AT = tuple(NSUB * (m + 1) + LAG for m in range(KC - 1)) + (UNITS,)
TAIL_FROM, TAIL_STEP = (10, 9), (2, 1)


def tail_at(layer, j):
    return TAIL_FROM[layer] + TAIL_STEP[layer] * j




def build(nc, x, ctxT, segT, seg, wq0, wkv0, wo0, rhs, wqkv1, bq1, bk1, bv1, wo1, bo1,
          wsw, bsw, w1, b1, w2, b2, out):
    fp32, bf16, f32r = mybir.dt.float32, mybir.dt.bfloat16, mybir.dt.float32r
    i32, u32 = mybir.dt.int32, mybir.dt.uint32
    ALU, ACT, AX = mybir.AluOpType, mybir.ActivationFunctionType, mybir.AxisListType

    x2_dram = nc.dram_tensor("x2_scratch", [T, D], fp32, kind="Internal").ap()
    slots_dram = nc.dram_tensor("slots_scratch", [E * CAP, ROW], fp32, kind="Internal").ap()
    x_tiles = x.rearrange("(n p) d -> n p d", p=P)
    x2_tiles = x2_dram.rearrange("(n p) d -> n p d", p=P)
    out_tiles = out.rearrange("(n p) d -> n p d", p=P)
    slot_tiles = slots_dram.rearrange("(n p) d -> n p d", p=P)

    ctx = ExitStack()
    with ctx:
        attn = ExitStack()
        ctx.enter_context(attn)

        def keep(name, shape, dt):
            return ctx.enter_context(nc.sbuf_tensor(name, shape, dt))

        def sb(name, shape, dt):
            return attn.enter_context(nc.sbuf_tensor(name, shape, dt))

        def sem(name):
            return ctx.enter_context(nc.semaphore(name))

        ident = keep("ident", [P, P], fp32)
        eps_half = keep("eps_half", [P, 8], fp32)
        moments = keep("moments", [P, NSUB, 6], fp32)
        mean_var = keep("mean_var", [P, NSUB, 2], fp32)
        var_eps = keep("var_eps", [P, NSUB], fp32)
        rstd = keep("rstd", [P, NSUB], fp32)
        b1_sb = keep("b1_sb", [P, E * NU * UC], fp32)

        wq_hi, wq_lo = sb("wq_hi", [P, KC, D], f32r), sb("wq_lo", [P, KC, D], f32r)
        xT_hi, xT_lo = sb("xT_hi", [P, KC, SUP], f32r), sb("xT_lo", [P, KC, SUP], f32r)
        xa = sb("xa", [P, NSUB, D], fp32)
        w_stage = sb("w_stage", [P, KC, D], fp32)
        kd_hi, kd_lo = sb("kd_hi", [P, B, KC, HPC * KEYS], f32r), sb("kd_lo", [P, B, KC, HPC * KEYS], f32r)
        qT_hi, qT_lo = sb("qT_hi", [P, KC, SUP], f32r), sb("qT_lo", [P, KC, SUP], f32r)
        identb = sb("identb", [P, P], bf16)
        wo_hi, wo_lo = sb("wo_hi", [P, KC, D], f32r), sb("wo_lo", [P, KC, D], f32r)
        kT1 = sb("kT1", [P, 2, 2, B * KEYS], fp32)
        v_sb = sb("v_sb", [KEYS, 2, B, D], fp32)
        xb = sb("xb", [P, NSUB, D], fp32)
        prow = sb("prow", [P, ROWS_BUF, HPC * KEYS], fp32)
        probs = sb("probs", [KEYS, 2 * HPC, SUP], fp32)
        cT_hi, cT_lo = sb("cT_hi", [P, KC, SUP], f32r), sb("cT_lo", [P, KC, SUP], f32r)
        neg_max = sb("neg_max", [P, ROWS_BUF, HPC], fp32)
        sums = sb("sums", [P, ROWS_BUF, HPC], fp32)
        totals = sb("totals", [P, ROWS_BUF, HPC], fp32)
        inv = sb("inv", [P, ROWS_BUF, HPC], fp32)
        hideT = sb("hideT", [KEYS, SUP], bf16)
        seg_row = sb("seg_row", [KEYS, SUP], i32)
        seg_f = sb("seg_f", [KEYS, SUP], fp32)
        seg_col = sb("seg_col", [P, NT], i32)
        seg_cf = sb("seg_cf", [P, NT], fp32)
        times = sb("times", [P, NT], fp32)
        more = sb("more", [P, NT], fp32)
        key_num = sb("key_num", [P, 1], fp32)
        xs = sb("xs", [P, NSUB, ROW], fp32)
        xn = sb("xn", [P, NSUB, D], fp32)
        t_moments = sb("t_moments", [P, NSUB, 6], fp32)
        t_mean_var = sb("t_mean_var", [P, NSUB, 2], fp32)
        t_var_eps = sb("t_var_eps", [P, NSUB], fp32)
        t_rstd = sb("t_rstd", [P, NSUB], fp32)
        zb = sb("zb", [P, D], bf16)
        zT = sb("zT", [P, KC, P], bf16)
        rq = sb("rq", [P, KC, D], bf16)
        rscale = sb("rscale", [P, D], fp32)
        amax = sb("amax", [P, NSUB], fp32)
        lscale = sb("lscale", [P, NSUB], fp32)
        linv = sb("linv", [P, NSUB], fp32)
        minus_magic = sb("minus_magic", [P, 1], fp32)
        bq_sb, bk_sb = sb("bq_sb", [P, KC], fp32), sb("bk_sb", [P, KC], fp32)
        bo_sb = rscale
        wsw_sb = sb("wsw_sb", [P, KC, E], fp32)
        bsw_sb = sb("bsw_sb", [E, 1], fp32)
        xrT = rq[:, 0:2, :].rearrange("p a b -> p (a b)").bitcast(fp32).rearrange("p (k t) -> p k t", k=KC)
        logT = rq[0:E, 2:4, :].rearrange("p a b -> p (a b)").bitcast(fp32)
        logits = sb("logits", [P, NSUB, E], fp32)
        top8 = sb("top8", [P, NSUB, 8], fp32)
        top_at = sb("top_at", [P, NSUB, 8], u32)
        route = sb("route", [P, NSUB], fp32)
        expl = sb("expl", [P, NSUB, E], fp32)
        psum_e = sb("psum_e", [P, NSUB], fp32)
        pmax = sb("pmax", [P, NSUB], fp32)
        scale_t = sb("scale_t", [P, NSUB], fp32)
        lane8 = sb("lane8", [P, E], fp32)
        onehot = sb("onehot", [P, NSUB, E], bf16)
        upto = sb("upto", [P, P], bf16)
        onesb = sb("onesb", [P, P], bf16)
        carry = sb("carry", [P, E], fp32)
        place = sb("place", [P, NSUB, E], fp32)
        pos = sb("pos", [P, NSUB], fp32)
        full = sb("full", [P, NSUB], fp32)
        slot_f = sb("slot_f", [P, NSUB], fp32)
        slot = sb("slot", [P, NSUB], u32)
        token_num = sb("token_num", [P, NT], i32)
        wk_stage = (probs[:, 0:4, :], xn[:, :, :])
        wv_stage = (probs[:, 4:8, :], xs[:, :, 0:D])
        bv_sb = prow[:, 0, :]
        kT0 = xb[:, 2:4, :].rearrange("p a (c n) -> p a c n", c=2)
        ctxT_sb = xb[:, 0:2, :].rearrange("p a (c n) -> p (a c) n", c=2)

        kT = (kT0, kT1)

        attn.close()
        moe = ExitStack()
        ctx.enter_context(moe)

        def mb(name, shape, dt):
            return moe.enter_context(nc.sbuf_tensor(name, shape, dt))

        NR = NU
        w1_raw = mb("w1_raw", [P, NR, KC, UF], fp32)
        w2_raw = mb("w2_raw", [P, NR, UC, D], fp32)
        w2_hi, w2_lo = mb("w2_hi", [P, 2, UC, D], f32r), mb("w2_lo", [P, 2, UC, D], f32r)
        tok = mb("tok", [P, RT, ROW], fp32)
        tokn = mb("tokn", [P, RT, D], fp32)
        tT = mb("tT", [P, KC, CAP], fp32)
        hid = mb("hid", [P, 2, UC, CAP], fp32)
        h_hi, h_lo = mb("h_hi", [P, 2, UC, CAP], f32r), mb("h_lo", [P, 2, UC, CAP], f32r)
        b2_sb = mb("b2_sb", [P, D], fp32)
        y_sb = mb("y_sb", [P, RT, D], fp32)
        e_moments = mb("e_moments", [P, RT, 6], fp32)
        e_mean_var = mb("e_mean_var", [P, RT, 2], fp32)
        e_var_eps = mb("e_var_eps", [P, RT], fp32)
        e_rstd = mb("e_rstd", [P, RT], fp32)
        tok_id = mb("tok_id", [P, RT], u32)

        banks = [ctx.enter_context(nc.psum_tensor(f"bank{i}", [P, 512], fp32)) for i in range(8)]
        row_bank, pT_bank = banks[0:2], banks[2:4]
        ctx_bank, tail_bank = banks[4], banks[5]
        x_bank = (ctx_bank, tail_bank)
        counts = tail_bank[:, 2 * NSUB * E:(3 * NSUB + 1) * E]
        g_bank = banks[6:8]
        hb_bank, y_bank, tt_bank = banks[0:2], banks[2:4], banks[4:6]

        ld_w = {n: sem("ld_" + n) for n in
                ("ctx", "wk0", "wv0", "wk1", "wv1", "wq0", "wo0", "wq1", "wo1", "rhs", "small", "bv", "bo")}
        consts_ready, pool_step, dve_step = sem("consts_ready"), sem("pool_step"), sem("dve_step")
        bias_scaled, tail_free = sem("bias_scaled"), sem("tail_free")
        k_done, k_evac, v_done, v_evac = sem("k_done"), sem("k_evac"), sem("v_done"), sem("v_evac")
        kd_hi_done, kd_done = sem("kd_hi_done"), sem("kd_done")
        wq_hi_done, wq_done, wo_hi_done, wo_done = (sem("wq_hi_done"), sem("wq_done"),
                                                    sem("wo_hi_done"), sem("wo_done"))
        met = sem("met")
        dve_consts, empty_row, hide_wide = sem("dve_consts"), sem("empty_row"), sem("hide_wide")
        rhs_amax, rhs_all, rhs_done = sem("rhs_amax"), sem("rhs_all"), sem("rhs_done")
        xa_load = [sem(f"xa_load{j}") for j in range(NSUB)]
        xb_load = [sem(f"xb_load{j}") for j in range(NSUB)]
        xb_biased = sem("xb_biased")
        seg_load, hide_step, hide_done = sem("seg_load"), sem("hide_step"), sem("hide_done")
        stats, aggr, rstd_step, rstd_done, xn_done = (sem("stats"), sem("aggr"), sem("rstd_step"),
                                                      sem("rstd_done"), sem("xn_done"))
        xT_done, xT_hi_done, xT_lo_done = sem("xT_done"), sem("xT_hi_done"), sem("xT_lo_done")
        q_done, q_hi_done, q_lo_done = sem("q_done"), sem("q_hi_done"), sem("q_lo_done")
        rows_done, max_done, exp_done = sem("rows_done"), sem("max_done"), sem("exp_done")
        total_done, inv_done, norm_done = sem("total_done"), sem("inv_done"), sem("norm_done")
        pT_done, pT_evac, pv_done = sem("pT_done"), sem("pT_evac"), sem("pv_done")
        c_hi_done, c_lo_done = sem("c_hi_done"), sem("c_lo_done")
        o_done, res_done = sem("o_done"), sem("res_done")
        t_stats, t_aggr, t_rstd_step, t_rstd_done = (sem("t_stats"), sem("t_aggr"), sem("t_rstd_step"),
                                                     sem("t_rstd_done"))
        txn_done = sem("txn_done")
        f_step, f_round, f_z, f_zT, f_zT_evac, f_acc, f_deq, x2_done = (
            sem("f_step"), sem("f_round"), sem("f_z"), sem("f_zT"), sem("f_zT_evac"),
            sem("f_acc"), sem("f_deq"), sem("x2_done"))
        x2_store = [sem(f"x2_store{j}") for j in range(NSUB)]
        r_T, r_T_evac, r_log, r_log_evac, r_lt, r_lt_evac = (
            sem("r_T"), sem("r_T_evac"), sem("r_log"), sem("r_log_evac"), sem("r_lt"), sem("r_lt_evac"))
        r_step, r_negtop, r_exp, r_hot, r_cum, r_slot, r_plain = (
            sem("r_step"), sem("r_negtop"), sem("r_exp"), sem("r_hot"), sem("r_cum"), sem("r_slot"), sem("r_plain"))
        plain_store, slot_store, xs_free = sem("plain_store"), sem("slot_store"), sem("xs_free")
        w_load = [[sem(f"w{n}_load{r}") for r in range(NR)] for n in (1, 2)]
        w_hi_done, w_lo_done = sem("w_hi_done"), sem("w_lo_done")
        tokn_load, tok_load, b2_load = sem("tokn_load"), sem("tok_load"), sem("b2_load")
        e_stats, e_aggr, e_rstd_step, e_rstd_done, e_xn = (sem("e_stats"), sem("e_aggr"), sem("e_rstd_step"),
                                                      sem("e_rstd"), sem("e_xn"))
        e_T, e_T_evac = sem("e_T"), sem("e_T_evac")
        e_h, e_relu, e_hhi, e_hlo = sem("e_h"), sem("e_relu"), sem("e_hhi"), sem("e_hlo")
        e_y, e_yb, e_yout, e_id, y_store = sem("e_y"), sem("e_yb"), sem("e_yout"), sem("e_id"), sem("y_store")

        SMALL = [(seg_col[:, :], segT), (bq_sb[:, :], bq1), (bk_sb[:, :], bk1),
                 (wsw_sb[:, :, :], wsw.rearrange("(k p) n -> p k n", p=P)), (bsw_sb[:, :], bsw), (b1_sb[:, :], b1)]
        ROUTE_STEPS = 22

        def bodies(engine, L, emit, loads=False):
            if L == 0:
                emit(L, -1, True, False, False, 0)
                emit(L, 0, True, True, False, 0)
            else:
                emit(L, 0, True, True, True, 0)
            with engine.Fori(1, NSUP_B - 1) as i:
                emit(L, i, True, True, True, 0)
            emit(L, NSUP_B - 1, True, True, True, 0)
            with engine.Fori(NSUP_B, NSUP - 1 - loads) as i:
                emit(L, i, True, True, True, 1)
            if loads:
                emit(L, NSUP - 2, True, True, True, 1)
            emit(L, NSUP - 1, L == 0, True, True, 1)
            if L == 1:
                emit(L, NSUP, False, False, True, 1)

        def at(i, value):
            return isinstance(i, int) and i == value

        def layers(L, i):
            return (1 if at(i, NSUP - 1) else L), (0 if at(i, 0) else L)

        X2_FIRST = 16 * E * RT // NSUB
        PLAIN_FIRST = 16
        PLAIN_ALL = PLAIN_FIRST + 16 * NT

        def mm3(out, a_hi, a_lo, b_hi, b_lo, start, stop):
            nc.tensor.matmul(out, a_hi, b_hi, start=start, stop=False)
            nc.tensor.matmul(out, a_hi, b_lo, start=False, stop=False)
            return nc.tensor.matmul(out, a_lo, b_hi, start=False, stop=stop)

        def wait(e, s, v):
            if not isinstance(v, int) or v > 0:
                e.wait_ge(s, v)

        def wait_apart(e, s, v):
            wait(e, s, v)
            e.sem_inc(met, 1)

        def cols128(n):
            return slice(n * P, (n + 1) * P)

        block = ctx.enter_context(nc.Block())


        @block.sync
        def _(sp):
            def load(dst, src, s):
                sp.dma_start(dst, src).then_inc(s, 16)

            def chunked(w):
                return w.rearrange("(k p) n -> p k n", p=P)

            load(ctxT_sb, chunked(ctxT), ld_w["ctx"])
            load(wk_stage[0], chunked(wkv0[:, 0:D]), ld_w["wk0"])
            for dst, src in SMALL:
                load(dst, src, ld_w["small"])
            load(wv_stage[0], chunked(wkv0[:, D:2 * D]), ld_w["wv0"])
            for j in range(NSUB):
                load(xa[:, j, :], x_tiles[j, :, :], xa_load[j])
            load(w_stage[:, :, :], chunked(wq0), ld_w["wq0"])
            load(wk_stage[1], chunked(wqkv1[:, D:2 * D]), ld_w["wk1"])
            load(wv_stage[1], chunked(wqkv1[:, 2 * D:3 * D]), ld_w["wv1"])
            load(bv_sb, bv1.to_broadcast([P, D]), ld_w["bv"])

            w1_u = w1.rearrange("e (k p) (u f) -> e u p k f", p=P, u=NU)
            w2_u = w2.rearrange("e (u c p) d -> e u p c d", p=P, u=NU)

            def rows_load(e):
                wait(sp, e_T, RT * e)
                for r in range(RT):
                    load(tokn[:, r, :], slot_tiles[RT * e + r, :, 0:D], tokn_load)

            def result_loads(e):
                wait(sp, e_yout, RT * e)
                for r in range(RT):
                    load(tok[:, r, :], slot_tiles[RT * e + r, :, :], tok_load)
                load(b2_sb[:, :], b2[bass.ds(e, 1), :].to_broadcast([P, D]), b2_load)

            def w1_load(e, u):
                load(w1_raw[:, u, :, :], w1_u[e, u, :, :, :], w_load[0][u])

            def w2_load(e, u):
                load(w2_raw[:, u, :, :], w2_u[e, u, :, :, :], w_load[1][u])

            def unit_loads(e, u):
                wait(sp, e_h, UC * (NU * (e - 1) + u + 1))
                w1_load(e, u)
                wait(sp, w_lo_done, NU * (e - 1) + u + 1)
                w2_load(e, u)

            def expert(e, more, units=True):
                for u in range(NU):
                    if units:
                        unit_loads(e, u)
                if more:
                    rows_load(e + 1)
                result_loads(e)

            def load_xa(L, i, j):
                wait(sp, xT_done, NSUB * (NSUP * L + i - 1) + j + 1)
                if L == 1:
                    sp.wait_ge(x2_store[j], X2_FIRST + 16 * (i + 1))
                load(xa[:, j, :], (x_tiles, x2_tiles)[L][NSUB * i + j, :, :], xa_load[j])

            def load_xb(L, i, j):
                wait(sp, res_done, NSUB * (NSUP * L + i - 1) + j + 1)
                load(xb[:, j, :], (x_tiles, x2_tiles)[L][NSUB * i + j, :, :], xb_load[j])

            def body(L, i, front, middle, tail, batch):
                FL, TL = layers(L, i)
                if L == 1 and at(i, 0):
                    sp.wait_ge(wq_done, 2)
                    load(w_stage[:, :, :], chunked(wo1), ld_w["wo1"])
                if front and FL == 0:
                    wait(sp, hide_step, 2 * i + 1)
                    load(seg_row[:, :], seg[:, bass.ds((i + 1) * SUP, SUP)].to_broadcast([KEYS, SUP]), seg_load)
                if middle:
                    if L == 0 and at(i, 0):
                        sp.wait_ge(wo_done, 1)
                        load(w_stage[:, :, :], chunked(rhs), ld_w["rhs"])
                        sp.wait_ge(v_done, 2 * B)
                        sp.wait_ge(kd_done, HPC * B)
                    for j in range(NSUB):
                        load_xb(L, i, j)
                if L == 1 and at(i, NSUP - 1):
                    sp.wait_ge(q_done, KC * 2 * NSUP)
                    for u in range(NU // 2):
                        w1_load(0, u)
                        w2_load(0, u)
                    for u in range(NU // 2, NU):
                        w1_load(0, u)
                if L == 1 and at(i, NSUP):
                    sp.wait_ge(rows_done, UNITS * 2 * NSUP)
                    for u in range(NU // 2, NU):
                        w2_load(0, u)
                for j in range(NSUB):
                    if not isinstance(i, int) or i < NSUP - 2:
                        load_xa(L, i + 2, j)
                    elif L == 0:
                        load_xa(1, i + 2 - NSUP, j)
                if at(i, -1):
                    sp.wait_ge(wq_done, 1)
                    load(w_stage[:, :, :], chunked(wo0), ld_w["wo0"])
                if L == 0 and at(i, 0):
                    sp.wait_ge(empty_row, 2)
                    for n in range(E * RT):
                        load(slot_tiles[n, :, :], xs[:, 0, :], x2_store[n % NSUB])
                    sp.wait_ge(rhs_done, 1)
                    load(w_stage[:, :, :], chunked(wqkv1[:, 0:D]), ld_w["wq1"])
                if tail:
                    for j in range(NSUB):
                        if TL == 0:
                            n = NSUB * (NSUP * L + i - 1) + j
                            sp.wait_ge(x2_done, n + 1)
                            load(x2_tiles[n, :, :], xs[:, j, 0:D], x2_store[j])
                        else:
                            n = NSUB * (i - 1) + j
                            sp.wait_ge(r_plain, n + 1)
                            load(out_tiles[n, :, :], xn[:, j, :], plain_store)
                if tail and TL == 1:
                    sp.wait_ge(slot_store, 16 * NSUB * i)
                    sp.sem_inc(xs_free, 1)
                if L == 1 and at(i, 0):
                    for j in range(NSUB):
                        sp.wait_ge(x2_store[j], X2_FIRST + 16 * NSUP)
                    sp.sem_inc(xs_free, 1)
                    sp.wait_ge(f_deq, NT)
                    load(bo_sb[:, :], bo1.to_broadcast([P, D]), ld_w["bo"])
            bodies(sp, 0, body, loads=True)
            bodies(sp, 1, body, loads=True)

            sp.wait_ge(slot_store, 16 * NT)
            sp.wait_ge(plain_store, PLAIN_ALL)
            rows_load(0)
            expert(0, True, units=False)
            with sp.Fori(1, E - 1) as e:
                expert(e, True)
            expert(E - 1, False)

        @block.gpsimd
        def _(pool):
            g = nc.gpsimd
            steps = [0]

            def step(ins):
                steps[0] += 1
                ins.then_inc(pool_step, 1)
                pool.wait_ge(pool_step, steps[0])

            step(g.memset(ident[:, :], 0.0))
            g.affine_select(out=ident[:, :], in_=ident[:, :], compare_op=ALU.not_equal, fill=1.0,
                            base=0, pattern=[[-1, P]], channel_multiplier=1).then_inc(consts_ready, 1)
            g.memset(kd_hi[:, :, :, :].bitcast(fp32), 0.0).then_inc(consts_ready, 1)
            g.memset(eps_half[:, :], -0.5)
            g.memset(minus_magic[:, :], -MAGIC)
            g.memset(carry[:, :], 0.0)
            g.memset(onesb[:, :], 1.0)
            step(g.memset(upto[:, :], 1.0))
            g.affine_select(out=upto[:, :], in_=upto[:, :], compare_op=ALU.is_ge, fill=0.0,
                            base=0, pattern=[[1, P]], channel_multiplier=-1)
            g.iota(key_num[:, :], pattern=[[0, 1]], base=0, channel_multiplier=1,
                   allow_small_or_imprecise_dtypes=True)
            g.iota(lane8[:, :], pattern=[[1, E]], base=0, channel_multiplier=0,
                   allow_small_or_imprecise_dtypes=True)
            g.iota(token_num[:, :], pattern=[[P, NT]], base=0, channel_multiplier=1).then_inc(consts_ready, 1)
            g.memset(xs[:, 1:NSUB, D:ROW], 0.0)
            def inverse_root(ve, mv, r, ready, count, mid, mid_count, done):
                wait_apart(pool, ready, count)
                g.tensor_scalar(ve[:, :], mv[:, :, 1], EPS, 0.0, ALU.add, ALU.add).then_inc(mid, 1)
                pool.wait_ge(mid, mid_count)
                n = ve.shape[1]
                g.tensor_tensor(r[:, :], ve[:, :], eps_half[:, 0:n], ALU.pow).then_inc(done, 1)

            def empty_slot():
                pool.wait_ge(v_done, 2 * B)
                step(g.memset(xs[:, 0, :], 0.0))
                g.iota(xs[:, 0, D:D + 1].bitcast(i32), pattern=[[0, 1]], base=NOWHERE,
                       channel_multiplier=0).then_inc(empty_row, 2)

            def body(L, i, front, middle, tail, batch):
                n, nf, nb = NSUP * L + i, NSUP * L + i + 1, NSUP * L + i - 1
                FL, TL = layers(L, i)
                if L == 0 and at(i, 0):
                    empty_slot()

                def bias_xb(j):
                    pool.wait_ge(xb_load[j], 16 * (nb + 1))
                    g.tensor_tensor(xb[:, j, :], xb[:, j, :], bo_sb[:, :], ALU.add).then_inc(xb_biased, 1)

                def normalise(u):
                    pool.wait_ge(inv_done, UNITS * n + u + 1)
                    pu = prow[:, u % ROWS_BUF, :].rearrange("p (g k) -> p g k", g=HPC)
                    g.tensor_tensor(pu, pu, inv[:, u % ROWS_BUF, :].unsqueeze(2).to_broadcast([P, HPC, KEYS]),
                                    ALU.mult).then_inc(norm_done, 1)

                for u in range(UNITS + 1):
                    if tail and TL == 1 and u < NSUB:
                        bias_xb(u)
                    if middle and u:
                        normalise(u - 1)
                    if L == 0 and at(i, 0) and u == 9:
                        pool.wait_ge(rhs_amax, 1)
                        g.partition_all_reduce(rscale[:, :], xn[:, 0, :], P,
                                               bass.bass_isa.ReduceOp.absmax).then_inc(rhs_all, 1)
                    if front and u == 1:
                        inverse_root(var_eps, mean_var, rstd, aggr, NSUB * (nf + 1), rstd_step, nf + 1, rstd_done)
                    if tail and u == 6:
                        inverse_root(t_var_eps, t_mean_var, t_rstd, t_aggr, NSUB * (nb + 1), t_rstd_step, nb + 1,
                                     t_rstd_done)
                    for j in range(NSUB):
                        if tail and TL == 0 and u == min(tail_at(0, j) + 2, UNITS):
                            pool.wait_ge(f_deq, NSUB * nb + j + 1)
                            g.tensor_tensor(xs[:, j, 0:D], xs[:, j, 0:D], xn[:, j, :], ALU.add).then_inc(x2_done, 1)
                if tail and TL == 1:
                    wait_apart(pool, r_slot, i)
                    for j in range(NSUB):
                        pool.indirect_dma_start(
                            slots_dram, bass.IndirectOffsetOnAxis(ap=slot[:, j:j + 1], axis=0),
                            xs[:, j, :], None, bounds_check=E * CAP - 1, oob_is_err=False).then_inc(slot_store, 16)
                if L == 1 and at(i, 0):
                    pool.wait_ge(ld_w["bo"], 16)
                    for j in range(NSUB):
                        pool.wait_ge(x2_store[j], X2_FIRST)
            bodies(pool, 0, body)
            bodies(pool, 1, body)

            def roots(e):
                inverse_root(e_var_eps, e_mean_var, e_rstd, e_aggr, RT * (e + 1), e_rstd_step, e + 1, e_rstd_done)

            def scatter(e):
                for r in range(RT):
                    wait_apart(pool, e_yout, RT * e + r + 1)
                    pool.indirect_dma_start(
                        out, bass.IndirectOffsetOnAxis(ap=tok_id[:, r:r + 1], axis=0),
                        y_sb[:, r, :], None, bounds_check=T - 1, oob_is_err=False).then_inc(y_store, 16)
            roots(0)
            pool.wait_ge(plain_store, PLAIN_ALL)
            with pool.Fori(0, E - 1) as e:
                roots(e + 1)
                scatter(e)
            scatter(E - 1)
            pool.wait_ge(y_store, 16 * E * RT)

        @block.scalar
        def _(act):
            a = nc.scalar

            def k_copy(L):
                for m in range(KC):
                    act.wait_ge(k_done, KC * L + m + 1)
                    bank = g_bank[m % 2][:, 0:B * KEYS]
                    if L == 0:
                        a.activation(kT[L][:, m // 2, m % 2, :], bank, ACT.Copy).then_inc(k_evac, 1)
                    else:
                        a.activation(kT[L][:, m // 2, m % 2, :], bank, ACT.Identity, bias=bk_sb[:, m:m + 1]).then_inc(k_evac, 1)

            def k_high(L, b):
                act.wait_ge(k_evac, KC * (L + 1))
                if L == 0:
                    act.wait_ge(consts_ready, 2)
                else:
                    act.wait_ge(rows_done, UNITS * NSUP_B * (b + 1))
                for g in range(HPC):
                    rows = slice(HD * g, HD * (g + 1))
                    a.activation(kd_hi[rows, b, :, cols128(g)].rearrange("p (a c) n -> p a c n", c=2),
                                 kT[L][rows, :, :, b * KEYS:(b + 1) * KEYS],
                                 ACT.Copy).then_inc(kd_hi_done, 1)

            act.wait_ge(ld_w["small"], 16 * len(SMALL))
            k_copy(0)
            k_high(0, 0)
            act.wait_ge(ld_w["wq0"], 16)
            a.activation(wq_hi[:, :, :], w_stage[:, :, :], ACT.Copy, scale=SCALE).then_inc(wq_hi_done, 1)
            k_high(0, 1)
            k_copy(1)

            act.wait_ge(bias_scaled, 1)

            def body(L, i, front, middle, tail, batch):
                n, nf, nb = NSUP * L + i, NSUP * L + i + 1, NSUP * L + i - 1
                FL, TL = layers(L, i)

                def exps(u):
                    act.wait_ge(max_done, UNITS * n + u + 1)
                    wait(act, pT_done, UNITS * n + u + 1 - ROWS_BUF)
                    for g in range(HPC):
                        e = a.activation(prow[:, u % ROWS_BUF, cols128(g)], row_bank[u % 2][:, cols128(g)], ACT.Exp,
                                         bias=neg_max[:, u % ROWS_BUF, g:g + 1],
                                         accum_out=sums[:, u % ROWS_BUF, g:g + 1])
                    e.then_inc(exp_done, 1)

                def probs_copy(u):
                    m, j = divmod(u, NSUB)
                    act.wait_ge(pT_done, UNITS * n + u + 1)
                    if j == 0:
                        wait(act, pv_done, KC * n + m - 1)
                    a.activation(probs[:, HPC * (m % 2):HPC * (m % 2 + 1), cols128(j)],
                                 pT_bank[u % 2][:, :].rearrange("p (g t) -> p g t", g=HPC),
                                 ACT.Copy).then_inc(pT_evac, 1)

                def x_high(j):
                    act.wait_ge(xT_done, NSUB * nf + j + 1)
                    wait(act, q_done, KC * nf)
                    a.activation(xT_hi[:, :, cols128(j)], x_bank[j % 2][:, :].rearrange("p (k t) -> p k t", k=KC),
                                 ACT.Copy).then_inc(xT_hi_done, 1)

                def q_high(m):
                    act.wait_ge(q_done, KC * nf + m + 1)
                    if FL == 0:
                        a.activation(qT_hi[:, m, :], g_bank[m % 2][:, :], ACT.Copy).then_inc(q_hi_done, 1)
                    else:
                        a.activation(qT_hi[:, m, :], g_bank[m % 2][:, :], ACT.Identity,
                                     bias=bq_sb[:, m:m + 1]).then_inc(q_hi_done, 1)

                def c_high(m):
                    act.wait_ge(pv_done, KC * n + m + 1)
                    wait(act, o_done, NSUB * n)
                    a.activation(cT_hi[:, m, :], ctx_bank[:, :], ACT.Copy).then_inc(c_hi_done, 1)

                def integers(j):
                    act.wait_ge(f_round, NSUB * nb + j + 1)
                    a.activation(zb[:, :], xn[:, j, :], ACT.Identity, bias=minus_magic[:, 0:1]).then_inc(f_z, 1)

                def integers_copy(j):
                    act.wait_ge(f_zT, NSUB * nb + j + 1)
                    a.activation(zT[:, :, :], tail_bank[:, 0:D // 2].bitcast(bf16).rearrange("p (k t) -> p k t", k=KC),
                                 ACT.Copy).then_inc(f_zT_evac, 1)

                def route_copy(j):
                    act.wait_ge(r_T, NSUB * (i - 1) + j + 1)
                    a.activation(xrT[:, :, :], tail_bank[:, :].rearrange("p (k t) -> p k t", k=KC),
                                 ACT.Copy).then_inc(r_T_evac, 1)

                def logits_bias(j):
                    act.wait_ge(r_log, NSUB * (i - 1) + j + 1)
                    a.activation(logT[:, cols128(j)], tail_bank[0:E, 0:P], ACT.Identity,
                                 bias=bsw_sb[:, 0:1]).then_inc(r_log_evac, 1)

                for u in range(UNITS + 1):
                    for j in range(NSUB):
                        if front and u == XT_AT[j] + 1:
                            x_high(j)
                    for m in range(KC - 1):
                        if front and u == Q_AT[m] + 1:
                            q_high(m)
                    for j in range(NSUB):
                        if tail and u == tail_at(TL, j) + 1:
                            (integers_copy, route_copy)[TL](j)
                    for m in range(KC - 1):
                        if middle and u == PV_AT[m] + 1:
                            c_high(m)
                    if middle and u >= LAG:
                        probs_copy(u - LAG)
                    for j in range(NSUB):
                        if tail and TL == 1 and u == tail_at(1, j) + 1:
                            logits_bias(j)
                    if middle and u < UNITS:
                        exps(u)
                    for j in range(NSUB):
                        if tail and TL == 0 and u == tail_at(0, j) - 1:
                            integers(j)
                    if tail and TL == 1 and u == 14:
                        act.wait_ge(r_negtop, i)
                        a.activation(expl[:, :, :], expl[:, :, :], ACT.Exp).then_inc(r_exp, 1)
                    if L == 0 and at(i, 0) and u == 1:
                        act.wait_ge(ld_w["wo0"], 16)
                        a.activation(wo_hi[:, :, :], w_stage[:, :, :], ACT.Copy).then_inc(wo_hi_done, 1)
                    if L == 0 and at(i, NSUP - 1) and u == 0:
                        act.wait_ge(ld_w["wq1"], 16)
                        act.wait_ge(q_done, KC * NSUP)
                        a.activation(wq_hi[:, :, :], w_stage[:, :, :], ACT.Copy, scale=SCALE).then_inc(wq_hi_done, 1)
                    if L == 0 and at(i, NSUP - 1) and u == 3:
                        k_high(1, 0)
                    if L == 1 and at(i, 0) and u == 3:
                        k_high(1, 1)
                    if L == 1 and at(i, 0) and u == 6:
                        act.wait_ge(ld_w["wo1"], 16)
                        act.wait_ge(o_done, NSUB * NSUP)
                        a.activation(wo_hi[:, :, :], w_stage[:, :, :], ACT.Copy).then_inc(wo_hi_done, 1)
                if tail and TL == 0:
                    integers_copy(NSUB - 1)
                if middle:
                    probs_copy(UNITS - 2)
                if front:
                    q_high(KC - 1)
                if middle:
                    probs_copy(UNITS - 1)
                    c_high(KC - 1)
            bodies(act, 0, body)
            bodies(act, 1, body)

            def split_high(e, u):
                c = NU * e + u
                act.wait_ge(w_load[1][u], 16 * (e + 1))
                wait(act, e_y, c - 1)
                a.activation(w2_hi[:, u % 2, :, :], w2_raw[:, u, :, :], ACT.Copy).then_inc(w_hi_done, 1)

            def hidden(e, u):
                c = NU * e + u
                for f in range(UC):
                    act.wait_ge(e_h, UC * c + f + 1)
                    if f == 0:
                        wait(act, e_hlo, c - 1)
                    a.activation(hid[:, u % 2, f, :], hb_bank[f % 2][:, 0:CAP], ACT.Relu,
                                 bias=b1_sb[:, bass.ds(c * UC + f, 1)]).then_inc(e_relu, 1)
                act.wait_ge(e_relu, UC * (c + 1))
                wait(act, e_y, c - 1)
                a.activation(h_hi[:, u % 2, :, :], hid[:, u % 2, :, :], ACT.Copy).then_inc(e_hhi, 1)

            def rows_copy(e):
                for r in range(RT):
                    act.wait_ge(e_T, RT * e + r + 1)
                    a.activation(tT[:, :, cols128(r)], tt_bank[r][:, :].rearrange("p (k t) -> p k t", k=KC),
                                 ACT.Copy).then_inc(e_T_evac, 1)

            act.wait_ge(rows_done, UNITS * 2 * NSUP)
            split_high(0, 0)
            act.wait_ge(plain_store, PLAIN_ALL)
            act.wait_ge(slot_store, 16 * NT)
            rows_copy(0)

            def expert(e, more):
                for u in range(NU):
                    hidden(e, u)
                    if u < NU - 1:
                        split_high(e, u + 1)
                    elif more:
                        rows_copy(e + 1)
                        split_high(e + 1, 0)
            expert(0, True)
            with act.Fori(1, E - 1) as e:
                expert(e, True)
            expert(E - 1, False)

        @block.vector
        def _(dve):
            v = nc.vector
            steps = [0]

            def step(ins):
                steps[0] += 1
                ins.then_inc(dve_step, 1)
                dve.wait_ge(dve_step, steps[0])

            def v_copy(L):
                for b in range(B):
                    dve.wait_ge(v_done, B * L + b + 1)
                    if L == 0:
                        v.tensor_copy(v_sb[:, L, b, :], row_bank[b][:, :]).then_inc(v_evac, 1)
                    else:
                        v.tensor_tensor(v_sb[:, L, b, :], row_bank[b][:, :], bv_sb, ALU.add).then_inc(v_evac, 1)

            def k_low(L, b):
                for g in range(HPC):
                    rows = slice(HD * g, HD * (g + 1))
                    dve.wait_ge(kd_hi_done, HPC * (B * L + b) + g + 1)
                    v.tensor_tensor(kd_lo[rows, b, :, cols128(g)].rearrange("p (a c) n -> p a c n", c=2),
                                    kT[L][rows, :, :, b * KEYS:(b + 1) * KEYS],
                                    kd_hi[rows, b, :, cols128(g)].bitcast(fp32).rearrange("p (a c) n -> p a c n", c=2),
                                    ALU.subtract).then_inc(kd_done, 1)

            v.memset(kd_lo[:, :, :, :].bitcast(fp32), 0.0).then_inc(dve_step, 1)
            steps[0] += 1
            dve.wait_ge(consts_ready, 3)
            v.tensor_copy(identb[:, :], ident[:, :]).then_inc(dve_consts, 1)
            dve.wait_ge(dve_step, steps[0])
            k_low(0, 0)
            dve.wait_ge(wq_hi_done, 1)
            v.scalar_tensor_tensor(wq_lo[:, :, :], w_stage[:, :, :], SCALE, wq_hi[:, :, :].bitcast(fp32),
                                   ALU.mult, ALU.subtract).then_inc(wq_done, 1)
            v_copy(0)
            k_low(0, 1)
            dve.wait_ge(ld_w["small"], 16 * len(SMALL))
            v.tensor_scalar(bq_sb[:, :], bq_sb[:, :], SCALE, 0.0, ALU.mult, ALU.add).then_inc(bias_scaled, 1)
            step(v.tensor_copy(seg_cf[:, :], seg_col[:, :]))
            step(v.tensor_scalar(times[:, :], seg_cf[:, :], float(KEYS - 2), 1.0, ALU.subtract, ALU.max))
            step(v.tensor_scalar(times[:, :], times[:, :], float(LOOKBACK + 1), 0.0, ALU.min, ALU.add))
            step(v.tensor_scalar(more[:, :], times[:, :], -1.0, 0.0, ALU.add, ALU.add))

            def rhs_maxima():
                dve.wait_ge(ld_w["rhs"], 16)
                v.tensor_reduce(xn[:, 0, :], w_stage[:, :, :].rearrange("p k n -> p n k"), AX.X, ALU.max,
                                apply_absolute_value=True).then_inc(rhs_amax, 1)

            def rhs_scale():
                dve.wait_ge(rhs_all, 1)
                step(v.tensor_scalar(rscale[:, :], rscale[:, :], 1e-12, float(np.float32(1) / np.float32(127)),
                                     ALU.max, ALU.mult))
                step(v.reciprocal(xn[:, 1, :], rscale[:, :]))

            def rhs_quantise(k):
                step(v.tensor_tensor(xn[:, 0, :], w_stage[:, k, :], xn[:, 1, :], ALU.mult))
                step(v.tensor_scalar(xn[:, 0, :], xn[:, 0, :], 127.0, -127.0, ALU.min, ALU.max))
                step(v.tensor_scalar(rq[:, k, :], xn[:, 0, :], MAGIC, MAGIC, ALU.add, ALU.subtract))

            def moments_means(n_rows, mom, mv, s1, s2, n):
                for j in range(n_rows):
                    wait_apart(dve, s1, n_rows * n + j + 1)
                    v.bn_aggr(mv[:, j, :], mom[:, j, :]).then_inc(s2, 1)

            def body(L, i, front, middle, tail, batch):
                n, nf, nb = NSUP * L + i, NSUP * L + i + 1, NSUP * L + i - 1
                FL, TL = layers(L, i)

                def row_max(u):
                    dve.wait_ge(rows_done, UNITS * n + u + 1)
                    v.tensor_reduce(neg_max[:, u % ROWS_BUF, :],
                                    row_bank[u % 2][:, :].rearrange("p (g k) -> p g k", g=HPC), AX.X, ALU.max,
                                    negate=True).then_inc(max_done, 1)

                def row_sums(u):
                    b = u % ROWS_BUF
                    dve.wait_ge(exp_done, UNITS * n + u + 1)
                    if L == 0:
                        at_last = prow[:, b, :].rearrange("p (g k) -> p g k", g=HPC)[:, :, KEYS - 1]
                        tile = bass.ds(i * NSUB + u % NSUB, 1)
                        v.scalar_tensor_tensor(totals[:, b, :], at_last, more[:, tile], sums[:, b, :],
                                               ALU.mult, ALU.add).then_inc(total_done, 1)
                        v.tensor_scalar(at_last, at_last, times[:, tile], 0.0, ALU.mult, ALU.add)
                        dve.wait_ge(total_done, UNITS * i + u + 1)
                        v.reciprocal(inv[:, b, :], totals[:, b, :]).then_inc(inv_done, 1)
                    else:
                        v.reciprocal(inv[:, b, :], sums[:, b, :]).then_inc(inv_done, 1)

                def normalise(j):
                    if j == 0:
                        dve.wait_ge(rstd_done, nf + 1)
                    v.tensor_scalar(xa[:, j, :], xa[:, j, :], mean_var[:, j, 0:1], rstd[:, j:j + 1],
                                    ALU.subtract, ALU.mult).then_inc(xn_done, 1)

                def x_low(j):
                    dve.wait_ge(xT_hi_done, NSUB * nf + j + 1)
                    v.tensor_tensor(xT_lo[:, :, cols128(j)], x_bank[j % 2][:, :].rearrange("p (k t) -> p k t", k=KC),
                                    xT_hi[:, :, cols128(j)].bitcast(fp32), ALU.subtract).then_inc(xT_lo_done, 1)

                def c_low(m):
                    dve.wait_ge(c_hi_done, KC * n + m + 1)
                    v.tensor_tensor(cT_lo[:, m, :], ctx_bank[:, :], cT_hi[:, m, :].bitcast(fp32),
                                    ALU.subtract).then_inc(c_lo_done, 1)

                def tail_norm(j):
                    if j == 0:
                        dve.wait_ge(t_rstd_done, nb + 1)
                        if TL == 1:
                            dve.wait_ge(plain_store, PLAIN_FIRST + 16 * NSUB * (i - 1))
                    v.tensor_scalar(xn[:, j, :], xs[:, j, 0:D], t_mean_var[:, j, 0:1], t_rstd[:, j:j + 1],
                                    ALU.subtract, ALU.mult).then_inc(txn_done, 1)

                def token_scale(j):
                    c = 4 * (NSUB * nb + j)
                    dve.wait_ge(txn_done, NSUB * nb + j + 1)
                    v.tensor_reduce(amax[:, j:j + 1], xn[:, j, :], AX.X, ALU.max,
                                    apply_absolute_value=True).then_inc(f_step, 1)
                    dve.wait_ge(f_step, c + 1)
                    v.tensor_scalar(lscale[:, j:j + 1], amax[:, j:j + 1], 1e-12,
                                    float(np.float32(1) / np.float32(127)), ALU.max, ALU.mult).then_inc(f_step, 1)
                    dve.wait_ge(f_step, c + 2)
                    v.reciprocal(linv[:, j:j + 1], lscale[:, j:j + 1]).then_inc(f_step, 1)

                def quantise(j):
                    c = 4 * (NSUB * nb + j)
                    dve.wait_ge(f_step, c + 3)
                    v.tensor_scalar(xn[:, j, :], xn[:, j, :], linv[:, j:j + 1], -127.0,
                                    ALU.mult, ALU.max).then_inc(f_step, 1)
                    dve.wait_ge(f_step, c + 4)
                    v.tensor_scalar(xn[:, j, :], xn[:, j, :], 127.0, MAGIC, ALU.min, ALU.add).then_inc(f_round, 1)

                def dequantise(j):
                    dve.wait_ge(f_acc, NSUB * nb + j + 1)
                    v.scalar_tensor_tensor(xn[:, j, :], tail_bank[:, :], lscale[:, j:j + 1], rscale[:, :],
                                           ALU.mult, ALU.mult).then_inc(f_deq, 1)

                count = [0]

                def link(ins):
                    count[0] += 1
                    ins.then_inc(r_step, 1)
                    dve.wait_ge(r_step, ROUTE_STEPS * (i - 1) + count[0])

                def mark(ins):
                    count[0] += 1
                    ins.then_inc(r_step, 1)

                def choose():
                    dve.wait_ge(r_lt, i)
                    v.tensor_copy(logits[:, :, :], tail_bank[:, 0:NSUB * E].rearrange("p (j e) -> p j e", e=E))\
                        .then_inc(r_lt_evac, 1)
                    wait_apart(dve, r_lt_evac, i)
                    for j in range(NSUB):
                        mark(v.max(top8[:, j, :], logits[:, j, :]))
                    dve.wait_ge(r_step, ROUTE_STEPS * (i - 1) + count[0])
                    v.tensor_tensor(expl[:, :, :], logits[:, :, :],
                                    top8[:, :, 0:1].to_broadcast([P, NSUB, E]), ALU.subtract).then_inc(r_negtop, 1)
                    for j in range(NSUB):
                        mark(v.max_index(top_at[:, j, :], top8[:, j, :], logits[:, j, :]))
                    dve.wait_ge(r_step, ROUTE_STEPS * (i - 1) + count[0])
                    link(v.tensor_copy(route[:, :], top_at[:, :, 0]))
                    v.tensor_tensor(onehot[:, :, :], lane8[:, :].unsqueeze(1).to_broadcast([P, NSUB, E]),
                                    route[:, :].unsqueeze(2).to_broadcast([P, NSUB, E]), ALU.is_equal)\
                        .then_inc(r_hot, 1)

                def place_tokens():
                    dve.wait_ge(r_exp, i)
                    link(v.tensor_reduce(psum_e[:, :], expl[:, :, :], AX.X, ALU.add))
                    link(v.reciprocal(pmax[:, :], psum_e[:, :]))
                    link(v.reciprocal(psum_e[:, :], pmax[:, :]))
                    link(v.tensor_tensor(scale_t[:, :], pmax[:, :], psum_e[:, :], ALU.mult))
                    dve.wait_ge(r_cum, i)
                    link(v.tensor_tensor(place[:, :, :], counts[:, 0:NSUB * E].rearrange("p (j e) -> p j e", e=E),
                                         carry[:, :].unsqueeze(1).to_broadcast([P, NSUB, E]), ALU.add))
                    link(v.tensor_tensor(carry[:, :], counts[:, NSUB * E:(NSUB + 1) * E], carry[:, :], ALU.add))
                    dve.sem_inc(tail_free, 1)
                    link(v.tensor_tensor(place[:, :, :], place[:, :, :], onehot[:, :, :], ALU.mult))
                    link(v.tensor_reduce(pos[:, :], place[:, :, :], AX.X, ALU.add))
                    mark(v.tensor_scalar(full[:, :], pos[:, :], CAP + 0.5, float(NOWHERE), ALU.is_gt, ALU.mult))
                    link(v.scalar_tensor_tensor(slot_f[:, :], route[:, :], float(CAP), pos[:, :], ALU.mult, ALU.add))
                    link(v.tensor_tensor(slot_f[:, :], slot_f[:, :], full[:, :], ALU.add))
                    mark(v.tensor_copy(xs[:, :, D + 1], scale_t[:, :]))
                    mark(v.tensor_copy(xs[:, :, D].bitcast(i32), token_num[:, bass.ds((i - 1) * NSUB, NSUB)]))
                    v.tensor_scalar(slot[:, :], slot_f[:, :], -1.0, 0.0, ALU.add, ALU.add).then_inc(r_slot, 1)
                    assert count[0] == ROUTE_STEPS

                def plain(j):
                    v.scalar_tensor_tensor(xn[:, j, :], xn[:, j, :], scale_t[:, j:j + 1], xs[:, j, 0:D],
                                           ALU.mult, ALU.add).then_inc(r_plain, 1)

                def window_ends():
                    dve.wait_ge(seg_load, 16 * (i + 2))
                    v.tensor_scalar(seg_f[:, :], seg_row[:, :], 0.0, float(KEYS - 1 + LOOKBACK),
                                    ALU.max, ALU.min).then_inc(hide_step, 1)
                    dve.wait_ge(hide_step, 2 * (i + 1) + 1)
                    v.tensor_scalar(seg_f[:, :], seg_f[:, :], key_num[:, 0:1], LOOKBACK / 2,
                                    ALU.subtract, ALU.subtract).then_inc(hide_step, 1)

                def distances():
                    dve.wait_ge(hide_step, 2 * (i + 2))
                    v.tensor_tensor(seg_f[:, :], seg_f[:, :], seg_f[:, :], ALU.mult).then_inc(hide_wide, 1)

                def hide():
                    dve.wait_ge(hide_wide, i + 2)
                    wait(dve, rows_done, UNITS * (i + 1))
                    v.tensor_scalar(hideT[:, :], seg_f[:, :], (LOOKBACK / 2 + 0.1) ** 2, HIDE,
                                    ALU.is_gt, ALU.mult).then_inc(hide_done, 1)

                def q_low(m):
                    dve.wait_ge(q_hi_done, KC * nf + m + 1)
                    if FL == 0:
                        v.tensor_tensor(qT_lo[:, m, :], g_bank[m % 2][:, :], qT_hi[:, m, :].bitcast(fp32),
                                        ALU.subtract).then_inc(q_lo_done, 1)
                    else:
                        v.scalar_tensor_tensor(qT_lo[:, m, :], g_bank[m % 2][:, :], bq_sb[:, m:m + 1],
                                               qT_hi[:, m, :].bitcast(fp32), ALU.add, ALU.subtract)\
                            .then_inc(q_lo_done, 1)

                def residual(j):
                    dve.wait_ge(o_done, NSUB * nb + j + 1)
                    if TL == 0:
                        dve.wait_ge(xb_load[j], 16 * (nb + 1))
                        dve.wait_ge(x2_store[j], X2_FIRST + 16 * nb)
                    else:
                        dve.wait_ge(xb_biased, NSUB * (i - 1) + j + 1)
                        dve.wait_ge(xs_free, i)
                    v.tensor_tensor(xs[:, j, 0:D], g_bank[j % 2][:, :], xb[:, j, :], ALU.add).then_inc(res_done, 1)

                for u in range(UNITS + 1):
                    if middle and u < UNITS:
                        row_max(u)
                    if front and FL == 0 and u == UNITS - 1:
                        hide()
                    if middle and u:
                        row_sums(u - 1)
                    for j in range(NSUB):
                        if front and u == XT_AT[j] + 1:
                            x_low(j)
                    for j in range(NSUB):
                        if front and u == (2, 2, 3, 4)[j]:
                            normalise(j)
                    if tail and 1 <= u <= NSUB:
                        residual(u - 1)
                    if front and u == 0:
                        for j in range(NSUB):
                            dve.wait_ge(xa_load[j], 16 * (nf + 1))
                            v.bn_stats(moments[:, j, :], xa[:, j, :]).then_inc(stats, 1)
                        moments_means(NSUB, moments, mean_var, stats, aggr, nf)
                    if tail and 2 <= u < 2 + NSUB:
                        j = u - 2
                        dve.wait_ge(res_done, NSUB * nb + j + 1)
                        v.bn_stats(t_moments[:, j, :], xs[:, j, 0:D]).then_inc(t_stats, 1)
                    if tail and u == 1 + NSUB:
                        moments_means(NSUB, t_moments, t_mean_var, t_stats, t_aggr, nb)
                    if front and FL == 0 and u == 1:
                        window_ends()
                    if front and FL == 0 and u == 6:
                        distances()
                    for m in range(KC):
                        if middle and m < KC - 1 and u == PV_AT[m] + 1:
                            c_low(m)
                        if front and m < KC - 1 and u == Q_AT[m] + 1:
                            q_low(m)
                    for j in range(NSUB):
                        if tail and TL == 0 and u == tail_at(0, j) + 1:
                            dequantise(j)
                        if tail and u == NSUB + 3 + TAIL_STEP[TL] * j:
                            tail_norm(j)
                            if TL == 0:
                                token_scale(j)
                        if tail and TL == 0 and u == NSUB + 4 + TAIL_STEP[0] * j:
                            quantise(j)
                    if tail and TL == 1 and u == 14:
                        choose()
                    if tail and TL == 1 and u == 16:
                        place_tokens()
                    if at(i, -1) and u == 3:
                        dve.wait_ge(ld_w["bv"], 16)
                        v_copy(1)
                    if L == 0 and at(i, 0):
                        if u == 2:
                            dve.wait_ge(wo_hi_done, 1)
                            v.tensor_tensor(wo_lo[:, :, :], w_stage[:, :, :], wo_hi[:, :, :].bitcast(fp32),
                                            ALU.subtract).then_inc(wo_done, 1)
                        elif u == 7:
                            rhs_maxima()
                        elif u == 12:
                            rhs_scale()
                        elif u > UNITS - KC:
                            rhs_quantise(u - UNITS + KC - 1)
                            if u == UNITS:
                                dve.sem_inc(rhs_done, 1)
                    if L == 0 and at(i, NSUP - 1) and u == 0:
                        dve.wait_ge(wq_hi_done, 2)
                        v.scalar_tensor_tensor(wq_lo[:, :, :], w_stage[:, :, :], SCALE, wq_hi[:, :, :].bitcast(fp32),
                                               ALU.mult, ALU.subtract).then_inc(wq_done, 1)
                    if L == 0 and at(i, NSUP - 1) and u == 4:
                        k_low(1, 0)
                    if L == 1 and at(i, 0) and u == 4:
                        k_low(1, 1)
                    if L == 1 and at(i, 0) and u == 7:
                        dve.wait_ge(wo_hi_done, 2)
                        v.tensor_tensor(wo_lo[:, :, :], w_stage[:, :, :], wo_hi[:, :, :].bitcast(fp32),
                                        ALU.subtract).then_inc(wo_done, 1)
                if front:
                    q_low(KC - 1)
                if tail and TL == 0:
                    dequantise(NSUB - 1)
                if middle:
                    c_low(KC - 1)
                if tail and TL == 1:
                    for j in range(NSUB):
                        plain(j)
                if L == 0 and at(i, 0):
                    for j in range(NSUB):
                        dve.wait_ge(x2_store[j], X2_FIRST)
                if L == 1 and at(i, 0):
                    dve.wait_ge(f_deq, NT)
                    dve.sem_inc(tail_free, 1)
                    dve.sem_inc(plain_store, PLAIN_FIRST)

            bodies(dve, 0, body)
            bodies(dve, 1, body)

            def split_low(e, u):
                dve.wait_ge(w_hi_done, NU * e + u + 1)
                v.tensor_tensor(w2_lo[:, u % 2, :, :], w2_raw[:, u, :, :], w2_hi[:, u % 2, :, :].bitcast(fp32),
                                ALU.subtract).then_inc(w_lo_done, 1)

            def rows_norm(e):
                dve.wait_ge(tokn_load, 16 * RT * (e + 1))
                for r in range(RT):
                    v.bn_stats(e_moments[:, r, :], tokn[:, r, :]).then_inc(e_stats, 1)
                moments_means(RT, e_moments, e_mean_var, e_stats, e_aggr, e)
                dve.wait_ge(e_rstd_done, e + 1)
                for r in range(RT):
                    v.tensor_scalar(tokn[:, r, :], tokn[:, r, :], e_mean_var[:, r, 0:1], e_rstd[:, r:r + 1],
                                    ALU.subtract, ALU.mult).then_inc(e_xn, 1)

            def hidden_low(e, u):
                c = NU * e + u
                dve.wait_ge(e_hhi, c + 1)
                wait(dve, e_y, c - 1)
                v.tensor_tensor(h_lo[:, u % 2, :, :], hid[:, u % 2, :, :], h_hi[:, u % 2, :, :].bitcast(fp32),
                                ALU.subtract).then_inc(e_hlo, 1)

            def results(e):
                dve.wait_ge(e_y, NU * (e + 1))
                dve.wait_ge(b2_load, 16 * (e + 1))
                dve.wait_ge(tok_load, 16 * RT * (e + 1))
                wait(dve, y_store, 16 * RT * e)
                for r in range(RT):
                    v.tensor_tensor(y_sb[:, r, :], y_bank[r][:, :], b2_sb[:, :], ALU.add).then_inc(e_yb, 1)
                v.tensor_copy(tok_id[:, :], tok[:, :, D].bitcast(i32)).then_inc(e_id, 1)
                for r in range(RT):
                    dve.wait_ge(e_yb, RT * e + r + 1)
                    v.scalar_tensor_tensor(y_sb[:, r, :], y_sb[:, r, :], tok[:, r, D + 1:D + 2], tok[:, r, 0:D],
                                           ALU.mult, ALU.add).then_inc(e_yout, 1)

            split_low(0, 0)
            dve.wait_ge(plain_store, PLAIN_ALL)
            dve.wait_ge(slot_store, 16 * NT)
            rows_norm(0)

            def expert(e, more):
                for u in range(NU):
                    hidden_low(e, u)
                    if u < NU - 1:
                        split_low(e, u + 1)
                    elif more:
                        split_low(e + 1, 0)
                    if more and u == 1:
                        rows_norm(e + 1)
                results(e)
            expert(0, True)
            with dve.Fori(1, E - 1) as e:
                expert(e, True)
            expert(E - 1, False)

        @block.tensor
        def _(pe):
            t = nc.tensor

            def k_and_v(L):
                if L == 0:
                    pe.wait_ge(ld_w["ctx"], 16)
                pe.wait_ge(ld_w[f"wk{L}"], 16)
                for m in range(KC):
                    wait(pe, k_evac, KC * L + m - 1)
                    for k in range(KC):
                        mm = t.matmul(g_bank[m % 2][:, 0:B * KEYS], wk_stage[L][:, k, cols128(m)], ctxT_sb[:, k, :],
                                      start=(k == 0), stop=(k == KC - 1))
                    mm.then_inc(k_done, 1)
                pe.wait_ge(ld_w[f"wv{L}"], 16)
                for b in range(B):
                    wait(pe, v_evac, B * L + b - 1)
                    for k in range(KC):
                        mm = t.matmul(row_bank[b][:, :], ctxT_sb[:, k, b * KEYS:(b + 1) * KEYS], wv_stage[L][:, k, :],
                                      start=(k == 0), stop=(k == KC - 1))
                    mm.then_inc(v_done, 1)

            k_and_v(0)
            k_and_v(1)
            pe.wait_ge(consts_ready, 3)
            pe.wait_ge(dve_consts, 1)
            pe.wait_ge(k_evac, 2 * KC)

            def body(L, i, front, middle, tail, batch):
                n, nf, nb = NSUP * L + i, NSUP * L + i + 1, NSUP * L + i - 1
                FL, TL = layers(L, i)

                def scores(u):
                    m, j = divmod(u, NSUB)
                    bank = row_bank[u % 2][:, :]
                    if u == 0:
                        pe.wait_ge(q_lo_done, KC * (n + 1))
                        pe.wait_ge(kd_done, HPC * (B * L + batch + 1))
                        if L == 0:
                            pe.wait_ge(hide_done, i + 1)
                            pe.wait_ge(v_evac, 2 * B)
                    wait(pe, exp_done, UNITS * n + u - 1)
                    mm = mm3(bank, qT_hi[:, m, cols128(j)], qT_lo[:, m, cols128(j)],
                             kd_hi[:, batch, m, :], kd_lo[:, batch, m, :], True, L == 1)
                    if L == 0:
                        mm = t.matmul(bank.rearrange("p (g k) -> p g k", g=HPC), hideT[:, cols128(j)],
                                      identb[:, :].unsqueeze(1).to_broadcast([P, HPC, KEYS]),
                                      start=False, stop=True)
                    mm.then_inc(rows_done, 1)

                def probs_transpose(u):
                    pe.wait_ge(norm_done, UNITS * n + u + 1)
                    wait(pe, pT_evac, UNITS * n + u - 1)
                    for g in range(HPC):
                        mm = t.transpose(pT_bank[u % 2][:, cols128(g)], prow[:, u % ROWS_BUF, cols128(g)], ident[:, :])
                    mm.then_inc(pT_done, 1)

                def weighted(m):
                    pe.wait_ge(pT_evac, UNITS * n + NSUB * (m + 1))
                    wait(pe, c_lo_done, KC * n + m)
                    if m == 0 and front:
                        pe.wait_ge(xT_lo_done, NSUB * nf + 3)
                    for g in range(HPC):
                        h = HPC * m + g
                        mm = t.matmul(ctx_bank[HD * g:HD * (g + 1), :], v_sb[:, L, batch, HD * h:HD * (h + 1)],
                                      probs[:, h % (2 * HPC), :], start=True, stop=True, tile_position=(0, HD * g))
                    mm.then_inc(pv_done, 1)

                def x_transpose(j):
                    pe.wait_ge(xn_done, NSUB * nf + j + 1)
                    if j >= 2:
                        pe.wait_ge(xT_lo_done, NSUB * nf + j - 1)
                    for k in range(KC):
                        mm = t.transpose(x_bank[j % 2][:, cols128(k)], xa[:, j, cols128(k)], ident[:, :])
                    mm.then_inc(xT_done, 1)

                def project_q(m):
                    if m == 0:
                        pe.wait_ge(wq_done, FL + 1)
                        pe.wait_ge(xT_lo_done, NSUB * (nf + 1))
                    if m < 2 and tail:
                        pe.wait_ge(res_done, NSUB * nb + 3 + m)
                    elif m < 2 and middle:
                        pe.wait_ge(q_lo_done, KC * n + 3 + m)
                    elif m >= 2:
                        pe.wait_ge(q_lo_done, KC * nf + m - 1)
                    for k in range(KC):
                        mm = mm3(g_bank[m % 2][:, :], wq_hi[:, k, cols128(m)], wq_lo[:, k, cols128(m)],
                                 xT_hi[:, k, :], xT_lo[:, k, :], k == 0, k == KC - 1)
                    mm.then_inc(q_done, 1)

                def project_out(j):
                    if j == 0:
                        pe.wait_ge(wo_done, TL + 1)
                        pe.wait_ge(c_lo_done, KC * nb + KC - 1)
                    if j < 2 and middle:
                        pe.wait_ge(q_lo_done, KC * n + 3 + j)
                    elif j < 2:
                        pe.wait_ge(res_done, NSUB * (nb - 1) + 3 + j)
                    else:
                        pe.wait_ge(res_done, NSUB * nb + j - 1)
                    for k in range(KC):
                        if j == 0 and k == KC - 1:
                            pe.wait_ge(c_lo_done, KC * (nb + 1))
                        mm = mm3(g_bank[j % 2][:, :], cT_hi[:, k, cols128(j)], cT_lo[:, k, cols128(j)],
                                 wo_hi[:, k, :], wo_lo[:, k, :], k == 0, k == KC - 1)
                    mm.then_inc(o_done, 1)

                def int8_transpose(j):
                    pe.wait_ge(f_z, NSUB * nb + j + 1)
                    if j:
                        pe.wait_ge(f_deq, NSUB * nb + j)
                    bank = tail_bank[:, 0:D // 2].bitcast(bf16)
                    for k in range(KC):
                        mm = t.transpose(bank[:, cols128(k)], zb[:, cols128(k)], identb[:, :])
                    mm.then_inc(f_zT, 1)

                def int8_product(j):
                    pe.wait_ge(f_zT_evac, NSUB * nb + j + 1)
                    for k in range(KC):
                        mm = t.matmul(tail_bank[:, :], zT[:, k, :], rq[:, k, :], start=(k == 0), stop=(k == KC - 1))
                    mm.then_inc(f_acc, 1)

                def route_transpose(j):
                    pe.wait_ge(txn_done, NSUB * nb + j + 1)
                    if j:
                        pe.wait_ge(r_log_evac, NSUB * (i - 1) + j)
                    else:
                        pe.wait_ge(tail_free, i)
                    for k in range(KC):
                        mm = t.transpose(tail_bank[:, cols128(k)], xn[:, j, cols128(k)], ident[:, :])
                    mm.then_inc(r_T, 1)

                def route_logits(j):
                    pe.wait_ge(r_T_evac, NSUB * (i - 1) + j + 1)
                    for k in range(KC):
                        mm = t.matmul(tail_bank[0:E, 0:P], wsw_sb[:, k, :], xrT[:, k, :],
                                      start=(k == 0), stop=(k == KC - 1))
                    mm.then_inc(r_log, 1)

                def logits_transpose():
                    wait_apart(pe, r_log_evac, NSUB * i)
                    for j in range(NSUB):
                        mm = t.transpose(tail_bank[:, E * j:E * (j + 1)], logT[:, cols128(j)], ident[0:E, 0:E])
                    mm.then_inc(r_lt, 1)

                def route_counts():
                    pe.wait_ge(r_hot, i)
                    for j in range(NSUB + 1):
                        for k in range(min(j, NSUB - 1) + 1):
                            full_tile = k < j
                            mm = t.matmul(counts[:, E * j:E * (j + 1)], (onesb if full_tile else upto)[:, :],
                                          onehot[:, k, :], start=(k == 0), stop=(k == min(j, NSUB - 1)))
                    mm.then_inc(r_cum, 1)

                for u in range(UNITS):
                    if middle:
                        scores(u)
                    if middle and u >= LAG:
                        probs_transpose(u - LAG)
                    for j in range(NSUB):
                        if tail and u == tail_at(TL, j) + 1:
                            (int8_product, route_logits)[TL](j)
                    if tail and u < NSUB:
                        project_out(u)
                    for j in range(NSUB):
                        if front and u == XT_AT[j]:
                            x_transpose(j)
                    for m in range(KC):
                        if front and u == Q_AT[m]:
                            project_q(m)
                    for j in range(NSUB):
                        if tail and u == tail_at(TL, j):
                            (int8_transpose, route_transpose)[TL](j)
                    for m in range(KC):
                        if middle and u == PV_AT[m]:
                            weighted(m)
                    if tail and TL == 1 and u == 13:
                        logits_transpose()
                    if tail and TL == 1 and u == 15:
                        route_counts()
                if middle:
                    probs_transpose(UNITS - LAG)
                if tail and TL == 0:
                    int8_transpose(NSUB - 1)
                if middle:
                    probs_transpose(UNITS - 2)
                if front:
                    project_q(KC - 1)
                if middle:
                    probs_transpose(UNITS - 1)
                if tail and TL == 0:
                    int8_product(NSUB - 1)
                if middle:
                    weighted(KC - 1)

            bodies(pe, 0, body)
            bodies(pe, 1, body)

            def rows_transpose(e):
                for r in range(RT):
                    pe.wait_ge(e_xn, RT * e + r + 1)
                    wait(pe, e_T_evac, RT * (e - 1) + r + 1)
                    for k in range(KC):
                        mm = t.transpose(tt_bank[r][:, cols128(k)], tokn[:, r, cols128(k)], ident[:, :])
                    mm.then_inc(e_T, 1)

            def hidden(e, u):
                c = NU * e + u
                pe.wait_ge(w_load[0][u], 16 * (e + 1))
                if u == 0:
                    pe.wait_ge(e_T_evac, RT * (e + 1))
                for f in range(UC):
                    wait(pe, e_relu, UC * c + f - 1)
                    for k in range(KC):
                        mm = t.matmul(hb_bank[f % 2][:, 0:CAP], w1_raw[:, u, k, cols128(f)], tT[:, k, :],
                                      start=(k == 0), stop=(k == KC - 1))
                    mm.then_inc(e_h, 1)

            def second(e, u):
                c = NU * e + u
                pe.wait_ge(w_lo_done, c + 1)
                pe.wait_ge(e_hlo, c + 1)
                if u == 0:
                    wait(pe, e_yb, RT * e)
                for r in range(RT):
                    for f in range(UC):
                        mm = mm3(y_bank[r][:, :], h_hi[:, u % 2, f, cols128(r)], h_lo[:, u % 2, f, cols128(r)],
                                 w2_hi[:, u % 2, f, :], w2_lo[:, u % 2, f, :],
                                 u == 0 and f == 0, u == NU - 1 and f == UC - 1)
                mm.then_inc(e_y, 1)

            def expert(e, more):
                for u in range(1, NU):
                    hidden(e, u)
                    second(e, u - 1)
                if more:
                    rows_transpose(e + 1)
                    hidden(e + 1, 0)
                second(e, NU - 1)

            rows_transpose(0)
            hidden(0, 0)
            expert(0, True)
            with pe.Fori(1, E - 1) as e:
                expert(e, True)
            expert(E - 1, False)


def kernel(x, ctx_1024, itok_BxS_0_511, L0_xattn_Wq, L0_xattn_Wkv, L0_xattn_Wo, L0_ffn_rhs,
           L1_xattn_in_proj_weight, L1_xattn_in_proj_bias, L1_xattn_out_w, L1_xattn_out_b,
           L1_ffn_w_switch, L1_ffn_b_switch, L1_ffn_w1, L1_ffn_b1, L1_ffn_w2, L1_ffn_b2):
    import concourse.bacc as bacc
    from concourse.bass_utils import run_bass_kernel_spmd

    def lay(a):
        return np.ascontiguousarray(np.asarray(a))

    def chunks(v):
        return lay(np.asarray(v).reshape(-1, P).T)

    bias = np.asarray(L1_xattn_in_proj_bias)
    seg = np.asarray(itok_BxS_0_511).reshape(T)
    arrays = {
        "x": lay(np.asarray(x).reshape(T, D)),
        "ctxT": lay(np.asarray(ctx_1024).reshape(B * KEYS, D).T),
        "segT": chunks(seg), "seg": lay(seg.reshape(1, T)),
        "wq0": lay(np.asarray(L0_xattn_Wq).T), "wkv0": lay(np.asarray(L0_xattn_Wkv).T),
        "wo0": lay(np.asarray(L0_xattn_Wo).T), "rhs": lay(L0_ffn_rhs),
        "wqkv1": lay(np.asarray(L1_xattn_in_proj_weight).T),
        "bq1": chunks(bias[0:D]), "bk1": chunks(bias[D:2 * D]), "bv1": lay(bias[2 * D:].reshape(1, D)),
        "wo1": lay(np.asarray(L1_xattn_out_w).T), "bo1": lay(np.asarray(L1_xattn_out_b).reshape(1, D)),
        "wsw": lay(L1_ffn_w_switch), "bsw": lay(np.asarray(L1_ffn_b_switch).reshape(E, 1)),
        "w1": lay(L1_ffn_w1), "b1": chunks(np.asarray(L1_ffn_b1).reshape(-1)),
        "w2": lay(L1_ffn_w2), "b2": lay(L1_ffn_b2),
    }
    nc = bacc.Bacc("TRN2", target_bir_lowering=False, num_devices=1)
    args = {n: nc.dram_tensor("in_" + n, a.shape, mybir.dt.from_np(a.dtype), kind="ExternalInput").ap()
            for n, a in arrays.items()}
    out = nc.dram_tensor("out", [T, D], mybir.dt.float32, kind="ExternalOutput").ap()
    build(nc, out=out, **args)
    r = run_bass_kernel_spmd(nc, [{"in_" + n: a for n, a in arrays.items()}], core_ids=[0])
    return r.results[0]["out"].reshape(B, S, D)
```

```python
import numpy as np
import concourse.bass as bass
from concourse import mybir
from contextlib import ExitStack

P = 128
B, S, D = 2, 2048, 512
T = B * S
KEYS = 128
H, HD = 16, 32
KC = D // P
HPC = H // KC
SUP = 512
NSUB = SUP // P
NSUP = T // SUP
NSUP_B = NSUP // B
NT = T // P
E, F = 8, 2048
CAP = T // 2 // E
RT = CAP // P
NU, UF = 4, F // 4
UC = UF // P
LOOKBACK = 3
ROW = D + 4
EPS = 1e-5
SCALE = HD ** -0.5
HIDE = -1e30
MAGIC = 1.5 * 2.0 ** 23
NOWHERE = 1 << 20

UNITS = KC * NSUB
ROWS_BUF = 4
LAG = 3
XT_AT = (3, 4, 5, 6)
Q_AT = (8, 10, 12, UNITS - 1)
PV_AT = tuple(NSUB * (m + 1) + LAG for m in range(KC - 1)) + (UNITS,)
NORM_AT = NSUB + 3
TAIL_FROM, TAIL_STEP = (10, 9), (2, 1)


def tail_at(layer, j):
    return TAIL_FROM[layer] + TAIL_STEP[layer] * j


def build(nc, x, ctxT, segT, seg, wq0, wkv0, wo0, rhs, wqkv1, bq1, bk1, bv1, wo1, bo1,
          wsw, bsw, w1, b1, w2, b2, out):
    fp32, bf16, f32r = mybir.dt.float32, mybir.dt.bfloat16, mybir.dt.float32r
    i32, u32 = mybir.dt.int32, mybir.dt.uint32
    ALU, ACT, AX = mybir.AluOpType, mybir.ActivationFunctionType, mybir.AxisListType

    x2_dram = nc.dram_tensor("x2_scratch", [T, D], fp32, kind="Internal").ap()
    slots_dram = nc.dram_tensor("slots_scratch", [E * CAP, ROW], fp32, kind="Internal").ap()
    x_tiles = x.rearrange("(n p) d -> n p d", p=P)
    x2_tiles = x2_dram.rearrange("(n p) d -> n p d", p=P)
    out_tiles = out.rearrange("(n p) d -> n p d", p=P)
    slot_tiles = slots_dram.rearrange("(n p) d -> n p d", p=P)

    ctx = ExitStack()
    with ctx:
        attn = ExitStack()
        ctx.enter_context(attn)

        def keep(name, shape, dt):
            return ctx.enter_context(nc.sbuf_tensor(name, shape, dt))

        def sb(name, shape, dt):
            return attn.enter_context(nc.sbuf_tensor(name, shape, dt))

        def sem(name):
            return ctx.enter_context(nc.semaphore(name))

        ident = keep("ident", [P, P], fp32)
        eps_half = keep("eps_half", [P, 8], fp32)
        moments = keep("moments", [P, NSUB, 6], fp32)
        mean_var = keep("mean_var", [P, NSUB, 2], fp32)
        var_eps = keep("var_eps", [P, NSUB], fp32)
        rstd = keep("rstd", [P, NSUB], fp32)
        b1_sb = keep("b1_sb", [P, E * NU * UC], fp32)

        wq_hi, wq_lo = sb("wq_hi", [P, KC, D], f32r), sb("wq_lo", [P, KC, D], f32r)
        xT_hi, xT_lo = sb("xT_hi", [P, KC, SUP], f32r), sb("xT_lo", [P, KC, SUP], f32r)
        xa = sb("xa", [P, NSUB, D], fp32)
        w_stage = sb("w_stage", [P, KC, D], fp32)
        kd_hi, kd_lo = sb("kd_hi", [P, B, KC, HPC * KEYS], f32r), sb("kd_lo", [P, B, KC, HPC * KEYS], f32r)
        qT_hi, qT_lo = sb("qT_hi", [P, KC, SUP], f32r), sb("qT_lo", [P, KC, SUP], f32r)
        identb = sb("identb", [P, P], bf16)
        wo_hi, wo_lo = sb("wo_hi", [P, KC, D], f32r), sb("wo_lo", [P, KC, D], f32r)
        kT1 = sb("kT1", [P, 2, 2, B * KEYS], fp32)
        v_sb = sb("v_sb", [KEYS, 2, B, D], fp32)
        xb = sb("xb", [P, NSUB, D], fp32)
        prow = sb("prow", [P, ROWS_BUF, HPC * KEYS], fp32)
        probs = sb("probs", [KEYS, 2 * HPC, SUP], fp32)
        cT_hi, cT_lo = sb("cT_hi", [P, KC, SUP], f32r), sb("cT_lo", [P, KC, SUP], f32r)
        neg_max = sb("neg_max", [P, ROWS_BUF, HPC], fp32)
        sums = sb("sums", [P, ROWS_BUF, HPC], fp32)
        totals = sb("totals", [P, ROWS_BUF, HPC], fp32)
        inv = sb("inv", [P, ROWS_BUF, HPC], fp32)
        hideT = sb("hideT", [KEYS, SUP], bf16)
        seg_row = sb("seg_row", [KEYS, SUP], i32)
        seg_f = sb("seg_f", [KEYS, SUP], fp32)
        seg_col = sb("seg_col", [P, NT], i32)
        seg_cf = sb("seg_cf", [P, NT], fp32)
        times = sb("times", [P, NT], fp32)
        more = sb("more", [P, NT], fp32)
        key_num = sb("key_num", [P, 1], fp32)
        xs = sb("xs", [P, NSUB, ROW], fp32)
        xn = sb("xn", [P, NSUB, D], fp32)
        t_moments = sb("t_moments", [P, NSUB, 6], fp32)
        t_mean_var = sb("t_mean_var", [P, NSUB, 2], fp32)
        t_var_eps = sb("t_var_eps", [P, NSUB], fp32)
        t_rstd = sb("t_rstd", [P, NSUB], fp32)
        zb = sb("zb", [P, D], bf16)
        zT = sb("zT", [P, KC, P], bf16)
        rq = sb("rq", [P, KC, D], bf16)
        rscale = sb("rscale", [P, D], fp32)
        amax = sb("amax", [P, NSUB], fp32)
        lscale = sb("lscale", [P, NSUB], fp32)
        linv = sb("linv", [P, NSUB], fp32)
        minus_magic = sb("minus_magic", [P, 1], fp32)
        bq_sb, bk_sb = sb("bq_sb", [P, KC], fp32), sb("bk_sb", [P, KC], fp32)
        bo_sb = rscale
        wsw_sb = sb("wsw_sb", [P, KC, E], fp32)
        bsw_sb = sb("bsw_sb", [E, 1], fp32)
        xrT = rq[:, 0:2, :].rearrange("p a b -> p (a b)").bitcast(fp32).rearrange("p (k t) -> p k t", k=KC)
        logT = rq[0:E, 2:4, :].rearrange("p a b -> p (a b)").bitcast(fp32)
        logits = sb("logits", [P, NSUB, E], fp32)
        top8 = sb("top8", [P, NSUB, 8], fp32)
        top_at = sb("top_at", [P, NSUB, 8], u32)
        route = sb("route", [P, NSUB], fp32)
        expl = sb("expl", [P, NSUB, E], fp32)
        psum_e = sb("psum_e", [P, NSUB], fp32)
        pmax = sb("pmax", [P, NSUB], fp32)
        scale_t = sb("scale_t", [P, NSUB], fp32)
        lane8 = sb("lane8", [P, E], fp32)
        onehot = sb("onehot", [P, NSUB, E], bf16)
        upto = sb("upto", [P, P], bf16)
        onesb = sb("onesb", [P, P], bf16)
        carry = sb("carry", [P, E], fp32)
        place = sb("place", [P, NSUB, E], fp32)
        pos = sb("pos", [P, NSUB], fp32)
        full = sb("full", [P, NSUB], fp32)
        slot_f = sb("slot_f", [P, NSUB], fp32)
        slot = sb("slot", [P, NSUB], u32)
        token_num = sb("token_num", [P, NT], i32)
        wk_stage = (probs[:, 0:4, :], xn[:, :, :])
        wv_stage = (probs[:, 4:8, :], xs[:, :, 0:D])
        bv_sb = rscale
        kT0 = xb[:, 2:4, :].rearrange("p a (c n) -> p a c n", c=2)
        ctxT_sb = xb[:, 0:2, :].rearrange("p a (c n) -> p (a c) n", c=2)
        kT = (kT0, kT1)

        attn.close()
        moe = ExitStack()
        ctx.enter_context(moe)

        def mb(name, shape, dt):
            return moe.enter_context(nc.sbuf_tensor(name, shape, dt))

        NR = NU
        w1_raw = mb("w1_raw", [P, NR, KC, UF], fp32)
        w2_raw = mb("w2_raw", [P, NR, UC, D], fp32)
        w2_hi, w2_lo = mb("w2_hi", [P, 2, UC, D], f32r), mb("w2_lo", [P, 2, UC, D], f32r)
        tok = mb("tok", [P, RT, ROW], fp32)
        tokn = mb("tokn", [P, RT, D], fp32)
        tT_hi, tT_lo = mb("tT_hi", [P, KC, CAP], f32r), mb("tT_lo", [P, KC, CAP], f32r)
        hrow = mb("hrow", [P, RT, UF], fp32)
        hid = mb("hid", [P, 2, UC, CAP], fp32)
        h_hi, h_lo = mb("h_hi", [P, 2, UC, CAP], f32r), mb("h_lo", [P, 2, UC, CAP], f32r)
        b2_sb = mb("b2_sb", [P, D], fp32)
        y_sb = mb("y_sb", [P, RT, D], fp32)
        e_moments = mb("e_moments", [P, RT, 6], fp32)
        e_mean_var = mb("e_mean_var", [P, RT, 2], fp32)
        e_var_eps = mb("e_var_eps", [P, RT], fp32)
        e_rstd = mb("e_rstd", [P, RT], fp32)
        tok_id = mb("tok_id", [P, RT], u32)
        w1_hi, w1_lo = mb("w1_hi", [P, 2, KC, UF], f32r), mb("w1_lo", [P, 2, KC, UF], f32r)

        banks = [ctx.enter_context(nc.psum_tensor(f"bank{i}", [P, 512], fp32)) for i in range(8)]
        row_bank, pT_bank = banks[0:2], banks[2:4]
        ctx_bank, tail_bank = banks[4], banks[5]
        x_bank = (ctx_bank, tail_bank)
        counts = tail_bank[:, 2 * NSUB * E:(3 * NSUB + 1) * E]
        g_bank = banks[6:8]
        hb_bank, y_bank, tt_bank, hT_bank = banks[0:2], banks[2:4], banks[4:6], banks[6:8]

        ld_w = {n: sem("ld_" + n) for n in
                ("ctx", "wk0", "wv0", "wk1", "wv1", "wq0", "wo0", "wq1", "wo1", "rhs", "small", "bv", "bo")}
        consts_ready, pool_step, dve_step = sem("consts_ready"), sem("pool_step"), sem("dve_step")
        bias_scaled, tail_free = sem("bias_scaled"), sem("tail_free")
        k_done, k_evac, v_done, v_evac = sem("k_done"), sem("k_evac"), sem("v_done"), sem("v_evac")
        kd_hi_done, kd_done = sem("kd_hi_done"), sem("kd_done")
        wq_hi_done, wq_done, wo_hi_done, wo_done = (sem("wq_hi_done"), sem("wq_done"),
                                                    sem("wo_hi_done"), sem("wo_done"))
        met = sem("met")
        dve_consts, empty_row, hide_wide = sem("dve_consts"), sem("empty_row"), sem("hide_wide")
        rhs_amax, rhs_all, rhs_done = sem("rhs_amax"), sem("rhs_all"), sem("rhs_done")
        xa_load = [sem(f"xa_load{j}") for j in range(NSUB)]
        xb_load = [sem(f"xb_load{j}") for j in range(NSUB)]
        xb_biased = sem("xb_biased")
        seg_load, hide_step, hide_done = sem("seg_load"), sem("hide_step"), sem("hide_done")
        stats, aggr, rstd_step, rstd_done, xn_done = (sem("stats"), sem("aggr"), sem("rstd_step"),
                                                      sem("rstd_done"), sem("xn_done"))
        xT_done, xT_hi_done, xT_lo_done = sem("xT_done"), sem("xT_hi_done"), sem("xT_lo_done")
        q_done, q_hi_done, q_lo_done = sem("q_done"), sem("q_hi_done"), sem("q_lo_done")
        rows_done, max_done, exp_done = sem("rows_done"), sem("max_done"), sem("exp_done")
        total_done, inv_done, norm_done = sem("total_done"), sem("inv_done"), sem("norm_done")
        pT_done, pT_evac, pv_done = sem("pT_done"), sem("pT_evac"), sem("pv_done")
        c_hi_done, c_lo_done = sem("c_hi_done"), sem("c_lo_done")
        o_done, res_done = sem("o_done"), sem("res_done")
        t_stats, t_aggr, t_rstd_step, t_rstd_done = (sem("t_stats"), sem("t_aggr"), sem("t_rstd_step"),
                                                     sem("t_rstd_done"))
        txn_done = sem("txn_done")
        f_step, f_round, f_z, f_zT, f_zT_evac, f_acc, f_deq, x2_done = (
            sem("f_step"), sem("f_round"), sem("f_z"), sem("f_zT"), sem("f_zT_evac"),
            sem("f_acc"), sem("f_deq"), sem("x2_done"))
        x2_store = [sem(f"x2_store{j}") for j in range(NSUB)]
        r_T, r_T_evac, r_log, r_log_evac, r_lt, r_lt_evac = (
            sem("r_T"), sem("r_T_evac"), sem("r_log"), sem("r_log_evac"), sem("r_lt"), sem("r_lt_evac"))
        r_step, r_negtop, r_exp, r_hot, r_cum, r_slot, r_plain = (
            sem("r_step"), sem("r_negtop"), sem("r_exp"), sem("r_hot"), sem("r_cum"), sem("r_slot"), sem("r_plain"))
        plain_store, slot_store, xs_free = sem("plain_store"), sem("slot_store"), sem("xs_free")
        w_load = [[sem(f"w{n}_load{r}") for r in range(NR)] for n in (1, 2)]
        w_hi_done = [sem(f"w{n}_hi_done") for n in (1, 2)]
        w_lo_done = [sem(f"w{n}_lo_done") for n in (1, 2)]
        tokn_load, tok_load, b2_load = sem("tokn_load"), sem("tok_load"), sem("b2_load")
        e_stats, e_aggr, e_rstd_step, e_rstd_done, e_xn = (sem("e_stats"), sem("e_aggr"), sem("e_rstd_step"),
                                                      sem("e_rstd"), sem("e_xn"))
        e_T, e_T_hi, e_T_lo = sem("e_T"), sem("e_T_hi"), sem("e_T_lo")
        e_hcopy, e_hT = [sem(f"e_hcopy{r}") for r in range(RT)], sem("e_hT")
        e_h, e_relu, e_hhi, e_hlo = sem("e_h"), sem("e_relu"), sem("e_hhi"), sem("e_hlo")
        e_y, e_yb, e_yout, e_id, y_store = sem("e_y"), sem("e_yb"), sem("e_yout"), sem("e_id"), sem("y_store")

        SMALL = [(seg_col[:, :], segT), (bq_sb[:, :], bq1), (bk_sb[:, :], bk1),
                 (wsw_sb[:, :, :], wsw.rearrange("(k p) n -> p k n", p=P)), (bsw_sb[:, :], bsw), (b1_sb[:, :], b1)]
        ROUTE_STEPS = 22

        def bodies(engine, L, emit, loads=False):
            if L == 0:
                emit(L, -1, True, False, False, 0)
                emit(L, 0, True, True, False, 0)
            else:
                emit(L, 0, True, True, True, 0)
            with engine.Fori(1, NSUP_B - 1) as i:
                emit(L, i, True, True, True, 0)
            emit(L, NSUP_B - 1, True, True, True, 0)
            with engine.Fori(NSUP_B, NSUP - 1 - loads) as i:
                emit(L, i, True, True, True, 1)
            if loads:
                emit(L, NSUP - 2, True, True, True, 1)
            emit(L, NSUP - 1, L == 0, True, True, 1)
            if L == 1:
                emit(L, NSUP, False, False, True, 1)

        def at(i, value):
            return isinstance(i, int) and i == value

        def layers(L, i):
            return (1 if at(i, NSUP - 1) else L), (0 if at(i, 0) else L)

        X2_FIRST = 16 * E * RT // NSUB
        PLAIN_FIRST = 16
        PLAIN_ALL = PLAIN_FIRST + 16 * NT

        def ahead(e, u, steps, more):
            if u + steps < NU:
                return e, u + steps
            return (e + 1, u + steps - NU) if more else None

        def mm3(out, a_hi, a_lo, b_hi, b_lo, start, stop):
            nc.tensor.matmul(out, a_hi, b_hi, start=start, stop=False)
            nc.tensor.matmul(out, a_hi, b_lo, start=False, stop=False)
            return nc.tensor.matmul(out, a_lo, b_hi, start=False, stop=stop)

        def wait(e, s, v):
            if not isinstance(v, int) or v > 0:
                e.wait_ge(s, v)

        def wait_apart(e, s, v):
            wait(e, s, v)
            e.sem_inc(met, 1)

        def cols128(n):
            return slice(n * P, (n + 1) * P)

        block = ctx.enter_context(nc.Block())


        @block.sync
        def _(sp):
            def load(dst, src, s):
                sp.dma_start(dst, src).then_inc(s, 16)

            def chunked(w):
                return w.rearrange("(k p) n -> p k n", p=P)

            load(ctxT_sb, chunked(ctxT), ld_w["ctx"])
            load(wk_stage[0], chunked(wkv0[:, 0:D]), ld_w["wk0"])
            for dst, src in SMALL:
                load(dst, src, ld_w["small"])
            load(seg_row[:, :], seg[:, 0:SUP].to_broadcast([KEYS, SUP]), seg_load)
            load(wv_stage[0], chunked(wkv0[:, D:2 * D]), ld_w["wv0"])
            for j in range(NSUB):
                load(xa[:, j, :], x_tiles[j, :, :], xa_load[j])
            load(w_stage[:, :, :], chunked(wq0), ld_w["wq0"])
            load(wk_stage[1], chunked(wqkv1[:, D:2 * D]), ld_w["wk1"])
            load(wv_stage[1], chunked(wqkv1[:, 2 * D:3 * D]), ld_w["wv1"])
            load(bv_sb[:, :], bv1.to_broadcast([P, D]), ld_w["bv"])

            w1_u = w1.rearrange("e (k p) (u f) -> e u p k f", p=P, u=NU)
            w2_u = w2.rearrange("e (u c p) d -> e u p c d", p=P, u=NU)

            def rows_load(e):
                wait(sp, e_T, RT * e)
                for r in range(RT):
                    load(tokn[:, r, :], slot_tiles[RT * e + r, :, 0:D], tokn_load)

            def result_loads(e):
                wait(sp, e_yout, RT * e)
                for r in range(RT):
                    load(tok[:, r, :], slot_tiles[RT * e + r, :, :], tok_load)
                load(b2_sb[:, :], b2[bass.ds(e, 1), :].to_broadcast([P, D]), b2_load)

            def w1_load(e, u):
                load(w1_raw[:, u, :, :], w1_u[e, u, :, :, :], w_load[0][u])

            def w2_load(e, u):
                load(w2_raw[:, u, :, :], w2_u[e, u, :, :, :], w_load[1][u])

            def unit_loads(e, u):
                wait(sp, w_lo_done[0], NU * (e - 1) + u + 1)
                w1_load(e, u)
                wait(sp, w_lo_done[1], NU * (e - 1) + u + 1)
                w2_load(e, u)

            def expert(e, more, units=True):
                for u in range(NU):
                    if units:
                        unit_loads(e, u)
                if more:
                    rows_load(e + 1)
                result_loads(e)

            def load_xa(L, i, j):
                wait(sp, xT_done, NSUB * (NSUP * L + i - 1) + j + 1)
                if L == 1:
                    sp.wait_ge(x2_store[j], X2_FIRST + 16 * (i + 1))
                load(xa[:, j, :], (x_tiles, x2_tiles)[L][NSUB * i + j, :, :], xa_load[j])

            def load_xb(L, i, j):
                wait(sp, res_done, NSUB * (NSUP * L + i - 1) + j + 1)
                load(xb[:, j, :], (x_tiles, x2_tiles)[L][NSUB * i + j, :, :], xb_load[j])

            def body(L, i, front, middle, tail, batch):
                FL, TL = layers(L, i)
                if L == 1 and at(i, 0):
                    sp.wait_ge(wq_done, 2)
                    load(w_stage[:, :, :], chunked(wo1), ld_w["wo1"])
                if front and FL == 0 and not at(i, -1):
                    sp.wait_ge(hide_step, 2 * i + 1)
                    load(seg_row[:, :], seg[:, bass.ds((i + 1) * SUP, SUP)].to_broadcast([KEYS, SUP]), seg_load)
                if middle:
                    if L == 0 and at(i, 0):
                        sp.wait_ge(wo_done, 1)
                        load(w_stage[:, :, :], chunked(rhs), ld_w["rhs"])
                        sp.wait_ge(v_done, 2 * B)
                        sp.wait_ge(kd_done, HPC * B)
                    for j in range(NSUB):
                        load_xb(L, i, j)
                if L == 1 and at(i, NSUP - 1):
                    sp.wait_ge(q_done, KC * 2 * NSUP)
                    for u in range(NU // 2):
                        w1_load(0, u)
                        w2_load(0, u)
                    for u in range(NU // 2, NU):
                        w1_load(0, u)
                if L == 1 and at(i, NSUP):
                    sp.wait_ge(rows_done, UNITS * 2 * NSUP)
                    for u in range(NU // 2, NU):
                        w2_load(0, u)
                for j in range(NSUB):
                    if not isinstance(i, int) or i < NSUP - 2:
                        load_xa(L, i + 2, j)
                    elif L == 0:
                        load_xa(1, i + 2 - NSUP, j)
                if at(i, -1):
                    sp.wait_ge(wq_done, 1)
                    load(w_stage[:, :, :], chunked(wo0), ld_w["wo0"])
                if L == 0 and at(i, 0):
                    sp.wait_ge(empty_row, 2)
                    for n in range(E * RT):
                        load(slot_tiles[n, :, :], xs[:, 0, :], x2_store[n % NSUB])
                    sp.wait_ge(rhs_done, 1)
                    load(w_stage[:, :, :], chunked(wqkv1[:, 0:D]), ld_w["wq1"])
                if tail:
                    for j in range(NSUB):
                        if TL == 0:
                            n = NSUB * (NSUP * L + i - 1) + j
                            sp.wait_ge(x2_done, n + 1)
                            load(x2_tiles[n, :, :], xs[:, j, 0:D], x2_store[j])
                        else:
                            n = NSUB * (i - 1) + j
                            sp.wait_ge(r_plain, n + 1)
                            load(out_tiles[n, :, :], xn[:, j, :], plain_store)
                if tail and TL == 1:
                    sp.wait_ge(slot_store, 16 * NSUB * i)
                    sp.sem_inc(xs_free, 1)
                if L == 1 and at(i, 0):
                    for j in range(NSUB):
                        sp.wait_ge(x2_store[j], X2_FIRST + 16 * NSUP)
                    sp.sem_inc(xs_free, 1)
                    sp.wait_ge(f_deq, NT)
                    load(bo_sb[:, :], bo1.to_broadcast([P, D]), ld_w["bo"])
            bodies(sp, 0, body, loads=True)
            bodies(sp, 1, body, loads=True)

            sp.wait_ge(slot_store, 16 * NT)
            sp.wait_ge(plain_store, PLAIN_ALL)
            rows_load(0)
            expert(0, True, units=False)
            with sp.Fori(1, E - 1) as e:
                expert(e, True)
            expert(E - 1, False)

        @block.gpsimd
        def _(pool):
            g = nc.gpsimd
            steps = [0]

            def step(ins):
                steps[0] += 1
                ins.then_inc(pool_step, 1)
                pool.wait_ge(pool_step, steps[0])

            step(g.memset(ident[:, :], 0.0))
            g.affine_select(out=ident[:, :], in_=ident[:, :], compare_op=ALU.not_equal, fill=1.0,
                            base=0, pattern=[[-1, P]], channel_multiplier=1).then_inc(consts_ready, 1)
            g.memset(kd_hi[:, :, :, :].bitcast(fp32), 0.0).then_inc(consts_ready, 1)
            g.memset(eps_half[:, :], -0.5)
            g.memset(minus_magic[:, :], -MAGIC)
            g.memset(carry[:, :], 0.0)
            g.memset(onesb[:, :], 1.0)
            step(g.memset(upto[:, :], 1.0))
            g.affine_select(out=upto[:, :], in_=upto[:, :], compare_op=ALU.is_ge, fill=0.0,
                            base=0, pattern=[[1, P]], channel_multiplier=-1)
            g.iota(key_num[:, :], pattern=[[0, 1]], base=0, channel_multiplier=1,
                   allow_small_or_imprecise_dtypes=True)
            g.iota(lane8[:, :], pattern=[[1, E]], base=0, channel_multiplier=0,
                   allow_small_or_imprecise_dtypes=True)
            g.iota(token_num[:, :], pattern=[[P, NT]], base=0, channel_multiplier=1).then_inc(consts_ready, 1)
            g.memset(xs[:, 1:NSUB, D:ROW], 0.0)
            def inverse_root(ve, mv, r, ready, count, mid, mid_count, done):
                wait_apart(pool, ready, count)
                g.tensor_scalar(ve[:, :], mv[:, :, 1], EPS, 0.0, ALU.add, ALU.add).then_inc(mid, 1)
                pool.wait_ge(mid, mid_count)
                n = ve.shape[1]
                g.tensor_tensor(r[:, :], ve[:, :], eps_half[:, 0:n], ALU.pow).then_inc(done, 1)

            def empty_slot():
                pool.wait_ge(v_done, 2 * B)
                step(g.memset(xs[:, 0, :], 0.0))
                g.iota(xs[:, 0, D:D + 1].bitcast(i32), pattern=[[0, 1]], base=NOWHERE,
                       channel_multiplier=0).then_inc(empty_row, 2)

            def body(L, i, front, middle, tail, batch):
                n, nf, nb = NSUP * L + i, NSUP * L + i + 1, NSUP * L + i - 1
                FL, TL = layers(L, i)

                def bias_xb(j):
                    pool.wait_ge(xb_load[j], 16 * (nb + 1))
                    g.tensor_tensor(xb[:, j, :], xb[:, j, :], bo_sb[:, :], ALU.add).then_inc(xb_biased, 1)

                def normalise(u):
                    pool.wait_ge(inv_done, UNITS * n + u + 1)
                    pu = prow[:, u % ROWS_BUF, :].rearrange("p (g k) -> p g k", g=HPC)
                    g.tensor_tensor(pu, pu, inv[:, u % ROWS_BUF, :].unsqueeze(2).to_broadcast([P, HPC, KEYS]),
                                    ALU.mult).then_inc(norm_done, 1)

                for u in range(UNITS + 1):
                    if tail and TL == 1 and u < NSUB:
                        bias_xb(u)
                    if middle and u:
                        normalise(u - 1)
                    if L == 0 and at(i, 0) and u == 5:
                        empty_slot()
                    if L == 0 and at(i, 0) and u == 9:
                        pool.wait_ge(rhs_amax, 1)
                        g.partition_all_reduce(rscale[:, :], xn[:, 0, :], P,
                                               bass.bass_isa.ReduceOp.absmax).then_inc(rhs_all, 1)
                    if front and u == 1:
                        inverse_root(var_eps, mean_var, rstd, aggr, NSUB * (nf + 1), rstd_step, nf + 1, rstd_done)
                    if tail and u == 6:
                        inverse_root(t_var_eps, t_mean_var, t_rstd, t_aggr, NSUB * (nb + 1), t_rstd_step, nb + 1,
                                     t_rstd_done)
                    for j in range(NSUB):
                        if tail and TL == 0 and u == min(tail_at(0, j) + 2, UNITS):
                            pool.wait_ge(f_deq, NSUB * nb + j + 1)
                            g.tensor_tensor(xs[:, j, 0:D], xs[:, j, 0:D], xn[:, j, :], ALU.add).then_inc(x2_done, 1)
                if tail and TL == 1:
                    wait_apart(pool, r_slot, i)
                    for j in range(NSUB):
                        pool.indirect_dma_start(
                            slots_dram, bass.IndirectOffsetOnAxis(ap=slot[:, j:j + 1], axis=0),
                            xs[:, j, :], None, bounds_check=E * CAP - 1, oob_is_err=False).then_inc(slot_store, 16)
                if L == 1 and at(i, 0):
                    pool.wait_ge(ld_w["bo"], 16)
                    for j in range(NSUB):
                        pool.wait_ge(x2_store[j], X2_FIRST)
            bodies(pool, 0, body)
            bodies(pool, 1, body)

            def roots(e):
                inverse_root(e_var_eps, e_mean_var, e_rstd, e_aggr, RT * (e + 1), e_rstd_step, e + 1, e_rstd_done)

            def scatter(e):
                for r in range(RT):
                    wait_apart(pool, e_yout, RT * e + r + 1)
                    pool.indirect_dma_start(
                        out, bass.IndirectOffsetOnAxis(ap=tok_id[:, r:r + 1], axis=0),
                        y_sb[:, r, :], None, bounds_check=T - 1, oob_is_err=False).then_inc(y_store, 16)
            roots(0)
            pool.wait_ge(plain_store, PLAIN_ALL)
            with pool.Fori(0, E - 1) as e:
                roots(e + 1)
                scatter(e)
            scatter(E - 1)
            pool.wait_ge(y_store, 16 * E * RT)

        @block.scalar
        def _(act):
            a = nc.scalar

            def k_copy(L, m):
                act.wait_ge(k_done, KC * L + m + 1)
                bank = g_bank[m % 2][:, 0:B * KEYS]
                if L == 0:
                    a.activation(kT[L][:, m // 2, m % 2, :], bank, ACT.Copy).then_inc(k_evac, 1)
                else:
                    a.activation(kT[L][:, m // 2, m % 2, :], bank, ACT.Identity, bias=bk_sb[:, m:m + 1]).then_inc(k_evac, 1)

            def k_high(L, b, heads=range(HPC)):
                act.wait_ge(k_evac, KC * (L + 1))
                if L == 0:
                    act.wait_ge(consts_ready, 2)
                else:
                    act.wait_ge(rows_done, UNITS * NSUP_B * (b + 1))
                for g in heads:
                    rows = slice(HD * g, HD * (g + 1))
                    a.activation(kd_hi[rows, b, :, cols128(g)].rearrange("p (a c) n -> p a c n", c=2),
                                 kT[L][rows, :, :, b * KEYS:(b + 1) * KEYS],
                                 ACT.Copy).then_inc(kd_hi_done, 1)

            act.wait_ge(ld_w["small"], 16 * len(SMALL))
            for m in range(KC):
                k_copy(0, m)
            act.wait_ge(ld_w["wq0"], 16)
            a.activation(wq_hi[:, :, :], w_stage[:, :, :], ACT.Copy, scale=SCALE).then_inc(wq_hi_done, 1)

            act.wait_ge(bias_scaled, 1)

            def body(L, i, front, middle, tail, batch):
                n, nf, nb = NSUP * L + i, NSUP * L + i + 1, NSUP * L + i - 1
                FL, TL = layers(L, i)

                def exps(u):
                    act.wait_ge(max_done, UNITS * n + u + 1)
                    wait(act, pT_done, UNITS * n + u + 1 - ROWS_BUF)
                    for g in range(HPC):
                        e = a.activation(prow[:, u % ROWS_BUF, cols128(g)], row_bank[u % 2][:, cols128(g)], ACT.Exp,
                                         bias=neg_max[:, u % ROWS_BUF, g:g + 1],
                                         accum_out=sums[:, u % ROWS_BUF, g:g + 1])
                    e.then_inc(exp_done, 1)

                def probs_copy(u):
                    m, j = divmod(u, NSUB)
                    act.wait_ge(pT_done, UNITS * n + u + 1)
                    if j == 0:
                        wait(act, pv_done, KC * n + m - 1)
                    a.activation(probs[:, HPC * (m % 2):HPC * (m % 2 + 1), cols128(j)],
                                 pT_bank[u % 2][:, :].rearrange("p (g t) -> p g t", g=HPC),
                                 ACT.Copy).then_inc(pT_evac, 1)

                def x_high(j):
                    act.wait_ge(xT_done, NSUB * nf + j + 1)
                    wait(act, q_done, KC * nf)
                    a.activation(xT_hi[:, :, cols128(j)], x_bank[j % 2][:, :].rearrange("p (k t) -> p k t", k=KC),
                                 ACT.Copy).then_inc(xT_hi_done, 1)

                def q_high(m):
                    act.wait_ge(q_done, KC * nf + m + 1)
                    if FL == 0:
                        a.activation(qT_hi[:, m, :], g_bank[m % 2][:, :], ACT.Copy).then_inc(q_hi_done, 1)
                    else:
                        a.activation(qT_hi[:, m, :], g_bank[m % 2][:, :], ACT.Identity,
                                     bias=bq_sb[:, m:m + 1]).then_inc(q_hi_done, 1)

                def c_high(m):
                    act.wait_ge(pv_done, KC * n + m + 1)
                    wait(act, o_done, NSUB * n)
                    a.activation(cT_hi[:, m, :], ctx_bank[:, :], ACT.Copy).then_inc(c_hi_done, 1)

                def integers(j):
                    act.wait_ge(f_round, NSUB * nb + j + 1)
                    a.activation(zb[:, :], xn[:, j, :], ACT.Identity, bias=minus_magic[:, 0:1]).then_inc(f_z, 1)

                def integers_copy(j):
                    act.wait_ge(f_zT, NSUB * nb + j + 1)
                    a.activation(zT[:, :, :], tail_bank[:, 0:D // 2].bitcast(bf16).rearrange("p (k t) -> p k t", k=KC),
                                 ACT.Copy).then_inc(f_zT_evac, 1)

                def route_copy(j):
                    act.wait_ge(r_T, NSUB * (i - 1) + j + 1)
                    a.activation(xrT[:, :, :], tail_bank[:, :].rearrange("p (k t) -> p k t", k=KC),
                                 ACT.Copy).then_inc(r_T_evac, 1)

                def logits_bias(j):
                    act.wait_ge(r_log, NSUB * (i - 1) + j + 1)
                    a.activation(logT[:, cols128(j)], tail_bank[0:E, 0:P], ACT.Identity,
                                 bias=bsw_sb[:, 0:1]).then_inc(r_log_evac, 1)

                for u in range(UNITS + 1):
                    if L == 0 and at(i, 0) and u in (1, 2):
                        k_copy(1, 2 * u - 2)
                        k_copy(1, 2 * u - 1)
                    for j in range(NSUB):
                        if front and u == XT_AT[j] + 1:
                            x_high(j)
                    for m in range(KC - 1):
                        if front and u == Q_AT[m] + 1:
                            q_high(m)
                    for j in range(NSUB):
                        if tail and u == tail_at(TL, j) + 1:
                            (integers_copy, route_copy)[TL](j)
                    for m in range(KC - 1):
                        if middle and u == PV_AT[m] + 1:
                            c_high(m)
                    if middle and u >= LAG:
                        probs_copy(u - LAG)
                    for j in range(NSUB):
                        if tail and TL == 1 and u == tail_at(1, j) + 1:
                            logits_bias(j)
                    if middle and u < UNITS:
                        exps(u)
                    for j in range(NSUB):
                        if tail and TL == 0 and u == tail_at(0, j) - 1:
                            integers(j)
                    if tail and TL == 1 and u == 14:
                        act.wait_ge(r_negtop, i)
                        a.activation(expl[:, :, :], expl[:, :, :], ACT.Exp).then_inc(r_exp, 1)
                    if at(i, -1) and u == XT_AT[3] + 1:
                        k_high(0, 0)
                    if L == 0 and at(i, 0) and u == 3:
                        k_high(0, 1)
                    if L == 0 and at(i, 0) and u == 1:
                        act.wait_ge(ld_w["wo0"], 16)
                        a.activation(wo_hi[:, :, :], w_stage[:, :, :], ACT.Copy).then_inc(wo_hi_done, 1)
                    if L == 0 and at(i, NSUP - 1) and u == 0:
                        act.wait_ge(ld_w["wq1"], 16)
                        act.wait_ge(q_done, KC * NSUP)
                        a.activation(wq_hi[:, :, :], w_stage[:, :, :], ACT.Copy, scale=SCALE).then_inc(wq_hi_done, 1)
                    if L == 0 and at(i, NSUP - 1) and 9 <= u < 9 + HPC:
                        k_high(1, 0, (u - 9,))
                    if L == 1 and at(i, 0) and 9 <= u < 9 + HPC:
                        k_high(1, 1, (u - 9,))
                    if L == 1 and at(i, 0) and u == 6:
                        act.wait_ge(ld_w["wo1"], 16)
                        act.wait_ge(o_done, NSUB * NSUP)
                        a.activation(wo_hi[:, :, :], w_stage[:, :, :], ACT.Copy).then_inc(wo_hi_done, 1)
                if tail and TL == 0:
                    integers_copy(NSUB - 1)
                if middle:
                    probs_copy(UNITS - 2)
                if front:
                    q_high(KC - 1)
                if middle:
                    probs_copy(UNITS - 1)
                    c_high(KC - 1)
            bodies(act, 0, body)
            bodies(act, 1, body)

            def w1_high(e, u):
                act.wait_ge(w_load[0][u], 16 * (e + 1))
                wait(act, e_h, RT * (NU * e + u - 1))
                a.activation(w1_hi[:, u % 2, :, :], w1_raw[:, u, :, :], ACT.Copy).then_inc(w_hi_done[0], 1)

            def w2_high(e, u):
                act.wait_ge(w_load[1][u], 16 * (e + 1))
                wait(act, e_y, NU * e + u - 1)
                a.activation(w2_hi[:, u % 2, :, :], w2_raw[:, u, :, :], ACT.Copy).then_inc(w_hi_done[1], 1)

            def hidden_copy(e, u):
                act.wait_ge(e_h, RT * (NU * e + u) + 1)
                a.activation(hrow[:, 0, :], hb_bank[0][:, :], ACT.Copy).then_inc(e_hcopy[0], 1)

            def hidden(e, u):
                c = NU * e + u
                act.wait_ge(e_hT, c + 1)
                wait(act, e_hlo, c - 1)
                for f in range(UC):
                    a.activation(hid[:, u % 2, f, :], hT_bank[f // 2][:, CAP * (f % 2):CAP * (f % 2 + 1)], ACT.Relu,
                                 bias=b1_sb[:, bass.ds(c * UC + f, 1)]).then_inc(e_relu, 1)
                act.wait_ge(e_relu, UC * (c + 1))
                wait(act, e_y, c - 1)
                a.activation(h_hi[:, u % 2, :, :], hid[:, u % 2, :, :], ACT.Copy).then_inc(e_hhi, 1)

            def rows_high(e):
                wait(act, e_h, RT * NU * e)
                for r in range(RT):
                    act.wait_ge(e_T, RT * e + r + 1)
                    a.activation(tT_hi[:, :, cols128(r)], tt_bank[r][:, :].rearrange("p (k t) -> p k t", k=KC),
                                 ACT.Copy).then_inc(e_T_hi, 1)

            act.wait_ge(rows_done, UNITS * 2 * NSUP)
            w2_high(0, 0)
            act.wait_ge(plain_store, PLAIN_ALL)
            act.wait_ge(slot_store, 16 * NT)
            w1_high(0, 0)
            rows_high(0)
            hidden_copy(0, 0)
            w1_high(0, 1)
            hidden(0, 0)
            w2_high(0, 1)

            def expert(e, more):
                for u in range(NU):
                    one, two = ahead(e, u, 1, more), ahead(e, u, 2, more)
                    if one:
                        hidden_copy(*one)
                    if more and u == NU - 2:
                        rows_high(e + 1)
                    if two:
                        w1_high(*two)
                    if one:
                        hidden(*one)
                    if two:
                        w2_high(*two)
            expert(0, True)
            with act.Fori(1, E - 1) as e:
                expert(e, True)
            expert(E - 1, False)

        @block.vector
        def _(dve):
            v = nc.vector
            steps = [0]

            def step(ins):
                steps[0] += 1
                ins.then_inc(dve_step, 1)
                dve.wait_ge(dve_step, steps[0])

            def v_copy(L, b):
                dve.wait_ge(v_done, B * L + b + 1)
                if L == 0:
                    v.tensor_copy(v_sb[:, L, b, :], row_bank[b][:, :]).then_inc(v_evac, 1)
                else:
                    v.tensor_tensor(v_sb[:, L, b, :], g_bank[b][:, :], bv_sb[:, :], ALU.add).then_inc(v_evac, 1)

            def k_low(L, b, heads=range(HPC)):
                for g in heads:
                    rows = slice(HD * g, HD * (g + 1))
                    dve.wait_ge(kd_hi_done, HPC * (B * L + b) + g + 1)
                    v.tensor_tensor(kd_lo[rows, b, :, cols128(g)].rearrange("p (a c) n -> p a c n", c=2),
                                    kT[L][rows, :, :, b * KEYS:(b + 1) * KEYS],
                                    kd_hi[rows, b, :, cols128(g)].bitcast(fp32).rearrange("p (a c) n -> p a c n", c=2),
                                    ALU.subtract).then_inc(kd_done, 1)

            v.memset(kd_lo[:, :, :, :].bitcast(fp32), 0.0).then_inc(dve_step, 1)
            steps[0] += 1
            dve.wait_ge(consts_ready, 3)
            v.tensor_copy(identb[:, :], ident[:, :]).then_inc(dve_consts, 1)
            dve.wait_ge(ld_w["small"], 16 * len(SMALL))
            v.tensor_scalar(bq_sb[:, :], bq_sb[:, :], SCALE, 0.0, ALU.mult, ALU.add).then_inc(bias_scaled, 1)

            def times_last():
                step(v.tensor_copy(seg_cf[:, :], seg_col[:, :]))
                step(v.tensor_scalar(times[:, :], seg_cf[:, :], float(KEYS - 2), 1.0, ALU.subtract, ALU.max))
                step(v.tensor_scalar(times[:, :], times[:, :], float(LOOKBACK + 1), 0.0, ALU.min, ALU.add))
                step(v.tensor_scalar(more[:, :], times[:, :], -1.0, 0.0, ALU.add, ALU.add))

            def rhs_maxima():
                dve.wait_ge(ld_w["rhs"], 16)
                v.tensor_reduce(xn[:, 0, :], w_stage[:, :, :].rearrange("p k n -> p n k"), AX.X, ALU.max,
                                apply_absolute_value=True).then_inc(rhs_amax, 1)

            def rhs_scale():
                dve.wait_ge(rhs_all, 1)
                step(v.tensor_scalar(rscale[:, :], rscale[:, :], 1e-12, float(np.float32(1) / np.float32(127)),
                                     ALU.max, ALU.mult))
                step(v.reciprocal(xn[:, 1, :], rscale[:, :]))

            def rhs_quantise(k):
                step(v.tensor_tensor(xn[:, 0, :], w_stage[:, k, :], xn[:, 1, :], ALU.mult))
                step(v.tensor_scalar(xn[:, 0, :], xn[:, 0, :], 127.0, -127.0, ALU.min, ALU.max))
                step(v.tensor_scalar(rq[:, k, :], xn[:, 0, :], MAGIC, MAGIC, ALU.add, ALU.subtract))

            def moments_means(n_rows, mom, mv, s1, s2, n):
                for j in range(n_rows):
                    wait_apart(dve, s1, n_rows * n + j + 1)
                    v.bn_aggr(mv[:, j, :], mom[:, j, :]).then_inc(s2, 1)

            def body(L, i, front, middle, tail, batch):
                n, nf, nb = NSUP * L + i, NSUP * L + i + 1, NSUP * L + i - 1
                FL, TL = layers(L, i)

                def row_max(u):
                    dve.wait_ge(rows_done, UNITS * n + u + 1)
                    v.tensor_reduce(neg_max[:, u % ROWS_BUF, :],
                                    row_bank[u % 2][:, :].rearrange("p (g k) -> p g k", g=HPC), AX.X, ALU.max,
                                    negate=True).then_inc(max_done, 1)

                def row_sums(u):
                    b = u % ROWS_BUF
                    dve.wait_ge(exp_done, UNITS * n + u + 1)
                    if L == 0:
                        at_last = prow[:, b, :].rearrange("p (g k) -> p g k", g=HPC)[:, :, KEYS - 1]
                        tile = bass.ds(i * NSUB + u % NSUB, 1)
                        v.scalar_tensor_tensor(totals[:, b, :], at_last, more[:, tile], sums[:, b, :],
                                               ALU.mult, ALU.add).then_inc(total_done, 1)
                        v.tensor_scalar(at_last, at_last, times[:, tile], 0.0, ALU.mult, ALU.add)
                        dve.wait_ge(total_done, UNITS * i + u + 1)
                        v.reciprocal(inv[:, b, :], totals[:, b, :]).then_inc(inv_done, 1)
                    else:
                        v.reciprocal(inv[:, b, :], sums[:, b, :]).then_inc(inv_done, 1)

                def normalise(j):
                    if j == 0:
                        dve.wait_ge(rstd_done, nf + 1)
                    v.tensor_scalar(xa[:, j, :], xa[:, j, :], mean_var[:, j, 0:1], rstd[:, j:j + 1],
                                    ALU.subtract, ALU.mult).then_inc(xn_done, 1)

                def x_low(j):
                    dve.wait_ge(xT_hi_done, NSUB * nf + j + 1)
                    v.tensor_tensor(xT_lo[:, :, cols128(j)], x_bank[j % 2][:, :].rearrange("p (k t) -> p k t", k=KC),
                                    xT_hi[:, :, cols128(j)].bitcast(fp32), ALU.subtract).then_inc(xT_lo_done, 1)

                def c_low(m):
                    dve.wait_ge(c_hi_done, KC * n + m + 1)
                    v.tensor_tensor(cT_lo[:, m, :], ctx_bank[:, :], cT_hi[:, m, :].bitcast(fp32),
                                    ALU.subtract).then_inc(c_lo_done, 1)

                def tail_norm(j):
                    if j == 0:
                        dve.wait_ge(t_rstd_done, nb + 1)
                        if TL == 1:
                            dve.wait_ge(plain_store, PLAIN_FIRST + 16 * NSUB * (i - 1))
                    v.tensor_scalar(xn[:, j, :], xs[:, j, 0:D], t_mean_var[:, j, 0:1], t_rstd[:, j:j + 1],
                                    ALU.subtract, ALU.mult).then_inc(txn_done, 1)

                def token_scale(j):
                    c = 4 * (NSUB * nb + j)
                    dve.wait_ge(txn_done, NSUB * nb + j + 1)
                    v.tensor_reduce(amax[:, j:j + 1], xn[:, j, :], AX.X, ALU.max,
                                    apply_absolute_value=True).then_inc(f_step, 1)
                    dve.wait_ge(f_step, c + 1)
                    v.tensor_scalar(lscale[:, j:j + 1], amax[:, j:j + 1], 1e-12,
                                    float(np.float32(1) / np.float32(127)), ALU.max, ALU.mult).then_inc(f_step, 1)
                    dve.wait_ge(f_step, c + 2)
                    v.reciprocal(linv[:, j:j + 1], lscale[:, j:j + 1]).then_inc(f_step, 1)

                def quantise(j):
                    c = 4 * (NSUB * nb + j)
                    dve.wait_ge(f_step, c + 3)
                    v.tensor_scalar(xn[:, j, :], xn[:, j, :], linv[:, j:j + 1], -127.0,
                                    ALU.mult, ALU.max).then_inc(f_step, 1)
                    dve.wait_ge(f_step, c + 4)
                    v.tensor_scalar(xn[:, j, :], xn[:, j, :], 127.0, MAGIC, ALU.min, ALU.add).then_inc(f_round, 1)

                def dequantise(j):
                    dve.wait_ge(f_acc, NSUB * nb + j + 1)
                    v.scalar_tensor_tensor(xn[:, j, :], tail_bank[:, :], lscale[:, j:j + 1], rscale[:, :],
                                           ALU.mult, ALU.mult).then_inc(f_deq, 1)

                count = [0]

                def link(ins):
                    count[0] += 1
                    ins.then_inc(r_step, 1)
                    dve.wait_ge(r_step, ROUTE_STEPS * (i - 1) + count[0])

                def mark(ins):
                    count[0] += 1
                    ins.then_inc(r_step, 1)

                def choose():
                    dve.wait_ge(r_lt, i)
                    v.tensor_copy(logits[:, :, :], tail_bank[:, 0:NSUB * E].rearrange("p (j e) -> p j e", e=E))\
                        .then_inc(r_lt_evac, 1)
                    wait_apart(dve, r_lt_evac, i)
                    for j in range(NSUB):
                        mark(v.max(top8[:, j, :], logits[:, j, :]))
                    dve.wait_ge(r_step, ROUTE_STEPS * (i - 1) + count[0])
                    v.tensor_tensor(expl[:, :, :], logits[:, :, :],
                                    top8[:, :, 0:1].to_broadcast([P, NSUB, E]), ALU.subtract).then_inc(r_negtop, 1)
                    for j in range(NSUB):
                        mark(v.max_index(top_at[:, j, :], top8[:, j, :], logits[:, j, :]))
                    dve.wait_ge(r_step, ROUTE_STEPS * (i - 1) + count[0])
                    link(v.tensor_copy(route[:, :], top_at[:, :, 0]))
                    v.tensor_tensor(onehot[:, :, :], lane8[:, :].unsqueeze(1).to_broadcast([P, NSUB, E]),
                                    route[:, :].unsqueeze(2).to_broadcast([P, NSUB, E]), ALU.is_equal)\
                        .then_inc(r_hot, 1)

                def place_tokens():
                    dve.wait_ge(r_exp, i)
                    link(v.tensor_reduce(psum_e[:, :], expl[:, :, :], AX.X, ALU.add))
                    link(v.reciprocal(pmax[:, :], psum_e[:, :]))
                    link(v.reciprocal(psum_e[:, :], pmax[:, :]))
                    link(v.tensor_tensor(scale_t[:, :], pmax[:, :], psum_e[:, :], ALU.mult))
                    dve.wait_ge(r_cum, i)
                    link(v.tensor_tensor(place[:, :, :], counts[:, 0:NSUB * E].rearrange("p (j e) -> p j e", e=E),
                                         carry[:, :].unsqueeze(1).to_broadcast([P, NSUB, E]), ALU.add))
                    link(v.tensor_tensor(carry[:, :], counts[:, NSUB * E:(NSUB + 1) * E], carry[:, :], ALU.add))
                    dve.sem_inc(tail_free, 1)
                    link(v.tensor_tensor(place[:, :, :], place[:, :, :], onehot[:, :, :], ALU.mult))
                    link(v.tensor_reduce(pos[:, :], place[:, :, :], AX.X, ALU.add))
                    mark(v.tensor_scalar(full[:, :], pos[:, :], CAP + 0.5, float(NOWHERE), ALU.is_gt, ALU.mult))
                    link(v.scalar_tensor_tensor(slot_f[:, :], route[:, :], float(CAP), pos[:, :], ALU.mult, ALU.add))
                    link(v.tensor_tensor(slot_f[:, :], slot_f[:, :], full[:, :], ALU.add))
                    mark(v.tensor_copy(xs[:, :, D + 1], scale_t[:, :]))
                    mark(v.tensor_copy(xs[:, :, D].bitcast(i32), token_num[:, bass.ds((i - 1) * NSUB, NSUB)]))
                    v.tensor_scalar(slot[:, :], slot_f[:, :], -1.0, 0.0, ALU.add, ALU.add).then_inc(r_slot, 1)
                    assert count[0] == ROUTE_STEPS

                def plain(j):
                    v.scalar_tensor_tensor(xn[:, j, :], xn[:, j, :], scale_t[:, j:j + 1], xs[:, j, 0:D],
                                           ALU.mult, ALU.add).then_inc(r_plain, 1)

                def window_ends():
                    dve.wait_ge(seg_load, 16 * (i + 2))
                    v.tensor_scalar(seg_f[:, :], seg_row[:, :], 0.0, float(KEYS - 1 + LOOKBACK),
                                    ALU.max, ALU.min).then_inc(hide_step, 1)
                    dve.wait_ge(hide_step, 2 * (i + 1) + 1)
                    v.tensor_scalar(seg_f[:, :], seg_f[:, :], key_num[:, 0:1], LOOKBACK / 2,
                                    ALU.subtract, ALU.subtract).then_inc(hide_step, 1)

                def distances():
                    dve.wait_ge(hide_step, 2 * (i + 2))
                    v.tensor_tensor(seg_f[:, :], seg_f[:, :], seg_f[:, :], ALU.mult).then_inc(hide_wide, 1)

                def hide():
                    dve.wait_ge(hide_wide, i + 2)
                    wait(dve, rows_done, UNITS * (i + 1))
                    v.tensor_scalar(hideT[:, :], seg_f[:, :], (LOOKBACK / 2 + 0.1) ** 2, HIDE,
                                    ALU.is_gt, ALU.mult).then_inc(hide_done, 1)

                def q_low(m):
                    dve.wait_ge(q_hi_done, KC * nf + m + 1)
                    if FL == 0:
                        v.tensor_tensor(qT_lo[:, m, :], g_bank[m % 2][:, :], qT_hi[:, m, :].bitcast(fp32),
                                        ALU.subtract).then_inc(q_lo_done, 1)
                    else:
                        v.scalar_tensor_tensor(qT_lo[:, m, :], g_bank[m % 2][:, :], bq_sb[:, m:m + 1],
                                               qT_hi[:, m, :].bitcast(fp32), ALU.add, ALU.subtract)\
                            .then_inc(q_lo_done, 1)

                def residual(j):
                    dve.wait_ge(o_done, NSUB * nb + j + 1)
                    if TL == 0:
                        dve.wait_ge(xb_load[j], 16 * (nb + 1))
                        dve.wait_ge(x2_store[j], X2_FIRST + 16 * nb)
                    else:
                        dve.wait_ge(xb_biased, NSUB * (i - 1) + j + 1)
                        dve.wait_ge(xs_free, i)
                    v.tensor_tensor(xs[:, j, 0:D], g_bank[j % 2][:, :], xb[:, j, :], ALU.add).then_inc(res_done, 1)

                for u in range(UNITS + 1):
                    if middle and u < UNITS:
                        row_max(u)
                    if front and FL == 0 and u == UNITS - 1:
                        hide()
                    if middle and u:
                        row_sums(u - 1)
                    if L == 0 and at(i, 0) and u in (3, 4):
                        dve.wait_ge(ld_w["bv"], 16)
                        v_copy(1, u - 3)
                    for j in range(NSUB):
                        if front and u == XT_AT[j] + 1:
                            x_low(j)
                    for j in range(NSUB):
                        if front and u == (2, 2, 3, 4)[j]:
                            normalise(j)
                    if tail and 1 <= u <= NSUB:
                        residual(u - 1)
                    if front and u == 0:
                        for j in range(NSUB):
                            dve.wait_ge(xa_load[j], 16 * (nf + 1))
                            v.bn_stats(moments[:, j, :], xa[:, j, :]).then_inc(stats, 1)
                        moments_means(NSUB, moments, mean_var, stats, aggr, nf)
                    if tail and 2 <= u < 2 + NSUB:
                        j = u - 2
                        dve.wait_ge(res_done, NSUB * nb + j + 1)
                        v.bn_stats(t_moments[:, j, :], xs[:, j, 0:D]).then_inc(t_stats, 1)
                    if tail and u == 1 + NSUB:
                        moments_means(NSUB, t_moments, t_mean_var, t_stats, t_aggr, nb)
                    if front and FL == 0 and u == 1:
                        window_ends()
                    if front and FL == 0 and u == 6:
                        distances()
                    for m in range(KC):
                        if middle and m < KC - 1 and u == PV_AT[m] + 1:
                            c_low(m)
                        if front and m < KC - 1 and u == Q_AT[m] + 1:
                            q_low(m)
                    for j in range(NSUB):
                        if tail and TL == 0 and u == tail_at(0, j) + 1:
                            dequantise(j)
                        if tail and u == NORM_AT + TAIL_STEP[TL] * j:
                            tail_norm(j)
                            if TL == 0:
                                token_scale(j)
                        if tail and TL == 0 and u == NORM_AT + 1 + TAIL_STEP[0] * j:
                            quantise(j)
                    if tail and TL == 1 and u == 14:
                        choose()
                    if tail and TL == 1 and u == 16:
                        place_tokens()
                    if at(i, -1) and u == 5:
                        dve.wait_ge(wq_hi_done, 1)
                        v.scalar_tensor_tensor(wq_lo[:, :, :], w_stage[:, :, :], SCALE, wq_hi[:, :, :].bitcast(fp32),
                                               ALU.mult, ALU.subtract).then_inc(wq_done, 1)
                    if at(i, -1) and u == 7:
                        v_copy(0, 0)
                        v_copy(0, 1)
                        dve.wait_ge(dve_step, steps[0])
                        k_low(0, 0)
                        times_last()
                    if L == 0 and at(i, 0) and u == 4:
                        k_low(0, 1)
                    if L == 0 and at(i, 0):
                        if u == 2:
                            dve.wait_ge(wo_hi_done, 1)
                            v.tensor_tensor(wo_lo[:, :, :], w_stage[:, :, :], wo_hi[:, :, :].bitcast(fp32),
                                            ALU.subtract).then_inc(wo_done, 1)
                        elif u == 7:
                            rhs_maxima()
                        elif u == 12:
                            rhs_scale()
                        elif u > UNITS - KC:
                            rhs_quantise(u - UNITS + KC - 1)
                            if u == UNITS:
                                dve.sem_inc(rhs_done, 1)
                    if L == 0 and at(i, NSUP - 1) and u == 0:
                        dve.wait_ge(wq_hi_done, 2)
                        v.scalar_tensor_tensor(wq_lo[:, :, :], w_stage[:, :, :], SCALE, wq_hi[:, :, :].bitcast(fp32),
                                               ALU.mult, ALU.subtract).then_inc(wq_done, 1)
                    if L == 0 and at(i, NSUP - 1) and 10 <= u < 10 + HPC:
                        k_low(1, 0, (u - 10,))
                    if L == 1 and at(i, 0) and 10 <= u < 10 + HPC:
                        k_low(1, 1, (u - 10,))
                    if L == 1 and at(i, 0) and u == 7:
                        dve.wait_ge(wo_hi_done, 2)
                        v.tensor_tensor(wo_lo[:, :, :], w_stage[:, :, :], wo_hi[:, :, :].bitcast(fp32),
                                        ALU.subtract).then_inc(wo_done, 1)
                if tail and TL == 1:
                    plain(0)
                    plain(1)
                if front:
                    q_low(KC - 1)
                if tail and TL == 1:
                    plain(2)
                if tail and TL == 0:
                    dequantise(NSUB - 1)
                if tail and TL == 1:
                    plain(3)
                if middle:
                    c_low(KC - 1)
                if L == 0 and at(i, 0):
                    for j in range(NSUB):
                        dve.wait_ge(x2_store[j], X2_FIRST)
                if L == 1 and at(i, 0):
                    dve.wait_ge(f_deq, NT)
                    dve.sem_inc(tail_free, 1)
                    dve.sem_inc(plain_store, PLAIN_FIRST)

            bodies(dve, 0, body)
            bodies(dve, 1, body)

            def w1_low(e, u):
                dve.wait_ge(w_hi_done[0], NU * e + u + 1)
                v.tensor_tensor(w1_lo[:, u % 2, :, :], w1_raw[:, u, :, :], w1_hi[:, u % 2, :, :].bitcast(fp32),
                                ALU.subtract).then_inc(w_lo_done[0], 1)

            def w2_low(e, u):
                dve.wait_ge(w_hi_done[1], NU * e + u + 1)
                v.tensor_tensor(w2_lo[:, u % 2, :, :], w2_raw[:, u, :, :], w2_hi[:, u % 2, :, :].bitcast(fp32),
                                ALU.subtract).then_inc(w_lo_done[1], 1)

            def hidden_copy(e, u):
                dve.wait_ge(e_h, RT * (NU * e + u) + 2)
                v.tensor_copy(hrow[:, 1, :], hb_bank[1][:, :]).then_inc(e_hcopy[1], 1)

            def rows_low(e):
                for r in range(RT):
                    dve.wait_ge(e_T_hi, RT * e + r + 1)
                    v.tensor_tensor(tT_lo[:, :, cols128(r)], tt_bank[r][:, :].rearrange("p (k t) -> p k t", k=KC),
                                    tT_hi[:, :, cols128(r)].bitcast(fp32), ALU.subtract).then_inc(e_T_lo, 1)

            def rows_norm(e):
                dve.wait_ge(tokn_load, 16 * RT * (e + 1))
                for r in range(RT):
                    v.bn_stats(e_moments[:, r, :], tokn[:, r, :]).then_inc(e_stats, 1)
                moments_means(RT, e_moments, e_mean_var, e_stats, e_aggr, e)
                dve.wait_ge(e_rstd_done, e + 1)
                for r in range(RT):
                    v.tensor_scalar(tokn[:, r, :], tokn[:, r, :], e_mean_var[:, r, 0:1], e_rstd[:, r:r + 1],
                                    ALU.subtract, ALU.mult).then_inc(e_xn, 1)

            def hidden_low(e, u):
                c = NU * e + u
                dve.wait_ge(e_hhi, c + 1)
                wait(dve, e_y, c - 1)
                v.tensor_tensor(h_lo[:, u % 2, :, :], hid[:, u % 2, :, :], h_hi[:, u % 2, :, :].bitcast(fp32),
                                ALU.subtract).then_inc(e_hlo, 1)

            def results(e):
                dve.wait_ge(e_y, NU * (e + 1))
                dve.wait_ge(b2_load, 16 * (e + 1))
                dve.wait_ge(tok_load, 16 * RT * (e + 1))
                wait(dve, y_store, 16 * RT * e)
                for r in range(RT):
                    v.tensor_tensor(y_sb[:, r, :], y_bank[r][:, :], b2_sb[:, :], ALU.add).then_inc(e_yb, 1)
                v.tensor_copy(tok_id[:, :], tok[:, :, D].bitcast(i32)).then_inc(e_id, 1)
                for r in range(RT):
                    dve.wait_ge(e_yb, RT * e + r + 1)
                    v.scalar_tensor_tensor(y_sb[:, r, :], y_sb[:, r, :], tok[:, r, D + 1:D + 2], tok[:, r, 0:D],
                                           ALU.mult, ALU.add).then_inc(e_yout, 1)

            w2_low(0, 0)
            dve.wait_ge(plain_store, PLAIN_ALL)
            dve.wait_ge(slot_store, 16 * NT)
            rows_norm(0)
            w1_low(0, 0)
            rows_low(0)
            hidden_copy(0, 0)
            w1_low(0, 1)
            hidden_low(0, 0)
            w2_low(0, 1)

            def expert(e, more):
                for u in range(NU):
                    one, two = ahead(e, u, 1, more), ahead(e, u, 2, more)
                    if one:
                        hidden_copy(*one)
                    if more and u == NU - 2:
                        rows_low(e + 1)
                    if two:
                        w1_low(*two)
                    if more and u == NU - 3:
                        rows_norm(e + 1)
                    if u == NU - 1:
                        results(e)
                    if one:
                        hidden_low(*one)
                    if two:
                        w2_low(*two)
            expert(0, True)
            with dve.Fori(1, E - 1) as e:
                expert(e, True)
            expert(E - 1, False)

        @block.tensor
        def _(pe):
            t = nc.tensor

            def project_k(L, m):
                if m == 0:
                    pe.wait_ge(ld_w[f"wk{L}"], 16)
                if L == 1 and m < 2:
                    pe.wait_ge(q_lo_done, 3 + m)
                else:
                    wait(pe, k_evac, KC * L + m - 1)
                for k in range(KC):
                    mm = t.matmul(g_bank[m % 2][:, 0:B * KEYS], wk_stage[L][:, k, cols128(m)], ctxT_sb[:, k, :],
                                  start=(k == 0), stop=(k == KC - 1))
                mm.then_inc(k_done, 1)

            def project_v(L, b):
                if b == 0:
                    pe.wait_ge(ld_w[f"wv{L}"], 16)
                if L == 1:
                    pe.wait_ge(k_evac, KC + 3 + b)
                bank = (row_bank, g_bank)[L][b]
                for k in range(KC):
                    mm = t.matmul(bank[:, :], ctxT_sb[:, k, b * KEYS:(b + 1) * KEYS], wv_stage[L][:, k, :],
                                  start=(k == 0), stop=(k == KC - 1))
                mm.then_inc(v_done, 1)

            pe.wait_ge(ld_w["ctx"], 16)
            for m in range(KC):
                project_k(0, m)
            pe.wait_ge(consts_ready, 3)
            pe.wait_ge(dve_consts, 1)
            pe.wait_ge(k_evac, KC)

            def body(L, i, front, middle, tail, batch):
                n, nf, nb = NSUP * L + i, NSUP * L + i + 1, NSUP * L + i - 1
                FL, TL = layers(L, i)

                def scores(u):
                    m, j = divmod(u, NSUB)
                    bank = row_bank[u % 2][:, :]
                    if u == 0:
                        pe.wait_ge(q_lo_done, KC * (n + 1))
                        pe.wait_ge(kd_done, HPC * (B * L + batch + 1))
                        if L == 0:
                            pe.wait_ge(hide_done, i + 1)
                            pe.wait_ge(v_evac, B)
                    wait(pe, exp_done, UNITS * n + u - 1)
                    mm = mm3(bank, qT_hi[:, m, cols128(j)], qT_lo[:, m, cols128(j)],
                             kd_hi[:, batch, m, :], kd_lo[:, batch, m, :], True, L == 1)
                    if L == 0:
                        mm = t.matmul(bank.rearrange("p (g k) -> p g k", g=HPC), hideT[:, cols128(j)],
                                      identb[:, :].unsqueeze(1).to_broadcast([P, HPC, KEYS]),
                                      start=False, stop=True)
                    mm.then_inc(rows_done, 1)

                def probs_transpose(u):
                    pe.wait_ge(norm_done, UNITS * n + u + 1)
                    wait(pe, pT_evac, UNITS * n + u - 1)
                    for g in range(HPC):
                        mm = t.transpose(pT_bank[u % 2][:, cols128(g)], prow[:, u % ROWS_BUF, cols128(g)], ident[:, :])
                    mm.then_inc(pT_done, 1)

                def weighted(m):
                    pe.wait_ge(pT_evac, UNITS * n + NSUB * (m + 1))
                    wait(pe, c_lo_done, KC * n + m)
                    if m == 0 and front:
                        pe.wait_ge(xT_lo_done, NSUB * nf + 3)
                    for g in range(HPC):
                        h = HPC * m + g
                        mm = t.matmul(ctx_bank[HD * g:HD * (g + 1), :], v_sb[:, L, batch, HD * h:HD * (h + 1)],
                                      probs[:, h % (2 * HPC), :], start=True, stop=True, tile_position=(0, HD * g))
                    mm.then_inc(pv_done, 1)

                def x_transpose(j):
                    pe.wait_ge(xn_done, NSUB * nf + j + 1)
                    if j >= 2:
                        pe.wait_ge(xT_lo_done, NSUB * nf + j - 1)
                    for k in range(KC):
                        mm = t.transpose(x_bank[j % 2][:, cols128(k)], xa[:, j, cols128(k)], ident[:, :])
                    mm.then_inc(xT_done, 1)

                def project_q(m):
                    if m == 0:
                        pe.wait_ge(wq_done, FL + 1)
                        pe.wait_ge(xT_lo_done, NSUB * (nf + 1))
                    if m < 2 and tail:
                        pe.wait_ge(res_done, NSUB * nb + 3 + m)
                    elif m < 2 and middle:
                        pe.wait_ge(v_evac, B + 1 + m)
                    elif m >= 2:
                        pe.wait_ge(q_lo_done, KC * nf + m - 1)
                    for k in range(KC):
                        mm = mm3(g_bank[m % 2][:, :], wq_hi[:, k, cols128(m)], wq_lo[:, k, cols128(m)],
                                 xT_hi[:, k, :], xT_lo[:, k, :], k == 0, k == KC - 1)
                    mm.then_inc(q_done, 1)

                def project_out(j):
                    if j == 0:
                        pe.wait_ge(wo_done, TL + 1)
                        pe.wait_ge(c_lo_done, KC * nb + KC - 1)
                    if j < 2 and middle:
                        pe.wait_ge(q_lo_done, KC * n + 3 + j)
                    elif j < 2:
                        pe.wait_ge(res_done, NSUB * (nb - 1) + 3 + j)
                    else:
                        pe.wait_ge(res_done, NSUB * nb + j - 1)
                    for k in range(KC):
                        if j == 0 and k == KC - 1:
                            pe.wait_ge(c_lo_done, KC * (nb + 1))
                        mm = mm3(g_bank[j % 2][:, :], cT_hi[:, k, cols128(j)], cT_lo[:, k, cols128(j)],
                                 wo_hi[:, k, :], wo_lo[:, k, :], k == 0, k == KC - 1)
                    mm.then_inc(o_done, 1)

                def int8_transpose(j):
                    pe.wait_ge(f_z, NSUB * nb + j + 1)
                    if j:
                        pe.wait_ge(f_deq, NSUB * nb + j)
                    bank = tail_bank[:, 0:D // 2].bitcast(bf16)
                    for k in range(KC):
                        mm = t.transpose(bank[:, cols128(k)], zb[:, cols128(k)], identb[:, :])
                    mm.then_inc(f_zT, 1)

                def int8_product(j):
                    pe.wait_ge(f_zT_evac, NSUB * nb + j + 1)
                    for k in range(KC):
                        mm = t.matmul(tail_bank[:, :], zT[:, k, :], rq[:, k, :], start=(k == 0), stop=(k == KC - 1))
                    mm.then_inc(f_acc, 1)

                def route_transpose(j):
                    pe.wait_ge(txn_done, NSUB * nb + j + 1)
                    if j:
                        pe.wait_ge(r_log_evac, NSUB * (i - 1) + j)
                    else:
                        pe.wait_ge(tail_free, i)
                    for k in range(KC):
                        mm = t.transpose(tail_bank[:, cols128(k)], xn[:, j, cols128(k)], ident[:, :])
                    mm.then_inc(r_T, 1)

                def route_logits(j):
                    pe.wait_ge(r_T_evac, NSUB * (i - 1) + j + 1)
                    for k in range(KC):
                        mm = t.matmul(tail_bank[0:E, 0:P], wsw_sb[:, k, :], xrT[:, k, :],
                                      start=(k == 0), stop=(k == KC - 1))
                    mm.then_inc(r_log, 1)

                def logits_transpose():
                    wait_apart(pe, r_log_evac, NSUB * i)
                    for j in range(NSUB):
                        mm = t.transpose(tail_bank[:, E * j:E * (j + 1)], logT[:, cols128(j)], ident[0:E, 0:E])
                    mm.then_inc(r_lt, 1)

                def route_counts():
                    pe.wait_ge(r_hot, i)
                    for j in range(NSUB + 1):
                        for k in range(min(j, NSUB - 1) + 1):
                            full_tile = k < j
                            mm = t.matmul(counts[:, E * j:E * (j + 1)], (onesb if full_tile else upto)[:, :],
                                          onehot[:, k, :], start=(k == 0), stop=(k == min(j, NSUB - 1)))
                    mm.then_inc(r_cum, 1)

                for u in range(UNITS):
                    if middle:
                        scores(u)
                    if middle and u >= LAG:
                        probs_transpose(u - LAG)
                    for j in range(NSUB):
                        if tail and TL == 1 and u == tail_at(1, j) + 1:
                            route_logits(j)
                    if tail and u < NSUB:
                        project_out(u)
                    if at(i, -1) and u in (XT_AT[1], XT_AT[3]):
                        project_v(0, XT_AT.index(u) // 2)
                    if L == 0 and at(i, 0) and u < 2:
                        project_k(1, 2 * u)
                        project_k(1, 2 * u + 1)
                    elif L == 0 and at(i, 0) and u < 2 + B:
                        project_v(1, u - 2)
                    for j in range(NSUB):
                        if front and u == XT_AT[j]:
                            x_transpose(j)
                    for m in range(KC):
                        if front and u == Q_AT[m]:
                            project_q(m)
                    for j in range(NSUB):
                        if tail and u == tail_at(TL, j):
                            (int8_transpose, route_transpose)[TL](j)
                    for m in range(KC):
                        if middle and u == PV_AT[m]:
                            weighted(m)
                    for j in range(NSUB):
                        if tail and TL == 0 and u == tail_at(0, j) + 1:
                            int8_product(j)
                    if tail and TL == 1 and u == 13:
                        logits_transpose()
                    if tail and TL == 1 and u == 15:
                        route_counts()
                if middle:
                    probs_transpose(UNITS - LAG)
                if tail and TL == 0:
                    int8_transpose(NSUB - 1)
                if middle:
                    probs_transpose(UNITS - 2)
                if middle:
                    probs_transpose(UNITS - 1)
                if tail and TL == 0:
                    int8_product(NSUB - 1)
                if middle:
                    weighted(KC - 1)

            bodies(pe, 0, body)
            bodies(pe, 1, body)

            def rows_transpose(e):
                for r in range(RT):
                    pe.wait_ge(e_xn, RT * e + r + 1)
                    wait(pe, e_T_lo, RT * (e - 1) + r + 1)
                    for k in range(KC):
                        mm = t.transpose(tt_bank[r][:, cols128(k)], tokn[:, r, cols128(k)], ident[:, :])
                    mm.then_inc(e_T, 1)

            def hidden(e, u):
                c = NU * e + u
                pe.wait_ge(w_lo_done[0], c + 1)
                if u == 0:
                    pe.wait_ge(e_T_lo, RT * (e + 1))
                for r in range(RT):
                    wait(pe, e_hcopy[r], c)
                    for k in range(KC):
                        mm = mm3(hb_bank[r][:, :], tT_hi[:, k, cols128(r)], tT_lo[:, k, cols128(r)],
                                 w1_hi[:, u % 2, k, :], w1_lo[:, u % 2, k, :], k == 0, k == KC - 1)
                    mm.then_inc(e_h, 1)

            def hidden_transpose(e, u):
                c = NU * e + u
                wait(pe, e_relu, UC * c)
                for r in range(RT):
                    pe.wait_ge(e_hcopy[r], c + 1)
                    for f in range(UC):
                        at_col = CAP * (f % 2) + P * r
                        mm = t.transpose(hT_bank[f // 2][:, at_col:at_col + P], hrow[:, r, cols128(f)], ident[:, :])
                mm.then_inc(e_hT, 1)

            def second(e, u):
                c = NU * e + u
                pe.wait_ge(w_lo_done[1], c + 1)
                pe.wait_ge(e_hlo, c + 1)
                if u == 0:
                    wait(pe, e_yb, RT * e)
                for r in range(RT):
                    for f in range(UC):
                        mm = mm3(y_bank[r][:, :], h_hi[:, u % 2, f, cols128(r)], h_lo[:, u % 2, f, cols128(r)],
                                 w2_hi[:, u % 2, f, :], w2_lo[:, u % 2, f, :],
                                 u == 0 and f == 0, u == NU - 1 and f == UC - 1)
                mm.then_inc(e_y, 1)

            def expert(e, more):
                for u in range(NU):
                    one = ahead(e, u, 1, more)
                    if one:
                        hidden(*one)
                    if more and u == NU - 2:
                        rows_transpose(e + 1)
                    second(e, u)
                    if one:
                        hidden_transpose(*one)

            rows_transpose(0)
            hidden(0, 0)
            hidden_transpose(0, 0)
            expert(0, True)
            with pe.Fori(1, E - 1) as e:
                expert(e, True)
            expert(E - 1, False)


def kernel(x, ctx_1024, itok_BxS_0_511, L0_xattn_Wq, L0_xattn_Wkv, L0_xattn_Wo, L0_ffn_rhs,
           L1_xattn_in_proj_weight, L1_xattn_in_proj_bias, L1_xattn_out_w, L1_xattn_out_b,
           L1_ffn_w_switch, L1_ffn_b_switch, L1_ffn_w1, L1_ffn_b1, L1_ffn_w2, L1_ffn_b2):
    import concourse.bacc as bacc
    from concourse.bass_utils import run_bass_kernel_spmd

    def lay(a):
        return np.ascontiguousarray(np.asarray(a))

    def chunks(v):
        return lay(np.asarray(v).reshape(-1, P).T)

    bias = np.asarray(L1_xattn_in_proj_bias)
    seg = np.asarray(itok_BxS_0_511).reshape(T)
    arrays = {
        "x": lay(np.asarray(x).reshape(T, D)),
        "ctxT": lay(np.asarray(ctx_1024).reshape(B * KEYS, D).T),
        "segT": chunks(seg), "seg": lay(seg.reshape(1, T)),
        "wq0": lay(np.asarray(L0_xattn_Wq).T), "wkv0": lay(np.asarray(L0_xattn_Wkv).T),
        "wo0": lay(np.asarray(L0_xattn_Wo).T), "rhs": lay(L0_ffn_rhs),
        "wqkv1": lay(np.asarray(L1_xattn_in_proj_weight).T),
        "bq1": chunks(bias[0:D]), "bk1": chunks(bias[D:2 * D]), "bv1": lay(bias[2 * D:].reshape(1, D)),
        "wo1": lay(np.asarray(L1_xattn_out_w).T), "bo1": lay(np.asarray(L1_xattn_out_b).reshape(1, D)),
        "wsw": lay(L1_ffn_w_switch), "bsw": lay(np.asarray(L1_ffn_b_switch).reshape(E, 1)),
        "w1": lay(L1_ffn_w1), "b1": chunks(np.asarray(L1_ffn_b1).reshape(-1)),
        "w2": lay(L1_ffn_w2), "b2": lay(L1_ffn_b2),
    }
    nc = bacc.Bacc("TRN2", target_bir_lowering=False, num_devices=1)
    args = {n: nc.dram_tensor("in_" + n, a.shape, mybir.dt.from_np(a.dtype), kind="ExternalInput").ap()
            for n, a in arrays.items()}
    out = nc.dram_tensor("out", [T, D], mybir.dt.float32, kind="ExternalOutput").ap()
    build(nc, out=out, **args)
    r = run_bass_kernel_spmd(nc, [{"in_" + n: a for n, a in arrays.items()}], core_ids=[0])
    return r.results[0]["out"].reshape(B, S, D)
```
